# Optimizing a Trainium2 kernel written in Bass

```python
import numpy as np
import jax
import jax.numpy as jnp

def _softmax(x, axis=-1):
    return jax.nn.softmax(x, axis=axis)

def _gelu(x):
    return jax.nn.gelu(x, approximate=True)

def _silu(x):
    return jax.nn.silu(x)

def _sigmoid(x):
    return jax.nn.sigmoid(x)

def _layernorm(x, axis=-1, eps=1e-05):
    m = jnp.mean(x, axis=axis, keepdims=True)
    v = jnp.var(x, axis=axis, keepdims=True)
    return (x - m) / jnp.sqrt(v + eps)

def _scatter_add(tgt, idx, src, axis=0):
    return tgt.at[idx].add(src)

def _segment_sum(src, seg, n):
    return jax.ops.segment_sum(src, seg, n)
kernel_name = 'mk_seq_postln_d2_jaxref_r4_e9c903'

def setup_inputs(seed: int=0):
    np.random.seed(seed)
    _w = jnp.asarray

    def _L0_attn_setup():
        import jax, jax.numpy as jnp
        import numpy as np
        B, N, C = (2, 512, 256)
        H = 16
        HD = C // H
        KA_IN = 2 * HD
        KA_OUT = HD
        T = 4
        KA_HID = KA_IN // 2
        KA_O = KA_OUT // T
        TEMPERATURE = 0.72
        SCALE = HD ** (-0.5)
        LN_EPS = 1e-05
        key = jax.random.key(seed)
        ks = jax.random.split(key, 20)

        def w(k, shape, fan_in):
            return jax.random.normal(k, shape, jnp.float32) / np.sqrt(fan_in)
        return {'x': jax.random.normal(ks[0], (B, N, C), jnp.float32), 'Wqkv': w(ks[1], (C, 3 * C), C), 'Wproj': w(ks[2], (C, C), C), 'bproj': jnp.zeros((C,), jnp.float32), 'alpha': jnp.ones((H,), jnp.float32), 'beta': jnp.ones((H,), jnp.float32), 'gamma': jnp.ones((H,), jnp.float32), 'A': w(ks[3], (T, KA_IN, KA_IN), KA_IN), 'Wphi1': w(ks[4], (T, KA_IN, KA_HID), KA_IN), 'bphi1': jnp.zeros((T, KA_HID), jnp.float32), 'Wphi2': w(ks[5], (T, KA_HID, KA_O), KA_HID), 'bphi2': jnp.zeros((T, KA_O), jnp.float32), 'Wpsi1': w(ks[6], (T, KA_IN, KA_IN), KA_IN), 'bpsi1': jnp.zeros((T, KA_IN), jnp.float32), 'ln_g': jnp.ones((T, KA_IN), jnp.float32), 'ln_b': jnp.zeros((T, KA_IN), jnp.float32), 'Wpsi2': w(ks[7], (T, KA_IN, KA_O), KA_IN), 'bpsi2': jnp.zeros((T, KA_O), jnp.float32), 'mixing': jnp.full((T,), 1.0 / T, jnp.float32), 'temp_scale': jnp.asarray(TEMPERATURE, jnp.float32)}
    _L0_attn_in = _L0_attn_setup()

    def _L0_ffn_setup():
        import jax, jax.numpy as jnp
        import numpy as np
        B, L, D = (4, 512, 256)
        H = 16
        E = 16
        NS = 16
        S = NS // E
        F = 1024
        EPS = 1e-05

        def _layernorm(x, g, b):
            mu = jnp.mean(x, axis=-1, keepdims=True)
            var = jnp.mean(jnp.square(x - mu), axis=-1, keepdims=True)
            return (x - mu) * jax.lax.rsqrt(var + EPS) * g + b

        def _mha(q, k, v, Wq, bq, Wk, bk, Wv, bv, Wo, bo):
            Bq, Lq, Dm = q.shape
            dh = Dm // H
            qh = (q @ Wq + bq).reshape(Bq, Lq, H, dh)
            kh = (k @ Wk + bk).reshape(Bq, -1, H, dh)
            vh = (v @ Wv + bv).reshape(Bq, -1, H, dh)
            scores = jnp.einsum('bqhd,bkhd->bhqk', qh, kh) / jnp.asarray(np.sqrt(dh), q.dtype)
            attn = jax.nn.softmax(scores, axis=-1)
            out = jnp.einsum('bhqk,bkhd->bqhd', attn, vh).reshape(Bq, Lq, Dm)
            return out @ Wo + bo
        key = jax.random.key(seed)
        ks = jax.random.split(key, 32)
        s = 0.02
        d = {}
        d['x'] = jax.random.normal(ks[0], (B, L, D), jnp.float32)
        d['slot_query'] = jax.random.normal(ks[1], (1, NS, D), jnp.float32) * 0.01
        for i, nm in enumerate(['d_Wq', 'd_Wk', 'd_Wv', 'd_Wo']):
            d[nm] = jax.random.normal(ks[2 + i], (D, D), jnp.float32) * s
        for nm in ['d_bq', 'd_bk', 'd_bv', 'd_bo']:
            d[nm] = jnp.zeros((D,), jnp.float32)
        for i, nm in enumerate(['c_Wq', 'c_Wk', 'c_Wv', 'c_Wo']):
            d[nm] = jax.random.normal(ks[6 + i], (D, D), jnp.float32) * s
        for nm in ['c_bq', 'c_bk', 'c_bv', 'c_bo']:
            d[nm] = jnp.zeros((D,), jnp.float32)
        d['e_ln_g'] = jnp.ones((E, D), jnp.float32)
        d['e_ln_b'] = jnp.zeros((E, D), jnp.float32)
        d['e_W1'] = jax.random.normal(ks[10], (E, D, F), jnp.float32) * s
        d['e_b1'] = jnp.zeros((E, F), jnp.float32)
        d['e_Wg'] = jax.random.normal(ks[11], (E, D, F), jnp.float32) * s
        d['e_bg'] = jnp.zeros((E, F), jnp.float32)
        d['e_W2'] = jax.random.normal(ks[12], (E, F, D), jnp.float32) * s
        d['e_b2'] = jnp.zeros((E, D), jnp.float32)
        return d
    _L0_ffn_in = _L0_ffn_setup()

    def _L1_attn_setup():
        import math
        import jax, jax.numpy as jnp
        import numpy as np
        N_HEADS = 8
        EPS = 1e-05
        key = jax.random.key(seed)
        ks = jax.random.split(key, 5)
        B, L, D = (4, 512, 256)
        w_scale = 0.02
        return {'x': jax.random.normal(ks[0], (B, L, D), dtype=jnp.float32), 'Wq': jax.random.normal(ks[1], (D, D), dtype=jnp.float32) * w_scale, 'Wk': jax.random.normal(ks[2], (D, D), dtype=jnp.float32) * w_scale, 'Wv': jax.random.normal(ks[3], (D, D), dtype=jnp.float32) * w_scale, 'Wo': jax.random.normal(ks[4], (D, D), dtype=jnp.float32) * w_scale, 'gn_weight': jnp.ones((D,), dtype=jnp.float32), 'gn_bias': jnp.zeros((D,), dtype=jnp.float32)}
    _L1_attn_in = _L1_attn_setup()

    def _L1_ffn_setup():
        import jax, jax.numpy as jnp
        import numpy as np
        DIM = 256
        DEPTH = 2
        HEADS = 8
        DIM_HEAD = 64
        WINDOW = 128
        INNER = HEADS * DIM_HEAD
        HID = int(DIM * 4 * 2 / 3)
        B, N = (2, 2048)
        QK_SCALE = 8.0

        def shift_token(t):
            t1, t2 = jnp.split(t, 2, axis=-1)
            t2 = jnp.pad(t2, ((0, 0), (1, 0), (0, 0)))[:, :-1]
            return jnp.concatenate([t1, t2], axis=-1)

        def l2norm(t):
            return t / jnp.clip(jnp.linalg.norm(t, axis=-1, keepdims=True), 1e-12)

        def rotate_half(x):
            x1, x2 = jnp.split(x, 2, axis=-1)
            return jnp.concatenate([-x2, x1], axis=-1)

        def rotary_xpos(q, k):
            n = q.shape[-2]
            half_idx = jnp.arange(0, DIM_HEAD, 2, dtype=jnp.float32)
            inv_freq = 1.0 / 10000.0 ** (half_idx / DIM_HEAD)
            t = jnp.arange(n, dtype=jnp.float32)
            freqs = t[:, None] * inv_freq[None, :]
            freqs = jnp.concatenate([freqs, freqs], axis=-1)
            base = (half_idx + 0.4 * DIM_HEAD) / (1.4 * DIM_HEAD)
            power = (t - n // 2) / float(WINDOW // 2)
            scale = base[None, :] ** power[:, None]
            scale = jnp.concatenate([scale, scale], axis=-1)
            cos, sin = (jnp.cos(freqs), jnp.sin(freqs))
            q = q * cos * scale + rotate_half(q) * sin * scale
            k = k * cos / scale + rotate_half(k) * sin / scale
            return (q, k)

        def local_attention(q, k, v):
            b, h, n, d = q.shape
            w = n // WINDOW
            bq = q.reshape(b, h, w, WINDOW, d) * QK_SCALE
            bk = k.reshape(b, h, w, WINDOW, d)
            bv = v.reshape(b, h, w, WINDOW, d)

            def look_around(t):
                p = jnp.pad(t, ((0, 0), (0, 0), (1, 0), (0, 0), (0, 0)))
                return jnp.concatenate([p[:, :, :w], p[:, :, 1:]], axis=3)
            bk, bv = (look_around(bk), look_around(bv))
            bt = jnp.arange(n).reshape(w, WINDOW)
            btp = jnp.pad(bt, ((1, 0), (0, 0)), constant_values=-1)
            btk = jnp.concatenate([btp[:w], btp[1:]], axis=1)
            sim = jnp.einsum('bhwid,bhwjd->bhwij', bq, bk)
            i = bt[:, :, None]
            j = btk[:, None, :]
            mask = (i < j) | (i > j + WINDOW) | (j == -1)
            sim = jnp.where(mask, -jnp.finfo(sim.dtype).max, sim)
            attn = jax.nn.softmax(sim, axis=-1)
            out = jnp.einsum('bhwij,bhwjd->bhwid', attn, bv)
            return out.reshape(b, h, n, d)

        def _layer(x, wqkv, qs, ksc, wo, lg, lb, w1, b1, w2, b2):
            b, n, _ = x.shape
            h = shift_token(x)
            qkv = h @ wqkv
            q, k, v = jnp.split(qkv, 3, axis=-1)
            to_heads = lambda t: t.reshape(b, n, HEADS, DIM_HEAD).transpose(0, 2, 1, 3)
            q, k, v = (to_heads(q), to_heads(k), to_heads(v))
            q = l2norm(q) * qs
            k = l2norm(k) * ksc
            q, k = rotary_xpos(q, k)
            o = local_attention(q, k, v)
            o = o.transpose(0, 2, 1, 3).reshape(b, n, INNER)
            x = x + o @ wo
            h = shift_token(x)
            mu = h.mean(-1, keepdims=True)
            var = h.var(-1, keepdims=True)
            h = (h - mu) / jnp.sqrt(var + 1e-05) * lg + lb
            h = h @ w1 + b1
            a, g = jnp.split(h, 2, axis=-1)
            h = a * jax.nn.gelu(g, approximate=False)
            x = x + h @ w2 + b2
            return x
        key = jax.random.key(seed)
        ks = jax.random.split(key, 6)
        return {'x': jax.random.normal(ks[0], (B, N, DIM), jnp.float32), 'wqkv': jax.random.normal(ks[1], (DEPTH, DIM, 3 * INNER), jnp.float32) * 0.02, 'q_scale': jnp.ones((DEPTH, DIM_HEAD), jnp.float32), 'k_scale': jnp.ones((DEPTH, DIM_HEAD), jnp.float32), 'wo': jax.random.normal(ks[2], (DEPTH, INNER, DIM), jnp.float32) * 0.02, 'ln_g': jnp.ones((DEPTH, DIM), jnp.float32), 'ln_b': jnp.zeros((DEPTH, DIM), jnp.float32), 'w1': jax.random.normal(ks[3], (DEPTH, DIM, 2 * HID), jnp.float32) * 0.02, 'b1': jnp.zeros((DEPTH, 2 * HID), jnp.float32), 'w2': jax.random.normal(ks[4], (DEPTH, HID, DIM), jnp.float32) * 0.02, 'b2': jnp.zeros((DEPTH, DIM), jnp.float32)}
    _L1_ffn_in = _L1_ffn_setup()
    _d = {'L0_attn_x': _L0_attn_in['x'], 'L0_attn_Wqkv': _L0_attn_in['Wqkv'], 'L0_attn_Wproj': _L0_attn_in['Wproj'], 'L0_attn_bproj': _L0_attn_in['bproj'], 'L0_attn_alpha': _L0_attn_in['alpha'], 'L0_attn_beta': _L0_attn_in['beta'], 'L0_attn_gamma': _L0_attn_in['gamma'], 'L0_attn_A': _L0_attn_in['A'], 'L0_attn_Wphi1': _L0_attn_in['Wphi1'], 'L0_attn_bphi1': _L0_attn_in['bphi1'], 'L0_attn_Wphi2': _L0_attn_in['Wphi2'], 'L0_attn_bphi2': _L0_attn_in['bphi2'], 'L0_attn_Wpsi1': _L0_attn_in['Wpsi1'], 'L0_attn_bpsi1': _L0_attn_in['bpsi1'], 'L0_attn_ln_g': _L0_attn_in['ln_g'], 'L0_attn_ln_b': _L0_attn_in['ln_b'], 'L0_attn_Wpsi2': _L0_attn_in['Wpsi2'], 'L0_attn_bpsi2': _L0_attn_in['bpsi2'], 'L0_attn_mixing': _L0_attn_in['mixing'], 'L0_attn_temp_scale': _L0_attn_in['temp_scale'], 'L0_ffn_slot_query': _L0_ffn_in['slot_query'], 'L0_ffn_d_Wq': _L0_ffn_in['d_Wq'], 'L0_ffn_d_Wk': _L0_ffn_in['d_Wk'], 'L0_ffn_d_Wv': _L0_ffn_in['d_Wv'], 'L0_ffn_d_Wo': _L0_ffn_in['d_Wo'], 'L0_ffn_d_bq': _L0_ffn_in['d_bq'], 'L0_ffn_d_bk': _L0_ffn_in['d_bk'], 'L0_ffn_d_bv': _L0_ffn_in['d_bv'], 'L0_ffn_d_bo': _L0_ffn_in['d_bo'], 'L0_ffn_c_Wq': _L0_ffn_in['c_Wq'], 'L0_ffn_c_Wk': _L0_ffn_in['c_Wk'], 'L0_ffn_c_Wv': _L0_ffn_in['c_Wv'], 'L0_ffn_c_Wo': _L0_ffn_in['c_Wo'], 'L0_ffn_c_bq': _L0_ffn_in['c_bq'], 'L0_ffn_c_bk': _L0_ffn_in['c_bk'], 'L0_ffn_c_bv': _L0_ffn_in['c_bv'], 'L0_ffn_c_bo': _L0_ffn_in['c_bo'], 'L0_ffn_e_ln_g': _L0_ffn_in['e_ln_g'], 'L0_ffn_e_ln_b': _L0_ffn_in['e_ln_b'], 'L0_ffn_e_W1': _L0_ffn_in['e_W1'], 'L0_ffn_e_b1': _L0_ffn_in['e_b1'], 'L0_ffn_e_Wg': _L0_ffn_in['e_Wg'], 'L0_ffn_e_bg': _L0_ffn_in['e_bg'], 'L0_ffn_e_W2': _L0_ffn_in['e_W2'], 'L0_ffn_e_b2': _L0_ffn_in['e_b2'], 'L1_attn_Wq': _L1_attn_in['Wq'], 'L1_attn_Wk': _L1_attn_in['Wk'], 'L1_attn_Wv': _L1_attn_in['Wv'], 'L1_attn_Wo': _L1_attn_in['Wo'], 'L1_attn_gn_weight': _L1_attn_in['gn_weight'], 'L1_attn_gn_bias': _L1_attn_in['gn_bias'], 'L1_ffn_wqkv': _L1_ffn_in['wqkv'], 'L1_ffn_q_scale': _L1_ffn_in['q_scale'], 'L1_ffn_k_scale': _L1_ffn_in['k_scale'], 'L1_ffn_wo': _L1_ffn_in['wo'], 'L1_ffn_ln_g': _L1_ffn_in['ln_g'], 'L1_ffn_ln_b': _L1_ffn_in['ln_b'], 'L1_ffn_w1': _L1_ffn_in['w1'], 'L1_ffn_b1': _L1_ffn_in['b1'], 'L1_ffn_w2': _L1_ffn_in['w2'], 'L1_ffn_b2': _L1_ffn_in['b2']}
    _x0 = _d['L0_attn_x']
    _d['L0_attn_x'] = jax.random.normal(jax.random.fold_in(jax.random.key(seed), 1), (8, 512, 256), dtype=_x0.dtype)
    del _x0
    return _d

def reference(L0_attn_x, L0_attn_Wqkv, L0_attn_Wproj, L0_attn_bproj, L0_attn_alpha, L0_attn_beta, L0_attn_gamma, L0_attn_A, L0_attn_Wphi1, L0_attn_bphi1, L0_attn_Wphi2, L0_attn_bphi2, L0_attn_Wpsi1, L0_attn_bpsi1, L0_attn_ln_g, L0_attn_ln_b, L0_attn_Wpsi2, L0_attn_bpsi2, L0_attn_mixing, L0_attn_temp_scale, L0_ffn_slot_query, L0_ffn_d_Wq, L0_ffn_d_Wk, L0_ffn_d_Wv, L0_ffn_d_Wo, L0_ffn_d_bq, L0_ffn_d_bk, L0_ffn_d_bv, L0_ffn_d_bo, L0_ffn_c_Wq, L0_ffn_c_Wk, L0_ffn_c_Wv, L0_ffn_c_Wo, L0_ffn_c_bq, L0_ffn_c_bk, L0_ffn_c_bv, L0_ffn_c_bo, L0_ffn_e_ln_g, L0_ffn_e_ln_b, L0_ffn_e_W1, L0_ffn_e_b1, L0_ffn_e_Wg, L0_ffn_e_bg, L0_ffn_e_W2, L0_ffn_e_b2, L1_attn_Wq, L1_attn_Wk, L1_attn_Wv, L1_attn_Wo, L1_attn_gn_weight, L1_attn_gn_bias, L1_ffn_wqkv, L1_ffn_q_scale, L1_ffn_k_scale, L1_ffn_wo, L1_ffn_ln_g, L1_ffn_ln_b, L1_ffn_w1, L1_ffn_b1, L1_ffn_w2, L1_ffn_b2):

    def _L0_attn_ref(x, Wqkv, Wproj, bproj, alpha, beta, gamma, A, Wphi1, bphi1, Wphi2, bphi2, Wpsi1, bpsi1, ln_g, ln_b, Wpsi2, bpsi2, mixing, temp_scale):
        import jax, jax.numpy as jnp
        import numpy as np
        B, N, C = (2, 512, 256)
        H = 16
        HD = C // H
        KA_IN = 2 * HD
        KA_OUT = HD
        T = 4
        KA_HID = KA_IN // 2
        KA_O = KA_OUT // T
        TEMPERATURE = 0.72
        SCALE = HD ** (-0.5)
        LN_EPS = 1e-05
        Bx, Nx, Cx = x.shape
        qkv = (x @ Wqkv).reshape(Bx, Nx, 3, H, HD).transpose(2, 0, 3, 1, 4)
        q, k, v = (qkv[0], qkv[1], qkv[2])
        attn = jnp.einsum('bhnd,bhmd->bhnm', q, k) * (SCALE / TEMPERATURE)
        attn = attn * alpha[None, :, None, None] + beta[None, :, None, None]
        attn = jax.nn.softmax(attn, axis=-1) * gamma[None, :, None, None]
        qk = jnp.concatenate([q.mean(-2), k.mean(-2)], -1).reshape(Bx * H, KA_IN)
        Ax = jnp.einsum('md,tde->tme', qk, A)
        phi = jax.nn.silu(jnp.einsum('md,tdh->tmh', qk, Wphi1) + bphi1[:, None, :])
        phi = jnp.einsum('tmh,tho->tmo', phi, Wphi2) + bphi2[:, None, :]
        psi = jnp.einsum('tme,teg->tmg', Ax, Wpsi1) + bpsi1[:, None, :]
        mu = psi.mean(-1, keepdims=True)
        var = ((psi - mu) ** 2).mean(-1, keepdims=True)
        psi = (psi - mu) / jnp.sqrt(var + LN_EPS) * ln_g[:, None, :] + ln_b[:, None, :]
        psi = jax.nn.gelu(psi, approximate=False)
        psi = jnp.einsum('tmg,tgo->tmo', psi, Wpsi2) + bpsi2[:, None, :]
        terms = phi * psi * temp_scale * mixing[:, None, None]
        ka = jnp.transpose(terms, (1, 0, 2)).reshape(Bx, H, 1, HD)
        enhanced_v = v * (1.0 + ka)
        out = jnp.einsum('bhnm,bhmd->bhnd', attn, enhanced_v)
        out = out.transpose(0, 2, 1, 3).reshape(Bx, Nx, Cx)
        return out @ Wproj + bproj

    def _L0_ffn_ref(x, slot_query, d_Wq, d_Wk, d_Wv, d_Wo, d_bq, d_bk, d_bv, d_bo, c_Wq, c_Wk, c_Wv, c_Wo, c_bq, c_bk, c_bv, c_bo, e_ln_g, e_ln_b, e_W1, e_b1, e_Wg, e_bg, e_W2, e_b2):
        import jax, jax.numpy as jnp
        import numpy as np
        B, L, D = (4, 512, 256)
        H = 16
        E = 16
        NS = 16
        S = NS // E
        F = 1024
        EPS = 1e-05

        def _layernorm(x, g, b):
            mu = jnp.mean(x, axis=-1, keepdims=True)
            var = jnp.mean(jnp.square(x - mu), axis=-1, keepdims=True)
            return (x - mu) * jax.lax.rsqrt(var + EPS) * g + b

        def _mha(q, k, v, Wq, bq, Wk, bk, Wv, bv, Wo, bo):
            Bq, Lq, Dm = q.shape
            dh = Dm // H
            qh = (q @ Wq + bq).reshape(Bq, Lq, H, dh)
            kh = (k @ Wk + bk).reshape(Bq, -1, H, dh)
            vh = (v @ Wv + bv).reshape(Bq, -1, H, dh)
            scores = jnp.einsum('bqhd,bkhd->bhqk', qh, kh) / jnp.asarray(np.sqrt(dh), q.dtype)
            attn = jax.nn.softmax(scores, axis=-1)
            out = jnp.einsum('bhqk,bkhd->bqhd', attn, vh).reshape(Bq, Lq, Dm)
            return out @ Wo + bo
        Bx = x.shape[0]
        q = jnp.broadcast_to(slot_query, (Bx, NS, D))
        o = q + _mha(q, x, x, d_Wq, d_bq, d_Wk, d_bk, d_Wv, d_bv, d_Wo, d_bo)
        os = o.reshape(Bx, E, S, D)
        h = _layernorm(os, e_ln_g[None, :, None, :], e_ln_b[None, :, None, :])
        u = jax.nn.silu(jnp.einsum('besd,edf->besf', h, e_W1) + e_b1[None, :, None, :])
        g = jax.nn.silu(jnp.einsum('besd,edf->besf', h, e_Wg) + e_bg[None, :, None, :])
        y = jnp.einsum('besf,efd->besd', u * g, e_W2) + e_b2[None, :, None, :]
        o = o + y.reshape(Bx, NS, D)
        out = _mha(x, o, o, c_Wq, c_bq, c_Wk, c_bk, c_Wv, c_bv, c_Wo, c_bo)
        return out

    def _L1_attn_ref(x, Wq, Wk, Wv, Wo, gn_weight, gn_bias):
        import math
        import jax, jax.numpy as jnp
        import numpy as np
        N_HEADS = 8
        EPS = 1e-05
        B, L, D = x.shape
        H = N_HEADS
        dh = D // H
        gammas = 1.0 - jnp.exp(jnp.linspace(math.log(1.0 / 32.0), math.log(1.0 / 512.0), H)).astype(x.dtype)

        def proj(W):
            return (x @ W.T).reshape(B, L, H, dh).transpose(1, 0, 2, 3)
        qT, kT, vT = (proj(Wq), proj(Wk), proj(Wv))
        g = gammas[None, :, None, None]

        def step(S, qkv_t):
            q_t, k_t, v_t = qkv_t
            S = g * S + k_t[..., :, None] * v_t[..., None, :]
            y_t = jnp.einsum('bhde,bhd->bhe', S, q_t)
            return (S, y_t)
        S0 = jnp.zeros((B, H, dh, dh), dtype=x.dtype)
        _, ys = jax.lax.scan(step, S0, (qT, kT, vT))
        out = ys.transpose(1, 0, 2, 3)
        mean = out.mean(axis=(1, 3), keepdims=True)
        var = out.var(axis=(1, 3), keepdims=True)
        out = (out - mean) * jax.lax.rsqrt(var + EPS)
        out = out.reshape(B, L, D) * gn_weight + gn_bias
        return out @ Wo.T

    def _L1_ffn_ref(x, wqkv, q_scale, k_scale, wo, ln_g, ln_b, w1, b1, w2, b2):
        import jax, jax.numpy as jnp
        import numpy as np
        DIM = 256
        DEPTH = 2
        HEADS = 8
        DIM_HEAD = 64
        WINDOW = 128
        INNER = HEADS * DIM_HEAD
        HID = int(DIM * 4 * 2 / 3)
        B, N = (2, 2048)
        QK_SCALE = 8.0

        def shift_token(t):
            t1, t2 = jnp.split(t, 2, axis=-1)
            t2 = jnp.pad(t2, ((0, 0), (1, 0), (0, 0)))[:, :-1]
            return jnp.concatenate([t1, t2], axis=-1)

        def l2norm(t):
            return t / jnp.clip(jnp.linalg.norm(t, axis=-1, keepdims=True), 1e-12)

        def rotate_half(x):
            x1, x2 = jnp.split(x, 2, axis=-1)
            return jnp.concatenate([-x2, x1], axis=-1)

        def rotary_xpos(q, k):
            n = q.shape[-2]
            half_idx = jnp.arange(0, DIM_HEAD, 2, dtype=jnp.float32)
            inv_freq = 1.0 / 10000.0 ** (half_idx / DIM_HEAD)
            t = jnp.arange(n, dtype=jnp.float32)
            freqs = t[:, None] * inv_freq[None, :]
            freqs = jnp.concatenate([freqs, freqs], axis=-1)
            base = (half_idx + 0.4 * DIM_HEAD) / (1.4 * DIM_HEAD)
            power = (t - n // 2) / float(WINDOW // 2)
            scale = base[None, :] ** power[:, None]
            scale = jnp.concatenate([scale, scale], axis=-1)
            cos, sin = (jnp.cos(freqs), jnp.sin(freqs))
            q = q * cos * scale + rotate_half(q) * sin * scale
            k = k * cos / scale + rotate_half(k) * sin / scale
            return (q, k)

        def local_attention(q, k, v):
            b, h, n, d = q.shape
            w = n // WINDOW
            bq = q.reshape(b, h, w, WINDOW, d) * QK_SCALE
            bk = k.reshape(b, h, w, WINDOW, d)
            bv = v.reshape(b, h, w, WINDOW, d)

            def look_around(t):
                p = jnp.pad(t, ((0, 0), (0, 0), (1, 0), (0, 0), (0, 0)))
                return jnp.concatenate([p[:, :, :w], p[:, :, 1:]], axis=3)
            bk, bv = (look_around(bk), look_around(bv))
            bt = jnp.arange(n).reshape(w, WINDOW)
            btp = jnp.pad(bt, ((1, 0), (0, 0)), constant_values=-1)
            btk = jnp.concatenate([btp[:w], btp[1:]], axis=1)
            sim = jnp.einsum('bhwid,bhwjd->bhwij', bq, bk)
            i = bt[:, :, None]
            j = btk[:, None, :]
            mask = (i < j) | (i > j + WINDOW) | (j == -1)
            sim = jnp.where(mask, -jnp.finfo(sim.dtype).max, sim)
            attn = jax.nn.softmax(sim, axis=-1)
            out = jnp.einsum('bhwij,bhwjd->bhwid', attn, bv)
            return out.reshape(b, h, n, d)

        def _layer(x, wqkv, qs, ksc, wo, lg, lb, w1, b1, w2, b2):
            b, n, _ = x.shape
            h = shift_token(x)
            qkv = h @ wqkv
            q, k, v = jnp.split(qkv, 3, axis=-1)
            to_heads = lambda t: t.reshape(b, n, HEADS, DIM_HEAD).transpose(0, 2, 1, 3)
            q, k, v = (to_heads(q), to_heads(k), to_heads(v))
            q = l2norm(q) * qs
            k = l2norm(k) * ksc
            q, k = rotary_xpos(q, k)
            o = local_attention(q, k, v)
            o = o.transpose(0, 2, 1, 3).reshape(b, n, INNER)
            x = x + o @ wo
            h = shift_token(x)
            mu = h.mean(-1, keepdims=True)
            var = h.var(-1, keepdims=True)
            h = (h - mu) / jnp.sqrt(var + 1e-05) * lg + lb
            h = h @ w1 + b1
            a, g = jnp.split(h, 2, axis=-1)
            h = a * jax.nn.gelu(g, approximate=False)
            x = x + h @ w2 + b2
            return x
        for l in range(DEPTH):
            x = _layer(x, wqkv[l], q_scale[l], k_scale[l], wo[l], ln_g[l], ln_b[l], w1[l], b1[l], w2[l], b2[l])
        return x
    x = L0_attn_x
    x = _layernorm(x + _L0_attn_ref(x, L0_attn_Wqkv, L0_attn_Wproj, L0_attn_bproj, L0_attn_alpha, L0_attn_beta, L0_attn_gamma, L0_attn_A, L0_attn_Wphi1, L0_attn_bphi1, L0_attn_Wphi2, L0_attn_bphi2, L0_attn_Wpsi1, L0_attn_bpsi1, L0_attn_ln_g, L0_attn_ln_b, L0_attn_Wpsi2, L0_attn_bpsi2, L0_attn_mixing, L0_attn_temp_scale), axis=-1)
    x = _layernorm(x + _L0_ffn_ref(x, L0_ffn_slot_query, L0_ffn_d_Wq, L0_ffn_d_Wk, L0_ffn_d_Wv, L0_ffn_d_Wo, L0_ffn_d_bq, L0_ffn_d_bk, L0_ffn_d_bv, L0_ffn_d_bo, L0_ffn_c_Wq, L0_ffn_c_Wk, L0_ffn_c_Wv, L0_ffn_c_Wo, L0_ffn_c_bq, L0_ffn_c_bk, L0_ffn_c_bv, L0_ffn_c_bo, L0_ffn_e_ln_g, L0_ffn_e_ln_b, L0_ffn_e_W1, L0_ffn_e_b1, L0_ffn_e_Wg, L0_ffn_e_bg, L0_ffn_e_W2, L0_ffn_e_b2), axis=-1)
    x = _layernorm(x + _L1_attn_ref(x, L1_attn_Wq, L1_attn_Wk, L1_attn_Wv, L1_attn_Wo, L1_attn_gn_weight, L1_attn_gn_bias), axis=-1)
    x = _layernorm(x + _L1_ffn_ref(x, L1_ffn_wqkv, L1_ffn_q_scale, L1_ffn_k_scale, L1_ffn_wo, L1_ffn_ln_g, L1_ffn_ln_b, L1_ffn_w1, L1_ffn_b1, L1_ffn_w2, L1_ffn_b2), axis=-1)
    return x

_drawn_inputs = setup_inputs


def setup_inputs(seed=0):
    import zlib

    import numpy as np

    out = dict(_drawn_inputs(seed))
    spreads = {'L0_attn_bproj': (0.0, 0.1),
     'L0_attn_alpha': (1.0, 0.2),
     'L0_attn_beta': (1.0, 0.6),
     'L0_attn_gamma': (1.0, 0.2),
     'L0_attn_bphi1': (0.0, 0.8),
     'L0_attn_bphi2': (0.0, 0.8),
     'L0_attn_bpsi1': (0.0, 0.8),
     'L0_attn_ln_g': (1.0, 0.6),
     'L0_attn_ln_b': (0.0, 0.8),
     'L0_attn_bpsi2': (0.0, 0.8),
     'L0_attn_mixing': (0.25, 0.6),
     'L0_ffn_d_bq': (0.0, 0.8),
     'L0_ffn_d_bk': (0.0, 2.0),
     'L0_ffn_d_bv': (0.0, 0.8),
     'L0_ffn_d_bo': (0.0, 0.655),
     'L0_ffn_c_bq': (0.0, 0.8),
     'L0_ffn_c_bk': (0.0, 2.0),
     'L0_ffn_c_bv': (0.0, 2.0),
     'L0_ffn_c_bo': (0.0, 0.8),
     'L0_ffn_e_ln_g': (1.0, 0.6),
     'L0_ffn_e_ln_b': (0.0, 0.8),
     'L0_ffn_e_b1': (0.0, 0.8),
     'L0_ffn_e_bg': (0.0, 0.8),
     'L0_ffn_e_b2': (0.0, 0.8),
     'L1_attn_gn_weight': (1.0, 0.2),
     'L1_attn_gn_bias': (0.0, 0.1),
     'L1_ffn_q_scale': (1.0, 0.6),
     'L1_ffn_k_scale': (1.0, 0.6),
     'L1_ffn_ln_g': (1.0, 0.6),
     'L1_ffn_ln_b': (0.0, 0.8),
     'L1_ffn_b1': (0.0, 0.796),
     'L1_ffn_b2': (0.0, 0.1)}
    factors = {'L0_attn_A': 8.0,
     'L0_attn_Wphi1': 8.0,
     'L0_attn_Wphi2': 8.0,
     'L0_attn_Wpsi1': 8.0,
     'L0_attn_Wpsi2': 8.0,
     'L0_ffn_slot_query': 8.0,
     'L0_ffn_d_Wq': 8.0,
     'L0_ffn_d_Wk': 8.0,
     'L0_ffn_d_Wv': 8.0,
     'L0_ffn_d_Wo': 8.0,
     'L0_ffn_c_Wq': 8.0,
     'L0_ffn_c_Wk': 8.0,
     'L0_ffn_c_Wv': 4.168,
     'L0_ffn_e_W1': 8.0,
     'L0_ffn_e_Wg': 8.0,
     'L0_ffn_e_W2': 8.0}
    for name, (base, spread) in spreads.items():
        noise = np.random.default_rng([zlib.crc32(name.encode()), seed]).standard_normal(out[name].shape)
        drawn = base * np.exp(spread * noise) if base else spread * noise
        out[name] = jnp.asarray(drawn.astype(out[name].dtype))
    for name, factor in factors.items():
        out[name] = (out[name] * factor).astype(out[name].dtype)
    return out
```

```python
import concourse.bass as bass
from concourse import mybir

F32 = mybir.dt.float32
BF16 = mybir.dt.bfloat16
ACT = mybir.ActivationFunctionType
ALU = mybir.AluOpType
AX = mybir.AxisListType

P = 128
SEQS, TOKENS, CH = 8, 512, 256
TILES = TOKENS // P
CHUNKS = CH // P
EPS = 1e-5


class Later:

    activation = lambda self, *a, **k: lambda e: e.activation(*a, **k)
    bn_aggr = lambda self, *a, **k: lambda e: e.bn_aggr(*a, **k)
    bn_stats = lambda self, *a, **k: lambda e: e.bn_stats(*a, **k)
    matmul = lambda self, *a, **k: lambda e: e.matmul(*a, **k)
    memset = lambda self, *a, **k: lambda e: e.memset(*a, **k)
    reciprocal = lambda self, *a, **k: lambda e: e.reciprocal(*a, **k)
    scalar_tensor_tensor = lambda self, *a, **k: lambda e: e.scalar_tensor_tensor(*a, **k)
    stream_shuffle = lambda self, *a, **k: lambda e: e.stream_shuffle(*a, **k)
    tensor_copy = lambda self, *a, **k: lambda e: e.tensor_copy(*a, **k)
    tensor_reduce = lambda self, *a, **k: lambda e: e.tensor_reduce(*a, **k)
    tensor_scalar = lambda self, *a, **k: lambda e: e.tensor_scalar(*a, **k)
    tensor_tensor = lambda self, *a, **k: lambda e: e.tensor_tensor(*a, **k)
    tensor_tensor_reduce = lambda self, *a, **k: lambda e: e.tensor_tensor_reduce(*a, **k)
    transpose = lambda self, *a, **k: lambda e: e.transpose(*a, **k)


class Queue:

    def __init__(self, sem):
        self.sem, self.count, self.steps, self.seen = sem, 0, [], {}

    def wait(self, marks):
        for m in marks:
            if m is None:
                continue
            if isinstance(m, list):
                self.wait(m)
                continue
            sem, value = m
            if self.seen.get(id(sem), 0) < value:
                self.seen[id(sem)] = value
                self.steps.append(("wait", sem, value))

    def __call__(self, issue, *marks):
        self.wait(marks)
        self.count += 1
        self.steps.append(("run", issue(Later()), self.sem, 1))
        return (self.sem, self.count)

    def quiet(self, issue, *marks):
        self.wait(marks)
        self.steps.append(("run", issue(Later()), None, 0))

    def emit(self, engine):
        for kind, a, b, *c in self.steps:
            if kind == "wait":
                engine.wait_ge(a, b)
            else:
                instruction = a(engine)
                if b is not None:
                    instruction.then_inc(b, c[0])


class Transfers:

    def __init__(self, sem):
        self.sem, self.count = sem, 0

    def start(self, queue, out, in_, *marks):
        queue.wait(marks)
        self.count += 16
        queue.steps.append(("run", lambda e: e.dma_start(out, in_), self.sem, 16))

    @property
    def mark(self):
        return (self.sem, self.count)


class Banks:

    def __init__(self, psum, ids):
        self.psum, self.free = psum, [(i, None) for i in ids]

    def take(self):
        i, mark = self.free.pop(0)
        return i, self.psum[:, i, :], mark

    def give(self, i, mark):
        self.free.append((i, mark))


class Space:

    PAGE = 32

    def __init__(self, arena, columns):
        self.arena = arena
        self.used = [False] * (columns // self.PAGE)
        self.marks = [[] for _ in self.used]

    def take(self, columns, top=False):
        n = -(-columns // self.PAGE)
        spots = range(len(self.used) - n + 1)
        for at in (reversed(spots) if top else spots):
            if not any(self.used[at:at + n]):
                self.used[at:at + n] = [True] * n
                before = {}
                for page in self.marks[at:at + n]:
                    for sem, value in page:
                        before[id(sem)] = max(before.get(id(sem), (0, 0, sem))[0], value), 0, sem
                before = [(sem, value) for value, _, sem in before.values()]
                for page in range(at, at + n):
                    self.marks[page] = []
                return Piece(self, at, n, self.arena[:, at * self.PAGE:at * self.PAGE + columns], before)
        raise RuntimeError(f"no {columns} columns free; {self.used.count(False) * self.PAGE} in pieces")


class Piece:
    def __init__(self, space, at, pages, ap, before):
        self.space, self.at, self.pages, self.ap, self.before = space, at, pages, ap, before

    def give(self, *marks):
        flat = []
        for m in marks:
            flat += m if isinstance(m, list) else [m]
        flat = [m for m in flat if m is not None]
        for page in range(self.at, self.at + self.pages):
            self.space.used[page] = False
            self.space.marks[page] = list(flat)


def split(ap, *sizes):
    names = "abcd"[:len(sizes)]
    return ap.rearrange(f"p ({' '.join(names)}) -> p {' '.join(names)}", **dict(zip(names, sizes)))


def spread(ap, shape):
    while len(ap.shape) < len(shape):
        ap = ap.unsqueeze(len(ap.shape))
    return ap.to_broadcast(list(shape))


def repeated(ap, count):
    return ap.unsqueeze(1).to_broadcast([ap.shape[0], count] + list(ap.shape[1:]))


class Program:
    def __init__(self, nc, dram, small_at, out, blocks=4):
        self.nc, self.dram, self.small_at, self.out, self.blocks = nc, dram, small_at, out, blocks


    def build(self):
        nc = self.nc
        from contextlib import ExitStack
        with ExitStack() as ctx:
            sem = lambda name: ctx.enter_context(nc.semaphore(name))
            columns = 206 * 256
            arena = ctx.enter_context(nc.sbuf_tensor("arena", [P, columns], F32))
            self.psum = ctx.enter_context(nc.psum_tensor("banks", [P, 8, 512], F32))
            self.space = Space(arena, columns)
            self.pe, self.act, self.dve, self.pool, self.sp = (Queue(sem(n)) for n in ("pe", "act", "dve", "pool", "sp"))
            self.sem = sem
            self.start()
            self.block1()
            if self.blocks >= 2:
                self.block2()
            if self.blocks >= 3:
                self.block3()
            if self.blocks >= 4:
                self.block4()
            self.finish()
            block = ctx.enter_context(nc.Block())
            block.tensor(lambda e: self.pe.emit(e))
            block.scalar(lambda e: self.act.emit(e))
            block.vector(lambda e: self.dve.emit(e))
            block.gpsimd(lambda e: self.pool.emit(e))
            block.sync(lambda e: self.sp.emit(e))

    def load(self, name, top=False, source=None, queue=None):
        source = self.dram[name] if source is None else source
        piece = self.space.take(source.shape[-1], top)
        t = Transfers(self.sem(f"load_{name}"))
        t.start(queue or self.sp, piece.ap, source, piece.before)
        return piece, t.mark

    def start(self):
        x_nat, xT = self.space.take(SEQS * TILES * CH), self.space.take(SEQS * CHUNKS * (TOKENS + 1))
        self.x_nat = split(x_nat.ap, SEQS, TILES, CH)
        self.xT = split(xT.ap, SEQS, CHUNKS, TOKENS + 1)
        self.x_ready, self.xT_ready = [None] * SEQS, [None] * SEQS
        self.xT_read = [[] for _ in range(SEQS)]
        self.small, self.small_ready = self.load("small")
        self.wqkv, self.wqkv_ready = self.load("a_wqkv", True)
        xT_in = split(self.dram["xT"], SEQS, CHUNKS, TOKENS)
        for b in range(SEQS):
            t = Transfers(self.sem(f"x{b}"))
            t.start(self.sp, self.xT[:, b, :, 1:], xT_in[:, b])
            self.xT_ready[b] = t.mark
            if b == 0:
                self.wproj, self.wproj_ready = self.load("a_wproj", True)
                self.wqk, self.wqk_ready = self.load("a_wqk", True)
            t = Transfers(self.sem(f"xn{b}"))
            t.start(self.sp, self.x_nat[:, b], self.dram["x"][b].rearrange("(t p) c -> p t c", p=P))
            self.x_ready[b] = t.mark
        self.edge_zero = self.pool(lambda e: e.memset(self.xT[:, :, :, 0:1], 0.0))
        self.half = self.space.take(64)
        self.half_ready = self.pool(lambda e: e.memset(self.half.ap, -0.5))
        ident = self.S("identity")
        self.ident16 = self.space.take(64)
        self.ident16 = self.ident16.ap.bitcast(BF16)
        self.ident16_ready = self.dve(lambda e: e.tensor_copy(self.ident16, ident), self.small_ready)

    def S(self, name):
        at, n = self.small_at[name]
        return self.small.ap[:, at:at + n]

    def finish(self):
        t = Transfers(self.sem("store"))
        for b in range(SEQS):
            t.start(self.sp, self.out[b].rearrange("(t p) c -> p t c", p=P), self.x_nat[:, b], self.x_ready[b])
        self.sp.wait([t.mark])


    def rsqrt(self, out, in_, scratch, count, *marks):
        eps = self.pool(lambda e: e.tensor_scalar(scratch, in_, EPS, None, ALU.add), *marks, self.half_ready)
        half = self.half.ap[:, 0:count]
        return self.pool(lambda e: e.tensor_tensor(out, scratch, half, ALU.pow), eps)

    def norm_and_turn(self, b, banks, sums, turn=True):
        x, small = self.x_nat[:, b], self.space.take(TILES * 10)
        stats = split(small.ap[:, 0:TILES * 6], TILES, 6)
        mv = split(small.ap[:, TILES * 6:TILES * 8], TILES, 2)
        rstd, scratch = small.ap[:, TILES * 8:TILES * 9], small.ap[:, TILES * 9:TILES * 10]
        for t in range(TILES):
            s = self.dve(lambda e, t=t: e.bn_stats(stats[:, t], x[:, t]), sums[t], small.before)
            m = self.dve(lambda e, t=t: e.bn_aggr(mv[:, t], stats[:, t]), s)
        yield
        r = self.rsqrt(rstd, mv[:, :, 1], scratch, TILES, m)
        done = []
        for t in range(TILES):
            done.append(self.dve(lambda e, t=t: e.tensor_scalar(
                x[:, t], x[:, t], mv[:, t, 0:1], rstd[:, t:t + 1], ALU.subtract, ALU.mult), r))
        small.give(done[-1])
        self.x_ready[b] = done[-1]
        if not turn:
            return
        yield
        for c in range(CHUNKS):
            i, bank, free = banks.take()
            for t in range(TILES):
                put = self.pe(lambda e, t=t: e.transpose(bank[:, t * P:(t + 1) * P], x[:, t, c * P:(c + 1) * P], self.S("identity")),
                              done[t], free)
            out = self.xT[:, b, c, 1:]
            q = self.act if c else self.dve
            if c:
                copied = self.act(lambda e: e.activation(out, bank, ACT.Copy), put, self.xT_read[b], self.edge_zero)
            else:
                first = self.dve(lambda e: e.tensor_copy(out, bank), put, self.xT_read[b], self.edge_zero)
            banks.give(i, copied if c else first)
            yield
        self.xT_ready[b] = [first, copied]
        self.xT_read[b] = []

    @staticmethod
    def interleave(makers, lanes, offset=0):
        active, rounds = [], 0
        makers = list(makers)
        while active or makers:
            if makers and len(active) < lanes and (not active or rounds >= offset):
                active.append(makers.pop(0)())
                rounds = 0
            rounds += 1
            for g in list(active):
                if next(g, "end") == "end":
                    active.remove(g)


    def gating(self, banks):
        S, sp = self.S, self.space
        H, HD = 16, 16
        work = sp.take(16 + 9 * P + 64)
        w = work.ap
        mean = split(w[:, 0:16], CHUNKS, SEQS)
        area = [w[:, 16 + i * P:16 + (i + 1) * P] for i in range(9)]
        wqk = split(self.wqk.ap, CHUNKS, H, 2 * HD)
        for b in range(SEQS):
            m = self.dve(lambda e, b=b: e.tensor_reduce(mean[:, :, b], self.xT[:, b, :, 1:], AX.X, ALU.add),
                         self.xT_ready[b], work.before)
            if b % 2:
                yield
        m = self.dve(lambda e: e.tensor_scalar(w[:, 0:16], w[:, 0:16], 1.0 / TOKENS, None, ALU.mult), m)
        i, bank, free = banks.take()
        for h in range(H):
            for c in range(CHUNKS):
                mm = self.pe(lambda e, h=h, c=c: e.matmul(bank[0:32, h * SEQS:(h + 1) * SEQS], wqk[:, c, h],
                                                          mean[:, c, :], start=c == 0, stop=c == 1), m, free, self.wqk_ready)
        self.wqk.give(mm)
        qk = area[0]
        qk_ready = self.act(lambda e: e.activation(qk[0:32, :], bank[0:32, 0:P], ACT.Copy), mm)
        banks.give(i, qk_ready)

        def product(out, lhsT, rhs, rows, *marks, copy=None):
            i, bank, free = banks.take()
            mm = self.pe(lambda e: e.matmul(bank[0:rows, 0:P], lhsT, rhs, start=True, stop=True), *marks, free)
            done = copy(bank, mm)
            banks.give(i, done)
            return done

        plain = lambda out, rows, bias: lambda bank, mm: self.dve(
            lambda e: e.tensor_scalar(out, bank[0:rows, 0:P], bias, None, ALU.add), mm)
        ax, hid, phi, psi, dev, sq, rs, pg, psi2 = area
        hid_r = product(None, S("a_phi1")[0:32], qk[0:32], P, qk_ready, copy=lambda bank, mm: self.act(
            lambda e: e.activation(hid, bank[:, 0:P], ACT.Silu, bias=S("a_bphi1")), mm))
        yield
        phi_r = product(None, S("a_phi2"), hid, 16, hid_r, copy=plain(phi[0:16], 16, S("a_bphi2")[0:16]))
        yield
        ax_r = product(None, S("a_A")[0:32], qk[0:32], P, copy=lambda bank, mm: self.dve(
            lambda e: e.tensor_copy(hid, bank[:, 0:P]), mm, phi_r))
        yield
        psi_r = product(None, S("a_psi1"), hid, P, ax_r, copy=plain(psi, P, S("a_bpsi1")))
        yield
        dev_r = product(None, S("same_head32"), psi, P, psi_r, copy=lambda bank, mm: self.dve(
            lambda e: e.scalar_tensor_tensor(dev, bank[:, 0:P], -1.0 / 32, psi, ALU.mult, ALU.add), mm))
        yield
        sq_r = self.dve(lambda e: e.tensor_tensor(sq, dev, dev, ALU.mult), dev_r)
        var_r = product(None, S("same_head32"), sq, P, sq_r, copy=lambda bank, mm: self.dve(
            lambda e: e.tensor_scalar(rs, bank[:, 0:P], 1.0 / 32, EPS, ALU.mult, ALU.add), mm))
        yield
        std_r = self.act(lambda e: e.activation(sq, rs, ACT.Sqrt), var_r)
        rstd_r = self.dve(lambda e: e.reciprocal(rs, sq), std_r)
        a = self.dve(lambda e: e.tensor_tensor(dev, dev, rs, ALU.mult), rstd_r)
        a = self.dve(lambda e: e.tensor_scalar(dev, dev, S("a_lng"), S("a_lnb"), ALU.mult, ALU.add), a)
        gelu_r = self.act(lambda e: e.activation(pg, dev, ACT.Gelu), a)
        yield
        psi2_r = product(None, S("a_psi2"), pg, 16, gelu_r, copy=plain(psi2[0:16], 16, S("a_bpsi2")[0:16]))
        yield
        t = self.dve(lambda e: e.tensor_tensor(psi2[0:16], psi2[0:16], phi[0:16], ALU.mult), psi2_r)
        t = self.dve(lambda e: e.tensor_scalar(psi2[0:16], psi2[0:16], S("a_temp")[0:16], S("a_mix")[0:16],
                                               ALU.mult, ALU.mult), t)
        i, bank, free = banks.take()
        terms = split(psi2, 4, 4, SEQS)
        place = split(S("spread16"), 4, P)
        for j in range(4):
            mm = self.pe(lambda e, j=j: e.matmul(split(bank[:, 0:32], 4, SEQS), place[0:16, j], terms[0:16, :, j, :],
                                                 start=j == 0, stop=j == 3), t, free)
        self.factor = sp.take(32)
        factor = split(self.factor.ap, 4, SEQS)
        f = self.dve(lambda e: e.scalar_tensor_tensor(factor, split(bank[:, 0:32], 4, SEQS), 1.0,
                                                      spread(S("a_gamma"), [P, 4, SEQS]), ALU.add, ALU.mult),
                     mm, self.factor.before)
        banks.give(i, f)
        work.give(f)
        self.factor_ready = f

    Q_PARTS, K_PARTS = (0, 0, 1, 1, 0, 2), (0, 1, 0, 1, 2, 0)

    def block1(self):
        sp, pe, act, dve, pool = self.space, self.pe, self.act, self.dve, self.pool
        S = self.S
        H, HD = 16, 16
        SCALE = HD ** -0.5 / 0.72
        max_banks, exp_banks = Banks(self.psum, (0, 1, 2)), Banks(self.psum, (3, 4, 5))
        out_banks, misc = Banks(self.psum, (6,)), Banks(self.psum, (7,))
        wqkv = split(self.wqkv.ap, CHUNKS, 3, CH)
        xT = self.xT

        setup = sp.take(2 + 16 + 64 + 64)
        alpha = setup.ap[:, 0:2]
        alpha_ready = dve(lambda e: e.tensor_scalar(alpha, S("a_alpha"), SCALE, None, ALU.mult), self.small_ready)
        beta16 = split(setup.ap[:, 2:2 + 32].bitcast(BF16)[:, 0:48], 3, H)
        rest = split(setup.ap[:, 40:40 + 32], 2, H)
        m = dve(lambda e: e.tensor_copy(beta16[:, 0], S("a_beta")), self.small_ready)
        m = dve(lambda e: e.tensor_tensor(rest[:, 0], S("a_beta"), beta16[:, 0], ALU.subtract), m)
        m = dve(lambda e: e.tensor_copy(beta16[:, 1], rest[:, 0]), m)
        m = dve(lambda e: e.tensor_tensor(rest[:, 1], rest[:, 0], beta16[:, 1], ALU.subtract), m)
        beta_ready = dve(lambda e: e.tensor_copy(beta16[:, 2], rest[:, 1]), m)

        parts_dram = self.nc.dram_tensor("parts", (2 * SEQS, P, 6, TOKENS), BF16).ap()

        halves = []
        for n in range(2):
            piece = sp.take(2 * 8 * TOKENS // 2)
            stack = split(piece.ap.bitcast(BF16), 2, 8, TOKENS)
            ones = S("ones5")[96:128]
            made = dve(lambda e: e.tensor_copy(split(piece.ap.bitcast(BF16), 2, 8 * TOKENS)[96:128, 1], ones.to_broadcast([32, 8 * TOKENS])),
                       self.small_ready, piece.before)
            halves.append(dict(piece=piece, stack=stack, made=made, read=[], dma=Transfers(self.sem(f"stack{n}")),
                               shift=[Transfers(self.sem(f"shift{n}{g}")) for g in (0, 1)]))
        shifts = []
        for n in range(2):
            piece = sp.take(TILES * P // 2)
            made = pool(lambda e: e.memset(piece.ap, 0.0), piece.before)
            shifts.append(dict(ap=split(piece.ap.bitcast(BF16), TILES, 4, 32), piece=piece, made=made, read=None))
        values = []
        for n in range(2):
            piece = sp.take(TILES * H * 32)
            made = pool(lambda e: e.memset(piece.ap, 1.0), piece.before)
            values.append(dict(ap=split(piece.ap, TILES, H, 32), piece=piece, made=made, read=[]))
        biased = []
        for b in range(SEQS):
            biased.append(pool(lambda e, b=b: e.tensor_tensor(self.x_nat[:, b], self.x_nat[:, b], repeated(S("a_bproj"), TILES), ALU.add),
                               self.x_ready[b], self.small_ready))

        def prepare(half):
            b, c = divmod(half, 2)
            buf = halves[half % 2]
            parts = sp.take(6 * TOKENS // 2)
            part = split(parts.ap.bitcast(BF16), 6, TOKENS)
            ready = []
            for side in (0, 1):
                i, bank, free = misc.take()
                for k in range(CHUNKS):
                    mm = pe(lambda e, k=k: e.matmul(bank, wqkv[:, k, side, c * P:(c + 1) * P], xT[:, b, k, 1:],
                                                    start=k == 0, stop=k == 1), free, self.xT_ready[b], self.wqkv_ready)
                rest = sp.take(2 * TOKENS)
                whole, left = rest.ap[:, 0:TOKENS], rest.ap[:, TOKENS:]
                if side == 0:
                    m = dve(lambda e: e.tensor_scalar(whole, bank, alpha[:, c:c + 1], None, ALU.mult), mm, alpha_ready, rest.before)
                else:
                    m = act(lambda e: e.activation(whole, bank, ACT.Copy), mm, rest.before)
                misc.give(i, m)
                hi, mid, lo = (part[:, 3 * side + n] for n in range(3))
                a = pool(lambda e: e.tensor_copy(hi, whole), m, parts.before)
                yield
                a = pool(lambda e: e.tensor_tensor(left, whole, hi, ALU.subtract), a)
                a = pool(lambda e: e.tensor_copy(mid, left), a)
                yield
                a = pool(lambda e: e.tensor_tensor(lo, left, mid, ALU.subtract), a)
                rest.give(a)
                kept = Transfers(self.sem(f"parts{half}_{side}")) if half < 2 else buf["kept"][side]
                kept.start(self.sp, parts_dram[half, :, 3 * side:3 * side + 3, :], part[:, 3 * side:3 * side + 3], a)
                buf.setdefault("kept", []).append(kept) if half < 2 else None
                yield
                yield
                for n, which in enumerate((self.Q_PARTS, self.K_PARTS)[side]):
                    buf["dma"].start(self.sp, buf["stack"][16 * n:16 * n + 16, side],
                                     parts_dram[half, :, 3 * side + which, :].rearrange("(h d) n -> d h n", d=HD),
                                     kept.mark, buf["read"], buf["made"])
                    if n == 2:
                        yield
                yield
            parts.give(kept.mark, buf["kept"][0].mark)
            buf["ready"] = buf["dma"].mark
            if c == 0:
                v = values[b % 2]
                for t in range(TILES):
                    i, bank, free = misc.take()
                    for k in range(CHUNKS):
                        mm = pe(lambda e, k=k: e.matmul(bank[:, 0:CH], xT[:, b, k, 1 + t * P:1 + (t + 1) * P], wqkv[:, k, 2, :],
                                                        start=k == 0, stop=k == 1), free, self.xT_ready[b])
                    src = split(bank[:, 0:CH], H, HD)
                    m = act(lambda e: e.activation(v["ap"][:, t, :, 0:HD], src, ACT.Copy), mm, v["made"], v["read"])
                    misc.give(i, m)
                    v["ready"] = m
                    yield

        def score_maxima(u, t):
            half, g2 = divmod(u, 2)
            buf, sh = halves[half % 2], shifts[u % 2]
            if t == 0:
                big = sp.take(TILES * 4 * 2)
                sh["max"], sh["max_piece"] = split(big.ap[:, 0:16], TILES, 4), big
            for j in range(4):
                i, bank, free = max_banks.take()
                st = buf["stack"]
                mm = pe(lambda e: e.matmul(bank, st[0:96, 0, 4 * g2 + j, t * P:(t + 1) * P], st[0:96, 1, 4 * g2 + j, :],
                                           start=True, stop=True), free, buf["ready"])
                m = dve(lambda e: e.tensor_reduce(sh["max"][:, t, j:j + 1], bank, AX.X, ALU.max, negate=True), mm, sh["max_piece"].before)
                max_banks.give(i, m)
            sh["max_ready"] = m

        def shift_rows(u):
            half, g2 = divmod(u, 2)
            buf, sh = halves[half % 2], shifts[u % 2]
            h0 = (half % 2) * 8 + g2 * 4
            rest = split(sh["max_piece"].ap[:, 16:32], TILES, 4)
            mx, out = sh["max"], sh["ap"]
            m = dve(lambda e: e.tensor_tensor(mx, mx, repeated(S("a_beta")[:, h0:h0 + 4], TILES), ALU.subtract), sh["max_ready"])
            m = dve(lambda e: e.tensor_copy(out[:, :, :, 0], mx), m, sh["made"], sh["read"])
            m = dve(lambda e: e.tensor_tensor(rest, mx, out[:, :, :, 0], ALU.subtract), m)
            m = dve(lambda e: e.tensor_copy(out[:, :, :, 1], rest), m)
            sh["max_piece"].give(m)
            for n in range(3):
                m = dve(lambda e, n=n: e.tensor_copy(out[:, :, :, 2 + n], repeated(beta16[:, n, h0:h0 + 4], TILES)), beta_ready)
            i, bank, free = misc.take()
            for t in range(TILES):
                mm = pe(lambda e, t=t: e.matmul(bank[:, t * P:(t + 1) * P], out[:, t].rearrange("p j s -> p (j s)"), self.ident16,
                                                start=True, stop=True), m, free, self.ident16_ready)
            sh["read"] = mm
            flat = sp.take(TOKENS // 2)
            rows = flat.ap.bitcast(BF16)
            m = act(lambda e: e.activation(rows, bank, ACT.Copy), mm, flat.before)
            misc.give(i, m)
            move = buf["shift"][g2]
            for j in range(4):
                move.start(self.sp, buf["stack"][96:128, 0, 4 * g2 + j, :], rows[32 * j:32 * j + 32, :], m, buf["read"])
            flat.give(move.mark)

        outs = {}

        def attend(u, t):
            half, g2 = divmod(u, 2)
            b = half // 2
            buf, v = halves[half % 2], values[b % 2]
            st = buf["stack"]
            e_piece = sp.take(4 * TOKENS)
            ex = split(e_piece.ap, 4, TOKENS)
            if t == 0:
                outs[u] = out_banks.take()
            i_out, out, out_free = outs[u]
            marks = []
            for j in range(4):
                i, bank, free = exp_banks.take()
                mm = pe(lambda e: e.matmul(bank, st[:, 1, 4 * g2 + j, t * P:(t + 1) * P], st[:, 0, 4 * g2 + j, :],
                                           start=True, stop=True), free, buf["ready"], buf["shift"][g2].mark)
                m = act(lambda e: e.activation(ex[:, j], bank, ACT.Exp), mm, e_piece.before)
                exp_banks.give(i, m)
                marks.append(m)
            if t == TILES - 1:
                buf["last"] = mm
            def values_product():
                h0 = (half % 2) * 8 + g2 * 4
                for j in range(4):
                    mm = pe(lambda e, j=j: e.matmul(out[32 * j:32 * j + 32, :], v["ap"][:, t, h0 + j, :], ex[:, j],
                                                    start=t == 0, stop=t == TILES - 1, skip_group_check=True),
                            marks[j], v["ready"], out_free)
                e_piece.give(mm)
                return mm
            return values_product

        headed = {}

        def normalise(u, mm):
            half, g2 = divmod(u, 2)
            b, g = half // 2, u % 4
            i_out, out, _ = outs[u]
            work = sp.take(TOKENS)
            o_piece = sp.take(TOKENS)
            m = dve(lambda e: e.stream_shuffle(work.ap, out, [16 + r % 16 for r in range(32)]), mm, work.before)
            m = act(lambda e: e.activation(work.ap, work.ap, ACT.Ln), m)
            m = act(lambda e: e.activation(work.ap, work.ap, ACT.Exp, scale=-1.0), m)
            f = split(self.factor.ap, 4, SEQS)[:, g, b:b + 1]
            m = dve(lambda e: e.scalar_tensor_tensor(o_piece.ap, out, f, work.ap, ALU.mult, ALU.mult), m, self.factor_ready, o_piece.before)
            out_banks.give(i_out, m)
            work.give(m)
            headed[u] = (o_piece, m)

        def project(b):
            wp = split(self.wproj.ap, 4, CH)
            sums = []
            for t in range(TILES):
                i, bank, free = misc.take()
                for g in range(4):
                    o_piece, m = headed[4 * b + g]
                    mm = pe(lambda e, g=g, o=o_piece: e.matmul(bank[:, 0:CH], o.ap[:, t * P:(t + 1) * P], wp[:, g],
                                                                start=g == 0, stop=g == 3), m, free, self.wproj_ready)
                x = self.x_nat[:, b, t]
                s = dve(lambda e: e.tensor_tensor(x, x, bank[:, 0:CH], ALU.add), mm, biased[b])
                misc.give(i, s)
                sums.append(s)
                yield
            for g in range(4):
                headed.pop(4 * b + g)[0].give(mm)
            yield from self.norm_and_turn(b, misc, sums)

        units = 2 * 2 * SEQS
        background = []

        def advance():
            while background:
                if next(background[0], "end") != "end":
                    return
                background.pop(0)

        for _ in prepare(0):
            pass
        background.append(self.gating(misc))
        self.factor_ready = None
        preparing, last_pv = {}, None
        for u in range(-1, units):
            if (u == -1 or (u > 0 and u % 2 == 0)) and (u + 3) // 2 < 2 * SEQS:
                half = 1 if u == -1 else u // 2 + 1
                halves[half % 2]["read"] = halves[half % 2].get("last")
                g = prepare(half)
                preparing[half] = g
                background.append(g)
            pending = None
            for t in range(TILES):
                if u >= 0:
                    following = attend(u, t)
                if u + 1 < units:
                    score_maxima(u + 1, t)
                if u >= 0:
                    if pending:
                        pending()
                    pending = following
                advance()
            if u >= 0:
                mm = pending()
                last = mm
                if (u // 2) % 2:
                    values[(u // 4) % 2]["read"] = mm
            if u + 1 < units:
                shift_rows(u + 1)
            if u == 0:
                while self.factor_ready is None:
                    advance()
            if u >= 0:
                normalise(u, mm)
                if u % 4 == 3:
                    background.append(project(u // 4))
            if u >= -1 and (u + 1) % 2 == 1:
                half = (u + 2) // 2
                while half in preparing and "done" != preparing[half] and preparing[half] in background:
                    advance()
        while background:
            advance()
        for d in halves:
            d["piece"].give(last)
        for d in shifts:
            d["piece"].give(d["read"])
        for d in values:
            d["piece"].give(last)
        setup.give(m_all := [self.pe_mark(), self.act_mark(), self.dve_mark(), self.pool_mark()])
        self.wqkv.give(m_all)
        self.wproj.give(m_all)
        self.factor.give(m_all)

    def pe_mark(self):
        return (self.pe.sem, self.pe.count)

    def act_mark(self):
        return (self.act.sem, self.act.count)

    def dve_mark(self):
        return (self.dve.sem, self.dve.count)

    def pool_mark(self):
        return (self.pool.sem, self.pool.count)


    def all_marks(self):
        return [self.pe_mark(), self.act_mark(), self.dve_mark(), self.pool_mark()]

    def block2(self):
        sp, pe, act, dve, pool, S = self.space, self.pe, self.act, self.dve, self.pool, self.S
        H, HD, SLOTS, EXPERTS, HIDDEN = 16, 16, 16, 16, 1024
        banks = Banks(self.psum, range(8))
        W = {}
        for n in ("d_Wq", "d_WkT", "d_Wv", "d_Wo"):
            W[n] = self.load(n, True)
        w2 = lambda n: split(W[n][0].ap, CHUNKS, CH)
        ident = S("identity")

        RING = 7
        order = [(m, 4 * q + j) for q in range(4) for m in ("e_W1", "e_Wg", "e_W2") for j in range(4)]
        ring = [sp.take(2048, True) for _ in range(RING)]
        ring_dma = [Transfers(self.sem(f"expert{n}")) for n in range(RING)]
        arrived, issued, released = {}, [0], {}
        def load_next(mark):
            n = issued[0]
            if n < len(order):
                m, e = order[n]
                ring_dma[n % RING].start(self.sp, ring[n % RING].ap, self.dram[m][e], ring[n % RING].before, mark)
                arrived[order[n]] = (ring[n % RING].ap, ring_dma[n % RING].mark)
                issued[0] += 1
        for _ in range(RING):
            load_next(None)
        bias = {}
        def load_bias(q):
            for n in ("e_b1", "e_bg"):
                piece = sp.take(HIDDEN, True)
                t = Transfers(self.sem(f"{n}{q}"))
                t.start(self.sp, piece.ap, self.dram[n][q], piece.before)
                bias[n, q] = (piece, t.mark)

        once = sp.take(32 + 2 * 256 * 2 + 8)
        q_T = split(once.ap[:, 0:32], CHUNKS, SLOTS)
        q_blk = split(once.ap[:, 32:32 + 512], CHUNKS, H, SLOTS)
        meet = split(once.ap[:, 544:544 + 512], CHUNKS, H * SLOTS)
        const = once.ap[:, 1056:1058]
        head_of = split(S("head_of"), CHUNKS, H)
        i, bank, free = banks.take()
        for f in range(CHUNKS):
            for k in range(CHUNKS):
                mm = pe(lambda e: e.matmul(bank[:, f * 16:f * 16 + 16], w2("d_Wq")[:, k, f * P:(f + 1) * P],
                                           split(S("slotT"), CHUNKS, SLOTS)[:, k], start=k == 0, stop=k == 1), free, W["d_Wq"][1])
        for f in range(CHUNKS):
            m = dve(lambda e: e.tensor_scalar(q_T[:, f], bank[:, f * 16:f * 16 + 16], S("d_bq")[:, f:f + 1], 0.25, ALU.add, ALU.mult),
                    mm, once.before)
        banks.give(i, m)
        for f in range(CHUNKS):
            blk = dve(lambda e: e.tensor_tensor(q_blk[:, f], repeated(q_T[:, f], H), spread(head_of[:, f], [P, H, SLOTS]), ALU.mult), m)
        i, bank, free = banks.take()
        for c in range(CHUNKS):
            for f in range(CHUNKS):
                mm = pe(lambda e: e.matmul(bank[:, c * 256:(c + 1) * 256], w2("d_WkT")[:, f, c * P:(c + 1) * P],
                                           q_blk[:, f].rearrange("p h s -> p (h s)"), start=f == 0, stop=f == 1), free, blk, W["d_WkT"][1])
        meet_ready = act(lambda e: e.activation(meet.rearrange("p c n -> p (c n)"), bank, ACT.Copy), mm, once.before)
        banks.give(i, meet_ready)
        i, bank, free = banks.take()
        for t in range(2):
            for f in range(CHUNKS):
                mm = pe(lambda e: e.matmul(bank[:, t:t + 1], q_blk[:, f].rearrange("p h s -> p (h s)")[:, t * P:(t + 1) * P],
                                           S("d_bk")[:, f:f + 1], start=f == 0, stop=f == 1), free, blk)
        const_ready = dve(lambda e: e.tensor_copy(const, bank[:, 0:2]), mm, meet_ready)
        banks.give(i, const_ready)

        gathered = sp.take(CHUNKS * H * P)
        g_view = split(gathered.ap, CHUNKS, H, SEQS, SLOTS)
        gathered_ready = []
        o_bias = []
        for b in range(SEQS):
            o_bias.append(None)

        def slots_attend(b):
            work = sp.take(2 * TOKENS + 16)
            s = split(work.ap[:, 0:2 * TOKENS], 2, TOKENS)
            st = work.ap[:, 2 * TOKENS:]
            turned = sp.take(TILES * 2 * P)
            aT = split(turned.ap, TILES, 2, P)
            copies = []
            for t in range(2):
                i, bank, free = banks.take()
                for c in range(CHUNKS):
                    mm = pe(lambda e: e.matmul(bank, meet[:, c, t * P:(t + 1) * P], self.xT[:, b, c, 1:], start=c == 0, stop=c == 1),
                            free, meet_ready, self.xT_ready[b])
                m = dve(lambda e: e.tensor_scalar(s[:, t], bank, const[:, t:t + 1], None, ALU.add), mm, const_ready, work.before)
                banks.give(i, m)
                yield
                m = dve(lambda e: e.tensor_reduce(st[:, t:t + 1], s[:, t], AX.X, ALU.max, negate=True), m)
                m = act(lambda e: e.activation(s[:, t], s[:, t], ACT.Exp, bias=st[:, t:t + 1], accum_out=st[:, 4 + t:5 + t]), m)
                yield
                m = dve(lambda e: e.reciprocal(st[:, 8 + t:9 + t], st[:, 4 + t:5 + t]), m)
                m = dve(lambda e: e.tensor_scalar(s[:, t], s[:, t], st[:, 8 + t:9 + t], None, ALU.mult), m)
                yield
                i, bank, free = banks.take()
                for n in range(TILES):
                    mm = pe(lambda e: e.transpose(bank[:, n * P:(n + 1) * P], s[:, t, n * P:(n + 1) * P], ident), m, free)
                m = act(lambda e: e.activation(aT[:, :, t], split(bank, TILES, P), ACT.Copy), mm, turned.before)
                banks.give(i, m)
                copies.append(m)
                yield
            work.give(m)
            i, bank, free = banks.take()
            for c in range(CHUNKS):
                for n in range(TILES):
                    mm = pe(lambda e: e.matmul(bank[:, c * 256:(c + 1) * 256], self.x_nat[:, b, n, c * P:(c + 1) * P],
                                               aT[:, n].rearrange("p t s -> p (t s)"), start=n == 0, stop=n == TILES - 1),
                            copies, free, self.x_ready[b])
            turned.give(mm)
            for c in range(CHUNKS):
                m = dve(lambda e: e.tensor_copy(g_view[:, c, :, b, :], split(bank[:, c * 256:(c + 1) * 256], H, SLOTS)), mm, gathered.before)
            banks.give(i, m)
            gathered_ready.append(m)
            o_bias[b] = pool(lambda e: e.tensor_tensor(self.x_nat[:, b], self.x_nat[:, b], repeated(S("c_bo"), TILES), ALU.add), mm)

        self.interleave([lambda b=b: slots_attend(b) for b in range(SEQS)], 3, 2)

        slots = sp.take(256 * 4 + 32)
        o, h, tmp = (slots.ap[:, n * 256:(n + 1) * 256] for n in range(3))
        oT = split(slots.ap[:, 768:1024], CHUNKS, P)
        st = slots.ap[:, 1024:]
        g3 = split(gathered.ap, CHUNKS, H, P)
        i, bank, free = banks.take()
        for hd in range(H):
            for c in range(CHUNKS):
                mm = pe(lambda e: e.matmul(bank[:, hd * 16:hd * 16 + 16], g3[:, c, hd], w2("d_Wv")[:, c, hd * 16:hd * 16 + 16],
                                           start=c == 0, stop=c == 1), free, gathered_ready, W["d_Wv"][1])
        gathered.give(mm)
        m = dve(lambda e: e.tensor_tensor(tmp, bank[:, 0:256], S("d_bv"), ALU.add), mm, slots.before)
        banks.give(i, m)

        def turned(src, m):
            i, bank, free = banks.take()
            for c in range(CHUNKS):
                mm = pe(lambda e: e.transpose(bank[:, c * P:(c + 1) * P], src[:, c * P:(c + 1) * P], ident), m, free)
            return i, split(bank[:, 0:256], CHUNKS, P), mm

        i, bank, mm = turned(tmp, m)
        m = dve(lambda e: e.tensor_copy(oT, bank), mm)
        banks.give(i, m)
        i, bank, free = banks.take()
        for c in range(CHUNKS):
            mm = pe(lambda e: e.matmul(bank[:, 0:256], oT[:, c], w2("d_Wo")[:, c], start=c == 0, stop=c == 1), m, free, W["d_Wo"][1])
        m = dve(lambda e: e.tensor_tensor(o, bank[:, 0:256], S("d_bo"), ALU.add), mm)
        banks.give(i, m)
        for n in ("d_Wq", "d_WkT", "d_Wv", "d_Wo"):
            W[n][0].give(m)
        once.give(self.all_marks())
        o_ready = dve(lambda e: e.tensor_tensor(o, o, S("slot"), ALU.add), m)
        m = dve(lambda e: e.bn_stats(st[:, 0:6], o), o_ready)
        m = dve(lambda e: e.bn_aggr(st[:, 6:8], st[:, 0:6]), m)
        m = self.rsqrt(st[:, 8:9], st[:, 7:8], st[:, 9:10], 1, m)
        m = dve(lambda e: e.tensor_scalar(h, o, st[:, 6:7], st[:, 8:9], ALU.subtract, ALU.mult), m)
        m = dve(lambda e: e.tensor_tensor(h, h, S("e_lng"), ALU.mult), m)
        h_ready = dve(lambda e: e.tensor_tensor(h, h, S("e_lnb"), ALU.add), m)
        i, bank, mm = turned(o, o_ready)
        oT_ready = dve(lambda e: e.tensor_copy(oT, bank), mm)
        banks.give(i, oT_ready)
        padded = sp.take(CHUNKS * EXPERTS * 32)
        hT = split(padded.ap, CHUNKS, EXPERTS, 32)
        z = pool(lambda e: e.memset(padded.ap, 0.0), padded.before)
        i, bank, mm = turned(h, h_ready)
        for c in range(CHUNKS):
            hT_ready = dve(lambda e: e.tensor_copy(hT[:, c, :, 0:SEQS].rearrange("p e b -> p b e"), split(bank[:, c], SEQS, EXPERTS)), mm, z)
        banks.give(i, hT_ready)

        for q in range(4):
            load_bias(q)
            act_in = []
            for which, (m_name, b_name) in enumerate((("e_W1", "e_b1"), ("e_Wg", "e_bg"))):
                piece, b_ready = bias[b_name, q]
                done = []
                taken = [banks.take() for _ in range(2)]
                for n in range(2):
                    for k in range(CHUNKS):
                        for j in range(4):
                            w, w_ready = arrived[m_name, 4 * q + j]
                            mm = pe(lambda e: e.matmul(taken[n][1][32 * j:32 * j + 32], hT[:, k, 4 * q + j],
                                                       split(w, CHUNKS, HIDDEN)[:, k, n * 512:(n + 1) * 512],
                                                       start=k == 0, stop=k == 1, skip_group_check=True), taken[n][2], hT_ready, w_ready)
                for j in range(4):
                    load_next(mm)
                for n in range(2):
                    m = dve(lambda e: e.tensor_tensor(piece.ap[:, n * 512:(n + 1) * 512], taken[n][1], piece.ap[:, n * 512:(n + 1) * 512], ALU.add), mm, b_ready)
                    banks.give(taken[n][0], m)
                m = act(lambda e: e.activation(piece.ap, piece.ap, ACT.Silu), m)
                act_in.append((piece, m))
            (u, u_r), (g, g_r) = act_in
            m = dve(lambda e: e.tensor_tensor(u.ap, u.ap, g.ap, ALU.mult), u_r, g_r)
            hid = sp.take(HIDDEN)
            hidT = split(hid.ap, 8, P)
            for n in range(2):
                i, bank, free = banks.take()
                for f in range(4):
                    mm = pe(lambda e: e.transpose(bank[:, f * P:(f + 1) * P], u.ap[:, (4 * n + f) * P:(4 * n + f + 1) * P], ident), m, free)
                hm = act(lambda e: e.activation(hidT[:, 4 * n:4 * n + 4], split(bank, 4, P), ACT.Copy), mm, hid.before)
                banks.give(i, hm)
            u.give(hm)
            g.give(hm)
            i, bank, free = banks.take()
            for f in range(8):
                for j in range(4):
                    w, w_ready = arrived["e_W2", 4 * q + j]
                    mm = pe(lambda e: e.matmul(bank[32 * j:32 * j + 32, 0:256], hidT[:, f, 32 * j:32 * j + 32], split(w, 8, 256)[:, f],
                                               start=f == 0, stop=f == 7, skip_group_check=True), hm, free, w_ready)
            for j in range(4):
                load_next(mm)
            m = dve(lambda e: e.tensor_copy(tmp, bank[:, 0:256]), mm)
            banks.give(i, m)
            hid.give(mm)
            i, bank, mm = turned(tmp, m)
            for c in range(CHUNKS):
                out = split(oT[:, c], SEQS, SLOTS)[:, :, 4 * q:4 * q + 4]
                m = dve(lambda e: e.tensor_tensor(out, out, split(bank[:, c], 4, 32)[:, :, 0:SEQS].rearrange("p j b -> p b j"), ALU.add), mm, oT_ready)
            banks.give(i, m)
            oT_ready = m
        for n in range(RING):
            ring[n].give(mm, ring_dma[n].mark)
        padded.give(self.all_marks())
        for c in range(CHUNKS):
            out = split(oT[:, c], SEQS, SLOTS)
            m = dve(lambda e: e.tensor_tensor(out, out, repeated(split(S("e_b2T"), CHUNKS, SLOTS)[:, c], SEQS), ALU.add), oT_ready)
        oT_ready = m

        for n in ("c_WqT", "c_Wk", "c_Wv", "c_Wo"):
            W[n] = self.load(n, True)
        kv = sp.take(2 * 256 + 256)
        kvT = split(kv.ap[:, 0:512], 2, CHUNKS, P)
        bq_wide = split(kv.ap[:, 512:768], CHUNKS, P)
        for f in range(CHUNKS):
            bq_ready = pool(lambda e: e.tensor_copy(bq_wide[:, f], S("c_bq")[:, f:f + 1].to_broadcast([P, P])), kv.before)
        for n, (name, bias_name, scale) in enumerate((("c_Wk", "c_bk", 0.25), ("c_Wv", "c_bv", 1.0))):
            i, bank, free = banks.take()
            for f in range(CHUNKS):
                for c in range(CHUNKS):
                    mm = pe(lambda e: e.matmul(bank[:, f * P:(f + 1) * P], w2(name)[:, c, f * P:(f + 1) * P], oT[:, c], start=c == 0, stop=c == 1),
                            oT_ready, free, W[name][1])
            for f in range(CHUNKS):
                kv_ready = dve(lambda e: e.tensor_scalar(kvT[:, n, f], bank[:, f * P:(f + 1) * P], S(bias_name)[:, f:f + 1], scale, ALU.add, ALU.mult), mm, kv.before)
            banks.give(i, kv_ready)
        slots.give(self.all_marks())

        def tokens_attend(b):
            blocks_piece = sp.take(2 * 512)
            blk = split(blocks_piece.ap, 2, CHUNKS, H, SLOTS)
            both = sp.take(512 + 512 + 256)
            meet_b, vo = split(both.ap[:, 0:512], CHUNKS, 256), split(both.ap[:, 512:1024], 2, CH)
            shift = both.ap[:, 1024:1280]
            for n in range(2):
                for f in range(CHUNKS):
                    kb = split(kvT[:, n, f], SEQS, SLOTS)[:, b]
                    m = dve(lambda e: e.tensor_tensor(blk[:, n, f], repeated(kb, H), spread(head_of[:, f], [P, H, SLOTS]), ALU.mult),
                            kv_ready, blocks_piece.before)
            flat = blk.rearrange("p n f h s -> p n f (h s)")
            yield
            i, bank, free = banks.take()
            for c in range(CHUNKS):
                for f in range(CHUNKS):
                    mm = pe(lambda e: e.matmul(bank[:, c * 256:(c + 1) * 256], w2("c_WqT")[:, f, c * P:(c + 1) * P], flat[:, 0, f],
                                               start=f == 0, stop=f == 1), m, free, W["c_WqT"][1])
            r1 = act(lambda e: e.activation(both.ap[:, 0:512], bank, ACT.Copy), mm, both.before)
            banks.give(i, r1)
            i, bank, free = banks.take()
            for f in range(CHUNKS):
                mm = pe(lambda e: e.matmul(bank[:, 0:256], bq_wide[:, f], flat[:, 0, f], start=f == 0, stop=f == 1), m, free, bq_ready)
            r2 = act(lambda e: e.activation(shift, bank[:, 0:256], ACT.Copy), mm, both.before)
            banks.give(i, r2)
            i, bank, free = banks.take()
            for t in range(2):
                for f in range(CHUNKS):
                    mm = pe(lambda e: e.matmul(bank[:, t * 256:(t + 1) * 256], flat[:, 1, f, t * P:(t + 1) * P], w2("c_Wo")[:, f],
                                               start=f == 0, stop=f == 1), m, free, W["c_Wo"][1])
            r3 = act(lambda e: e.activation(both.ap[:, 512:1024], bank, ACT.Copy), mm, both.before)
            banks.give(i, r3)
            blocks_piece.give(mm)
            yield
            sums = []
            for pair in range(2):
                work = sp.take(512 + 96)
                s, s3 = work.ap[:, 0:512], split(work.ap[:, 0:512], 2 * H, SLOTS)
                mx, den, rden = (work.ap[:, 512 + 32 * n:544 + 32 * n] for n in range(3))
                i, bank, free = banks.take()
                for t in range(2):
                    for c in range(CHUNKS):
                        n = 2 * pair + t
                        mm = pe(lambda e: e.matmul(bank[:, t * 256:(t + 1) * 256], self.xT[:, b, c, 1 + n * P:1 + (n + 1) * P], meet_b[:, c],
                                                   start=c == 0, stop=c == 1), r1, free, self.xT_ready[b])
                m = dve(lambda e: e.tensor_tensor(split(s, 2, 256), split(bank, 2, 256), repeated(shift, 2), ALU.add), mm, r2, work.before)
                banks.give(i, m)
                yield
                m = dve(lambda e: e.tensor_reduce(mx, s3, AX.X, ALU.max), m)
                m = dve(lambda e: e.tensor_tensor(s3, s3, spread(mx, [P, 2 * H, SLOTS]), ALU.subtract), m)
                m = act(lambda e: e.activation(s, s, ACT.Exp), m)
                yield
                m = dve(lambda e: e.tensor_reduce(den, s3, AX.X, ALU.add), m)
                m = dve(lambda e: e.reciprocal(rden, den), m)
                m = pool(lambda e: e.tensor_tensor(s3, s3, spread(rden, [P, 2 * H, SLOTS]), ALU.mult), m)
                yield
                i, bank, free = banks.take()
                for n in range(4):
                    mm = pe(lambda e: e.transpose(bank[:, n * P:(n + 1) * P], s[:, n * P:(n + 1) * P], ident), m, free)
                turned_piece = sp.take(512)
                aT = split(turned_piece.ap, 2, 2, P)
                m = act(lambda e: e.activation(turned_piece.ap, bank, ACT.Copy), mm, turned_piece.before)
                banks.give(i, m)
                work.give(m)
                yield
                i, bank, free = banks.take()
                for t in range(2):
                    for n in range(2):
                        mm = pe(lambda e: e.matmul(bank[:, t * 256:(t + 1) * 256], aT[:, t, n], vo[:, n], start=n == 0, stop=n == 1), m, r3, free)
                turned_piece.give(mm)
                x = self.x_nat[:, b, 2 * pair:2 * pair + 2]
                m = dve(lambda e: e.tensor_tensor(x, x, split(bank, 2, 256), ALU.add), mm, o_bias[b])
                banks.give(i, m)
                sums += [m, m]
                yield
            both.give(m)
            yield from self.norm_and_turn(b, banks, sums)

        self.interleave([lambda b=b: tokens_attend(b) for b in range(SEQS)], 3, 3)
        marks = self.all_marks()
        kv.give(marks)
        for n in ("c_WqT", "c_Wk", "c_Wv", "c_Wo"):
            W[n][0].give(marks)


    def block3(self):
        sp, pe, act, dve, pool, S = self.space, self.pe, self.act, self.dve, self.pool, self.S
        banks = Banks(self.psum, range(8))
        H, HD = 8, 32
        W = {n: self.load(n, True) for n in ("r_WqT", "r_WkvT", "r_WoT", "decay_q", "decay_k")}
        wq, wo = split(W["r_WqT"][0].ap, CHUNKS, CH), split(W["r_WoT"][0].ap, CHUNKS, CH)
        wkv = split(W["r_WkvT"][0].ap, CHUNKS, 2 * CH)
        decay = [split(W[n][0].ap, CHUNKS, TOKENS) for n in ("decay_q", "decay_k")]
        decay_ready = [W["decay_q"][1], W["decay_k"][1]]
        decay_nat = split(S("decay_k_nat"), TILES, H)
        block_ones, causal = S("same_head32"), S("causal")

        def retain(b):
            rotated = sp.take(2 * CHUNKS * TOKENS)
            qk = split(rotated.ap, 2, CHUNKS, TOKENS)
            qk_ready = []
            for side in range(2):
                for g in range(CHUNKS):
                    w = wq if side == 0 else wkv
                    i, bank, free = banks.take()
                    for c in range(CHUNKS):
                        mm = pe(lambda e: e.matmul(bank, w[:, c, g * P:(g + 1) * P], self.xT[:, b, c, 1:], start=c == 0, stop=c == 1),
                                free, self.xT_ready[b], W["r_WqT"][1], W["r_WkvT"][1])
                    m = dve(lambda e: e.tensor_tensor(qk[:, side, g], bank, decay[side][:, g], ALU.mult), mm, decay_ready, rotated.before)
                    banks.give(i, m)
                    qk_ready.append(m)
                    yield
            nat = sp.take(2 * TILES * CH)
            kn, vn = split(nat.ap[:, 0:TILES * CH], TILES, CH), split(nat.ap[:, TILES * CH:], TILES, CH)
            nat_ready = []
            for t in range(TILES):
                i, bank, free = banks.take()
                for c in range(CHUNKS):
                    mm = pe(lambda e: e.matmul(bank, self.xT[:, b, c, 1 + t * P:1 + (t + 1) * P], wkv[:, c], start=c == 0, stop=c == 1), free)
                m = dve(lambda e: e.tensor_tensor(split(kn[:, t], H, HD), split(bank[:, 0:CH], H, HD),
                                                  spread(decay_nat[:, t], [P, H, HD]), ALU.mult), mm, nat.before)
                m2 = act(lambda e: e.activation(vn[:, t], bank[:, CH:], ACT.Copy), mm, m, nat.before)
                banks.give(i, m2)
                nat_ready += [m, m2]
                yield
            normed = sp.take(2 * TOKENS)
            yn = split(normed.ap, 2, TOKENS)
            for g in range(2):
                state = sp.take(3 * P)
                s3 = split(state.ap, 3, P)
                i, bank, free = banks.take()
                for t in range(3):
                    mm = pe(lambda e: e.matmul(bank[:, t * P:(t + 1) * P], kn[:, t, g * P:(g + 1) * P], vn[:, t, g * P:(g + 1) * P],
                                               start=True, stop=True), nat_ready, free)
                m = dve(lambda e: e.tensor_tensor(s3, split(bank[:, 0:3 * P], 3, P), repeated(block_ones, 3), ALU.mult), mm, state.before)
                banks.give(i, m)
                m = pool(lambda e: e.tensor_tensor(s3[:, 1], s3[:, 1], s3[:, 0], ALU.add), m)
                state_ready = pool(lambda e: e.tensor_tensor(s3[:, 2], s3[:, 2], s3[:, 1], ALU.add), m)
                own = sp.take(4 * TOKENS)
                a = split(own.ap, 4, TOKENS)
                own_ready = []
                four = [banks.take() for _ in range(4)]
                for t in range(TILES):
                    for j in range(4):
                        r = slice(32 * j, 32 * j + 32)
                        mm = pe(lambda e: e.matmul(four[j][1][:, t * P:(t + 1) * P], qk[r, 1, g, t * P:(t + 1) * P], qk[r, 0, g, t * P:(t + 1) * P],
                                                   start=True, stop=True), qk_ready, four[j][2])
                for j in range(4):
                    m = dve(lambda e: e.tensor_tensor(split(a[:, j], TILES, P), split(four[j][1], TILES, P), repeated(causal, TILES), ALU.mult), mm, own.before)
                    banks.give(four[j][0], m)
                    own_ready.append(m)
                yield
                i, bank, free = banks.take()
                for t in range(TILES):
                    cols = slice(t * P, (t + 1) * P)
                    if t:
                        pe(lambda e: e.matmul(bank[:, cols], s3[:, t - 1], qk[:, 0, g, cols], start=True, stop=False, skip_group_check=True),
                           state_ready, free)
                    for j in range(4):
                        mm = pe(lambda e: e.matmul(bank[32 * j:32 * j + 32, cols], vn[:, t, g * P + 32 * j:g * P + 32 * j + 32], a[:, j, cols],
                                                   start=t == 0, stop=True, skip_group_check=True), own_ready, free)
                own.give(mm)
                state.give(mm)
                stats = sp.take(24)
                st = stats.ap
                m = dve(lambda e: e.bn_stats(st[:, 0:6], bank), mm, stats.before)
                m = dve(lambda e: e.bn_aggr(st[:, 6:8], st[:, 0:6]), m)
                m = dve(lambda e: e.scalar_tensor_tensor(st[:, 7:8], st[:, 6:7], st[:, 6:7], st[:, 7:8], ALU.mult, ALU.add), m)
                i2, bank2, free2 = banks.take()
                mm2 = pe(lambda e: e.matmul(bank2[:, 0:2], block_ones, st[:, 6:8], start=True, stop=True), m, free2)
                m = dve(lambda e: e.tensor_scalar(st[:, 8:10], bank2[:, 0:2], 1.0 / HD, None, ALU.mult), mm2)
                banks.give(i2, m)
                m = dve(lambda e: e.tensor_tensor(st[:, 10:11], st[:, 8:9], st[:, 8:9], ALU.mult), m)
                m = dve(lambda e: e.tensor_tensor(st[:, 11:12], st[:, 9:10], st[:, 10:11], ALU.subtract), m)
                m = self.rsqrt(st[:, 12:13], st[:, 11:12], st[:, 13:14], 1, m)
                yield
                m = dve(lambda e: e.tensor_tensor(st[:, 14:15], st[:, 12:13], S("r_gw")[:, g:g + 1], ALU.mult), m)
                m = dve(lambda e: e.tensor_tensor(st[:, 15:16], st[:, 8:9], st[:, 14:15], ALU.mult), m)
                m = dve(lambda e: e.tensor_tensor(st[:, 16:17], S("r_gb")[:, g:g + 1], st[:, 15:16], ALU.subtract), m)
                m = dve(lambda e: e.tensor_scalar(yn[:, g], bank, st[:, 14:15], st[:, 16:17], ALU.mult, ALU.add), m, normed.before)
                banks.give(i, m)
                stats.give(m)
                yield
            nat.give(mm)
            rotated.give(mm)
            sums = []
            for pair in range(2):
                i, bank, free = banks.take()
                for t in range(2):
                    n = 2 * pair + t
                    for g in range(2):
                        mm = pe(lambda e: e.matmul(bank[:, t * CH:(t + 1) * CH], yn[:, g, n * P:(n + 1) * P], wo[:, g], start=g == 0, stop=g == 1),
                                m, free, W["r_WoT"][1])
                x = self.x_nat[:, b, 2 * pair:2 * pair + 2]
                s = dve(lambda e: e.tensor_tensor(x, x, split(bank, 2, CH), ALU.add), mm, self.x_ready[b])
                banks.give(i, s)
                sums += [s, s]
                yield
            normed.give(mm)
            yield from self.norm_and_turn(b, banks, sums)

        self.interleave([lambda b=b: retain(b) for b in range(SEQS)], 2, 6)
        for n in W:
            W[n][0].give(self.all_marks())


    def turn(self, b, banks, m):
        copied = []
        for c in range(CHUNKS):
            i, bank, free = banks.take()
            for t in range(TILES):
                put = self.pe(lambda e: e.transpose(bank[:, t * P:(t + 1) * P], self.x_nat[:, b, t, c * P:(c + 1) * P], self.S("identity")), m, free)
            out = self.xT[:, b, c, 1:]
            if c:
                copied.append(self.act(lambda e: e.activation(out, bank, ACT.Copy), put, self.xT_read[b]))
            else:
                copied.append(self.dve(lambda e: e.tensor_copy(out, bank), put, self.xT_read[b]))
            banks.give(i, copied[-1])
            yield
        self.xT_ready[b] = copied
        self.xT_read[b] = []

    def block4(self):
        sp, pe, act, dve, pool, S = self.space, self.pe, self.act, self.dve, self.pool, self.S
        banks = Banks(self.psum, range(8))
        LAYERS, H, HD, HID_TILES = 2, 8, 64, 6
        ident = S("identity")
        xT = self.xT
        kept_x = self.nc.dram_tensor("kept_x", (SEQS, P, TILES * CH), F32).ap()
        kept_dma = [Transfers(self.sem(f"kept{b}")) for b in range(SEQS)]
        for b in range(SEQS):
            kept_dma[b].start(self.sp, kept_x[b], self.x_nat[:, b].rearrange("p t c -> p (t c)"), self.x_ready[b])
            self.x_ready[b] = [self.x_ready[b], kept_dma[b].mark]

        def attention(l, b, W, rot):
            wqkv, wo = split(W["w_qkv"][0].ap, CHUNKS, 3, H * HD), split(W["w_o"][0].ap, TILES, CH)
            cos, sin, rot_ready = rot
            kept = sp.take(2 * TILES * H * HD)
            kT, vn = split(kept.ap[:, 0:2048], 4, TOKENS), split(kept.ap[:, 2048:], TILES, H * HD)
            sums = []
            kv_ready = []
            for t in range(TILES):
                work = sp.take(2 * 1024 + 32)
                a1, a2 = split(work.ap[:, 0:1024], 2, H, HD), split(work.ap[:, 1024:2048], 2, H, HD)
                ss, rn = work.ap[:, 2048:2064], work.ap[:, 2064:2080]
                got = []
                for side in range(3):
                    i, bank, free = banks.take()
                    for c in range(CHUNKS):
                        at = 1 - c + t * P
                        mm = pe(lambda e: e.matmul(bank, xT[:, b, c, at:at + P], wqkv[:, c, side], start=c == 0, stop=c == 1),
                                free, self.xT_ready[b], W["w_qkv"][1])
                    if side == 2:
                        m = act(lambda e: e.activation(vn[:, t], bank, ACT.Copy), mm, kept.before)
                        banks.give(i, m)
                        kv_ready.append(m)
                        break
                    b3 = split(bank, H, HD)
                    m = act(lambda e: e.activation(a2[:, side], b3, ACT.Square), mm, work.before)
                    m = dve(lambda e: e.tensor_reduce(split(ss, 2, H)[:, side], a2[:, side], AX.X, ALU.add), m)
                    m = dve(lambda e: e.tensor_tensor(a1[:, side], b3, repeated(cos[:, t, side], H), ALU.mult), mm, rot_ready, work.before)
                    for half in range(2):
                        lo, hi = slice(32 * half, 32 * half + 32), slice(32 - 32 * half, 64 - 32 * half)
                        m = dve(lambda e: e.tensor_tensor(a2[:, side, :, lo], b3[:, :, hi], repeated(sin[:, t, side, lo], H), ALU.mult), m)
                    banks.give(i, m)
                    got.append(m)
                    yield
                m2 = pool(lambda e: e.tensor_scalar(ss, ss, 1e-24, None, ALU.max), got)
                m2 = pool(lambda e: e.tensor_tensor(rn, ss, self.half.ap[:, 0:16], ALU.pow), m2)
                m = pool(lambda e: e.tensor_tensor(work.ap[:, 0:1024], work.ap[:, 0:1024], work.ap[:, 1024:2048], ALU.add), got)
                m = pool(lambda e: e.tensor_tensor(split(work.ap[:, 0:1024], 16, HD), split(work.ap[:, 0:1024], 16, HD), spread(rn, [P, 16, HD]), ALU.mult), m, m2)
                yield
                q_piece = sp.take(512)
                qT = split(q_piece.ap, 4, P)
                for side in range(2):
                    i, bank, free = banks.take()
                    for pair in range(4):
                        mm = pe(lambda e: e.transpose(bank[:, pair * P:(pair + 1) * P], work.ap[:, side * 512 + pair * P:side * 512 + (pair + 1) * P], ident), m, free)
                    if side == 0:
                        q_ready = act(lambda e: e.activation(qT, split(bank, 4, P), ACT.Copy), mm, q_piece.before)
                        banks.give(i, q_ready)
                    else:
                        k_ready = act(lambda e: e.activation(kT[:, :, t * P:(t + 1) * P], split(bank, 4, P), ACT.Copy), mm, kept.before)
                        banks.give(i, k_ready)
                work.give(mm)
                yield
                first = 0 if t == 0 else -P
                n_keys = P - first
                probs = sp.take(H * 2 * P + 32)
                pr = split(probs.ap[:, 0:H * 2 * P], H, 2 * P)
                mx, den, rden = (probs.ap[:, H * 2 * P + 8 * n:H * 2 * P + 8 * n + 8] for n in range(3))
                for h in range(H):
                    r = slice(64 * (h % 2), 64 * (h % 2) + 64)
                    i, bank, free = banks.take()
                    mm = pe(lambda e: e.matmul(bank[:, 0:n_keys], qT[r, h // 2], kT[r, h // 2, t * P + first:(t + 1) * P], start=True, stop=True),
                            q_ready, k_ready, free)
                    m = dve(lambda e: e.tensor_tensor_reduce(out=pr[:, h, 2 * P - n_keys:], in0=bank[:, 0:n_keys], in1=S("window_mask")[:, 2 * P - n_keys:],
                                                             scale=1.0, scalar=-3.4e38, op0=ALU.add, op1=ALU.max, accum_out=mx[:, h:h + 1]), mm, probs.before)
                    banks.give(i, m)
                    if h == 3:
                        yield
                q_piece.give(mm)
                m = dve(lambda e: e.tensor_scalar(mx, mx, -1.0, None, ALU.mult), m)
                yield
                normal = []
                for h in range(H):
                    cols = pr[:, h, 2 * P - n_keys:]
                    m2 = act(lambda e: e.activation(cols, cols, ACT.Exp, bias=mx[:, h:h + 1], accum_out=den[:, h:h + 1]), m)
                    if h % 4 == 3:
                        q4 = slice(h - 3, h + 1)
                        m3 = dve(lambda e: e.reciprocal(rden[:, q4], den[:, q4]), m2)
                        for hh in range(h - 3, h + 1):
                            c2 = pr[:, hh, 2 * P - n_keys:]
                            normal.append(dve(lambda e: e.tensor_scalar(c2, c2, rden[:, hh:hh + 1], None, ALU.mult), m3))
                        yield
                io, obank, ofree = banks.take()
                turned = []
                for pair in range(4):
                    i, bank, free = banks.take()
                    b4 = split(bank, 2, 2, P)
                    for hh in range(2):
                        for n in range(0 if t else 1, 2):
                            mm = pe(lambda e: e.transpose(b4[:, hh, n], pr[:, 2 * pair + hh, n * P:(n + 1) * P], ident), normal[2 * pair + hh], free)
                    piece = sp.take(512)
                    pT = split(piece.ap, 2, 2, P)
                    src, dst = (b4, pT) if t else (b4[:, :, 1], pT[:, :, 1])
                    if pair % 2:
                        m = act(lambda e: e.activation(dst, src, ACT.Copy), mm, piece.before)
                    else:
                        m = dve(lambda e: e.tensor_copy(dst, src), mm, piece.before)
                    banks.give(i, m)
                    turned.append((piece, pT, m))
                probs.give(mm)
                for pair in range(4):
                    piece, pT, m = turned[pair]
                    for n in range(0 if t else 1, 2):
                        for hh in range(2):
                            h = 2 * pair + hh
                            mm = pe(lambda e: e.matmul(obank[64 * hh:64 * hh + 64, pair * P:(pair + 1) * P], vn[:, t - 1 + n, h * HD:(h + 1) * HD], pT[:, hh, n],
                                                       start=n == (0 if t else 1), stop=n == 1, skip_group_check=True), m, ofree, kv_ready)
                    piece.give(mm)
                o_piece = sp.take(512)
                m = act(lambda e: e.activation(o_piece.ap, obank, ACT.Copy), mm, o_piece.before)
                banks.give(io, m)
                yield
                i, bank, free = banks.take()
                for pair in range(4):
                    mm = pe(lambda e: e.matmul(bank[:, 0:CH], o_piece.ap[:, pair * P:(pair + 1) * P], wo[:, pair], start=pair == 0, stop=pair == 3), m, free, W["w_o"][1])
                o_piece.give(mm)
                x = self.x_nat[:, b, t]
                s = dve(lambda e: e.tensor_tensor(x, x, bank[:, 0:CH], ALU.add), mm, self.x_ready[b])
                banks.give(i, s)
                sums.append(s)
                yield
            kept.give(mm, s)
            self.x_ready[b] = sums

        def mlp(l, b, W):
            w1, w2 = split(W["w_1"][0].ap, CHUNKS, 2, HID_TILES, P), split(W["w_2"][0].ap, HID_TILES, CH)
            b1 = split(S(f"b_1{l}"), 2, HID_TILES)
            yield from self.turn(b, banks, self.x_ready[b])
            piece = sp.take(TILES * CH + 64)
            hn = split(piece.ap[:, 0:TILES * CH], TILES, CH)
            st = piece.ap[:, TILES * CH:]
            stats, mv, rstd, scratch = split(st[:, 0:48], TILES, 2, 6), split(st[:, 48:56], TILES, 2), st[:, 56:60], st[:, 60:64]
            i, bank, free = banks.take()
            shifted = split(bank, TILES, P)
            for t in range(TILES):
                mm = pe(lambda e: e.transpose(shifted[:, t], xT[:, b, 1, t * P:(t + 1) * P], ident), self.xT_ready[b], free)
            for t in range(TILES):
                m1 = dve(lambda e: e.bn_stats(stats[:, t, 0], self.x_nat[:, b, t, 0:P]), self.x_ready[b], piece.before)
                m2 = dve(lambda e: e.bn_stats(stats[:, t, 1], shifted[:, t]), mm, piece.before)
                m = dve(lambda e: e.bn_aggr(mv[:, t], stats[:, t].rearrange("p a b -> p (a b)")), m1, m2)
            m = self.rsqrt(rstd, mv[:, :, 1], scratch, TILES, m)
            yield
            done = []
            for t in range(TILES):
                m1 = dve(lambda e: e.tensor_scalar(hn[:, t, 0:P], self.x_nat[:, b, t, 0:P], mv[:, t, 0:1], rstd[:, t:t + 1], ALU.subtract, ALU.mult), m)
                m2 = dve(lambda e: e.tensor_scalar(hn[:, t, P:], shifted[:, t], mv[:, t, 0:1], rstd[:, t:t + 1], ALU.subtract, ALU.mult), m)
                done.append(m2)
            banks.give(i, m2)
            biased = pool(lambda e: e.tensor_tensor(self.x_nat[:, b], self.x_nat[:, b], repeated(S(f"b_2{l}"), TILES), ALU.add), m2)
            yield
            turned = sp.take(CHUNKS * TOKENS)
            hT = split(turned.ap, CHUNKS, TOKENS)
            h_ready = []
            for c in range(CHUNKS):
                i, bank, free = banks.take()
                for t in range(TILES):
                    mm = pe(lambda e: e.transpose(bank[:, t * P:(t + 1) * P], hn[:, t, c * P:(c + 1) * P], ident), done, free)
                g, bb = S(f"l_g{l}")[:, c:c + 1], S(f"l_b{l}")[:, c:c + 1]
                if c:
                    h_ready.append(act(lambda e: e.activation(hT[:, c], bank, ACT.Identity, bias=bb, scale=g), mm, turned.before))
                else:
                    h_ready.append(dve(lambda e: e.tensor_scalar(hT[:, c], bank, g, bb, ALU.mult, ALU.add), mm, turned.before))
                banks.give(i, h_ready[-1])
            piece.give(mm)
            yield
            hidden = []
            for n in range(HID_TILES):
                out = sp.take(TOKENS)
                ig, gate, gfree = banks.take()
                for c in range(CHUNKS):
                    mm = pe(lambda e: e.matmul(gate, w1[:, c, 1, n], hT[:, c], start=c == 0, stop=c == 1), h_ready, gfree, W["w_1"][1])
                m = act(lambda e: e.activation(out.ap, gate, ACT.Gelu, bias=b1[:, 1, n:n + 1]), mm, out.before)
                banks.give(ig, m)
                ia, lin, afree = banks.take()
                for c in range(CHUNKS):
                    mm = pe(lambda e: e.matmul(lin, w1[:, c, 0, n], hT[:, c], start=c == 0, stop=c == 1), h_ready, afree)
                m = dve(lambda e: e.scalar_tensor_tensor(out.ap, lin, b1[:, 0, n:n + 1], out.ap, ALU.add, ALU.mult), mm, m)
                banks.give(ia, m)
                hidden.append((out, m))
                yield
            turned.give(mm)
            sums = []
            for pair in range(2):
                i, bank, free = banks.take()
                for t in range(2):
                    n = 2 * pair + t
                    for k in range(HID_TILES):
                        mm = pe(lambda e: e.matmul(bank[:, t * CH:(t + 1) * CH], hidden[k][0].ap[:, n * P:(n + 1) * P], w2[:, k],
                                                   start=k == 0, stop=k == HID_TILES - 1), hidden[k][1], free, W["w_2"][1])
                x = self.x_nat[:, b, 2 * pair:2 * pair + 2]
                s = dve(lambda e: e.tensor_tensor(x, x, split(bank, 2, CH), ALU.add), mm, biased)
                banks.give(i, s)
                sums += [s, s]
                yield
            for out, _ in hidden:
                out.give(mm)
            self.x_ready[b] = sums
            if l == LAYERS - 1:
                again = sp.take(TILES * CH)
                kept_dma[b].start(self.sp, again.ap, kept_x[b], again.before)
                sums = [dve(lambda e: e.tensor_tensor(self.x_nat[:, b], self.x_nat[:, b], split(again.ap, TILES, CH), ALU.add),
                            sums, kept_dma[b].mark)] * TILES
                again.give(sums[0])
                yield from self.norm_and_turn(b, banks, sums, turn=False)
            else:
                yield from self.turn(b, banks, sums)

        for l in range(LAYERS):
            W = {n: self.load(f"{n}{l}", True) for n in ("w_qkv", "w_o", "w_1", "w_2")}
            tables = sp.take(2 * TILES * 2 * HD, True)
            cos, sin = split(tables.ap[:, 0:512], TILES, 2, HD), split(tables.ap[:, 512:], TILES, 2, HD)
            m1 = dve(lambda e: e.tensor_tensor(split(tables.ap[:, 0:512], TILES, 2 * HD), split(S("rot_cos"), TILES, 2 * HD), repeated(S(f"s_qk{l}"), TILES), ALU.mult), tables.before)
            m2 = dve(lambda e: e.tensor_tensor(split(tables.ap[:, 512:], TILES, 2 * HD), split(S("rot_sin"), TILES, 2 * HD), repeated(S(f"s_kq{l}"), TILES), ALU.mult), tables.before)

            def layer(b, l=l, W=W, rot=(cos, sin, [m1, m2])):
                yield from attention(l, b, W, rot)
                yield from mlp(l, b, W)

            self.interleave([lambda b=b: layer(b) for b in range(SEQS)], 2, 20)
            marks = self.all_marks()
            tables.give(marks)
            for n in W:
                W[n][0].give(marks)

def _chunked(w):
    K, N = w.shape
    return w.reshape(K // 128, 128, N).transpose(1, 0, 2).reshape(128, -1)


def _padded(w, shape):
    import numpy as np
    out = np.zeros(shape, w.dtype)
    out[tuple(slice(0, n) for n in w.shape)] = w
    return out


def _constants():
    import numpy as np
    f4 = np.float32
    p = np.arange(128)
    out = {}
    out["identity"] = np.eye(128, dtype=f4)
    out["same_head32"] = (p[:, None] // 32 == p[None, :] // 32).astype(f4)
    out["causal"] = (p[:, None] <= p[None, :]).astype(f4)
    out["ones5"] = _padded(np.ones((5, 1), f4), (32, 1)).repeat(1, 1)
    out["ones5"] = np.concatenate([np.zeros((96, 1), f4), out["ones5"]])
    out["head_of"] = np.stack([((c * 128 + p)[:, None] // 16 == np.arange(16)[None, :]) for c in (0, 1)], 1).astype(f4).reshape(128, 32)
    out["spread16"] = _padded(np.stack([np.eye(128, dtype=f4)[32 * j:32 * j + 16] for j in range(4)], 1).reshape(16, 512), (128, 512))
    g = (1.0 - np.exp(np.linspace(np.log(1.0 / 32.0), np.log(1.0 / 512.0), 8))).astype(f4).astype(np.float64)
    t = np.arange(512)
    rows = np.stack([g[(c * 128 + p) // 32] for c in (0, 1)], 1)
    out["decay_q"] = (rows[:, :, None] ** (t - 256)[None, None, :]).astype(f4).reshape(128, -1)
    out["decay_k"] = (rows[:, :, None] ** (256 - t)[None, None, :]).astype(f4).reshape(128, -1)
    tn = np.arange(4)[None, :] * 128 + p[:, None]
    out["decay_k_nat"] = (g[None, None, :] ** (256 - tn)[:, :, None]).astype(f4).reshape(128, -1)
    half = np.arange(0, 64, 2, dtype=f4)
    inv = (f4(1.0) / f4(10000.0) ** (half / f4(64))).astype(f4)
    tt = np.arange(512, dtype=f4)
    fr = (tt[:, None] * inv[None, :]).astype(f4)
    fr = np.concatenate([fr, fr], -1)
    base = ((half + f4(0.4 * 64)) / f4(1.4 * 64)).astype(f4)
    power = ((tt - f4(256)) / f4(64.0)).astype(f4)
    sc = (base[None, :] ** power[:, None]).astype(f4)
    sc = np.concatenate([sc, sc], -1)
    cos, sin = np.cos(fr), np.sin(fr)
    sin = sin * np.where(np.arange(64) < 32, -1, 1).astype(f4)
    tab = lambda a: np.stack([a * sc * f4(8.0), a / sc], 1).reshape(4, 128, 2, 64).transpose(1, 0, 2, 3).reshape(128, -1).astype(f4)
    out["rot_cos"], out["rot_sin"] = tab(cos), tab(sin)
    i, j = p[:, None], p[None, :]
    big = f4(-3.0e38)
    out["window_mask"] = np.concatenate([np.where(i > j, big, f4(0)), np.where(i < j, big, f4(0))], 1).astype(f4)
    return out


def _layouts(inp):
    import numpy as np
    I = {k: np.asarray(v) for k, v in inp.items()}
    A = {k[8:]: v for k, v in I.items() if k.startswith("L0_attn_")}
    D = {k[7:]: v for k, v in I.items() if k.startswith("L0_ffn_")}
    R = {k[8:]: v for k, v in I.items() if k.startswith("L1_attn_")}
    L = {k[7:]: v for k, v in I.items() if k.startswith("L1_ffn_")}
    p = np.arange(128)
    bc = lambda v: np.broadcast_to(v.reshape(1, -1), (128, v.size))
    col2 = lambda v: v.reshape(2, 128).T
    rows = lambda a: _padded(a, (128,) + a.shape[1:]).reshape(128, -1)
    big, small = {}, {}

    big["x"] = A["x"]
    big["xT"] = A["x"].reshape(8, 512, 2, 128).transpose(3, 0, 2, 1).reshape(128, -1)
    W = A["Wqkv"]
    big["a_wqkv"] = _chunked(W)
    big["a_wqk"] = _chunked(W[:, 0:512].reshape(256, 2, 16, 16).transpose(0, 2, 1, 3).reshape(256, 512))
    big["a_wproj"] = _padded(A["Wproj"].reshape(4, 4, 16, 256), (4, 4, 32, 256)).transpose(1, 2, 0, 3).reshape(128, -1)
    small["a_alpha"] = np.stack([A["alpha"][8 * c + p // 16] for c in (0, 1)], 1)
    small["a_beta"] = bc(A["beta"])
    small["a_gamma"] = np.stack([A["gamma"][4 * g + p // 32] for g in range(4)], 1)
    small["a_bproj"] = bc(A["bproj"])
    bd = lambda w, r: _padded(np.stack([_padded(w[t], (r, w.shape[2])) for t in range(4)]), (4, r, w.shape[2]))
    def block_diag(w, r, c):
        out = np.zeros((4 * r, 4 * c), w.dtype)
        for t in range(4):
            out[r * t:r * t + w.shape[1], c * t:c * t + w.shape[2]] = w[t]
        return out
    small["a_A"] = rows(A["A"].transpose(1, 0, 2).reshape(32, 128))
    small["a_phi1"] = rows(_padded(A["Wphi1"].transpose(1, 0, 2), (32, 4, 32)).reshape(32, 128))
    small["a_bphi1"] = _padded(A["bphi1"], (4, 32)).reshape(128, 1)
    small["a_phi2"] = block_diag(A["Wphi2"], 32, 4)
    small["a_bphi2"] = rows(A["bphi2"].reshape(16, 1))
    small["a_psi1"] = block_diag(A["Wpsi1"], 32, 32)
    small["a_bpsi1"] = A["bpsi1"].reshape(128, 1)
    small["a_lng"] = A["ln_g"].reshape(128, 1)
    small["a_lnb"] = A["ln_b"].reshape(128, 1)
    small["a_psi2"] = block_diag(A["Wpsi2"], 32, 4)
    small["a_bpsi2"] = rows(A["bpsi2"].reshape(16, 1))
    small["a_mix"] = rows(np.repeat(A["mixing"], 4).reshape(16, 1))
    small["a_temp"] = rows(np.broadcast_to(A["temp_scale"], (16, 1)))

    for n in ("d_Wq", "d_Wv", "d_Wo", "c_Wk", "c_Wv", "c_Wo"):
        big[n] = _chunked(D[n])
    big["d_WkT"] = _chunked(D["d_Wk"].T)
    big["c_WqT"] = _chunked(D["c_Wq"].T)
    for n in ("d_bq", "d_bk", "c_bq", "c_bk", "c_bv"):
        small[n] = col2(D[n])
    for n in ("d_bv", "d_bo", "c_bo"):
        small[n] = bc(D[n])
    small["slot"] = np.tile(D["slot_query"][0], (8, 1))
    small["slotT"] = _chunked(D["slot_query"][0].T)
    small["e_lng"] = np.tile(D["e_ln_g"], (8, 1))
    small["e_lnb"] = np.tile(D["e_ln_b"], (8, 1))
    big["e_b1"] = np.repeat(D["e_b1"].reshape(4, 4, 1, 1024), 32, 2).reshape(4, 128, 1024)
    big["e_bg"] = np.repeat(D["e_bg"].reshape(4, 4, 1, 1024), 32, 2).reshape(4, 128, 1024)
    small["e_b2T"] = _chunked(D["e_b2"].T)
    for n in ("e_W1", "e_Wg", "e_W2"):
        big[n] = np.stack([_chunked(w) for w in D[n]])

    big["r_WqT"], big["r_WoT"] = _chunked(R["Wq"].T), _chunked(R["Wo"].T)
    big["r_WkvT"] = _chunked(np.concatenate([R["Wk"].T, R["Wv"].T], 1))
    small["r_gw"] = col2(R["gn_weight"])
    small["r_gb"] = col2(R["gn_bias"])

    for l in range(2):
        big[f"w_qkv{l}"] = _chunked(L["wqkv"][l])
        big[f"w_o{l}"] = _chunked(L["wo"][l])
        w1 = L["w1"][l].reshape(256, 2, 682)
        big[f"w_1{l}"] = _chunked(_padded(w1, (256, 2, 768)).reshape(256, 1536))
        small[f"b_1{l}"] = _padded(L["b1"][l].reshape(2, 682), (2, 768)).reshape(12, 128).T
        big[f"w_2{l}"] = _chunked(_padded(L["w2"][l], (768, 256)))
        small[f"b_2{l}"] = bc(L["b2"][l])
        small[f"l_g{l}"] = col2(L["ln_g"][l])
        small[f"l_b{l}"] = col2(L["ln_b"][l])
        qk = np.stack([L["q_scale"][l], L["k_scale"][l]])
        small[f"s_qk{l}"] = bc(qk)
        small[f"s_kq{l}"] = bc(np.concatenate([qk[:, 32:], qk[:, :32]], 1))
    for n, a in _constants().items():
        (big if n in ("decay_q", "decay_k") else small)[n] = a
    at, cols = {}, 0
    for n, a in small.items():
        a = np.ascontiguousarray(a, np.float32).reshape(128, -1)
        small[n] = a
        at[n] = (cols, a.shape[1])
        cols += a.shape[1]
    big["small"] = np.concatenate([small[n] for n in small], 1)
    return {n: np.ascontiguousarray(a, np.float32) for n, a in big.items()}, at


def kernel(**inputs):
    import concourse.bacc as bacc
    from concourse.bass_utils import run_bass_kernel_spmd

    arrays, small_at = _layouts(inputs)
    nc = bacc.Bacc("TRN2", target_bir_lowering=False, num_devices=1)
    dram = {n: nc.dram_tensor(f"in_{n}", a.shape, mybir.dt.float32, kind="ExternalInput").ap() for n, a in arrays.items()}
    out = nc.dram_tensor("out_x", (8, 512, 256), mybir.dt.float32, kind="ExternalOutput").ap()
    Program(nc, dram, small_at, out).build()
    r = run_bass_kernel_spmd(nc, [{f"in_{n}": a for n, a in arrays.items()}], core_ids=[0])
    return r.results[0]["out_x"]
```

```python
import concourse.bass as bass
from concourse import mybir

F32 = mybir.dt.float32
BF16 = mybir.dt.bfloat16
ACT = mybir.ActivationFunctionType
ALU = mybir.AluOpType
AX = mybir.AxisListType

P = 128
SEQS, TOKENS, CH = 8, 512, 256
TILES = TOKENS // P
CHUNKS = CH // P
EPS = 1e-5


class Later:

    activation = lambda self, *a, **k: lambda e: e.activation(*a, **k)
    bn_aggr = lambda self, *a, **k: lambda e: e.bn_aggr(*a, **k)
    bn_stats = lambda self, *a, **k: lambda e: e.bn_stats(*a, **k)
    matmul = lambda self, *a, **k: lambda e: e.matmul(*a, **k)
    memset = lambda self, *a, **k: lambda e: e.memset(*a, **k)
    reciprocal = lambda self, *a, **k: lambda e: e.reciprocal(*a, **k)
    scalar_tensor_tensor = lambda self, *a, **k: lambda e: e.scalar_tensor_tensor(*a, **k)
    stream_shuffle = lambda self, *a, **k: lambda e: e.stream_shuffle(*a, **k)
    tensor_copy = lambda self, *a, **k: lambda e: e.tensor_copy(*a, **k)
    tensor_reduce = lambda self, *a, **k: lambda e: e.tensor_reduce(*a, **k)
    tensor_scalar = lambda self, *a, **k: lambda e: e.tensor_scalar(*a, **k)
    tensor_tensor = lambda self, *a, **k: lambda e: e.tensor_tensor(*a, **k)
    tensor_tensor_reduce = lambda self, *a, **k: lambda e: e.tensor_tensor_reduce(*a, **k)
    transpose = lambda self, *a, **k: lambda e: e.transpose(*a, **k)


class Queue:

    def __init__(self, sem):
        self.sem, self.count, self.steps, self.seen = sem, 0, [], {}

    def wait(self, marks):
        for m in marks:
            if m is None:
                continue
            if isinstance(m, list):
                self.wait(m)
                continue
            sem, value = m
            if self.seen.get(id(sem), 0) < value:
                self.seen[id(sem)] = value
                self.steps.append(("wait", sem, value))

    def __call__(self, issue, *marks):
        self.wait(marks)
        self.count += 1
        self.steps.append(("run", issue(Later()), self.sem, 1))
        return (self.sem, self.count)

    def quiet(self, issue, *marks):
        self.wait(marks)
        self.steps.append(("run", issue(Later()), None, 0))

    def emit(self, engine):
        for kind, a, b, *c in self.steps:
            if kind == "wait":
                engine.wait_ge(a, b)
            else:
                instruction = a(engine)
                if b is not None:
                    instruction.then_inc(b, c[0])


class Transfers:

    def __init__(self, sem):
        self.sem, self.count = sem, 0

    def start(self, queue, out, in_, *marks):
        queue.wait(marks)
        self.count += 16
        queue.steps.append(("run", lambda e: e.dma_start(out, in_), self.sem, 16))

    @property
    def mark(self):
        return (self.sem, self.count)


class Banks:

    def __init__(self, psum, ids):
        self.psum, self.free = psum, [(i, None) for i in ids]

    def take(self):
        i, mark = self.free.pop(0)
        return i, self.psum[:, i, :], mark

    def give(self, i, mark):
        self.free.append((i, mark))


class Space:

    PAGE = 32

    def __init__(self, arena, columns):
        self.arena = arena
        self.used = [False] * (columns // self.PAGE)
        self.marks = [[] for _ in self.used]
        self.given, self.gifts, self.rested = [0] * len(self.used), 0, False

    def take(self, columns, top=False):
        n = -(-columns // self.PAGE)
        spots = range(len(self.used) - n + 1)
        best = None
        for at in (reversed(spots) if top else spots):
            if self.used[at] or self.used[at + n - 1] or any(self.used[at:at + n]):
                continue
            if top or not self.rested:
                best = at
                break
            if best is None or self.given[at] != self.given[at - 1] or self.used[at - 1]:
                latest = max(self.given[at:at + n])
                if best is None or latest < best_latest:
                    best, best_latest = at, latest
        if best is None:
            raise RuntimeError(f"no {columns} columns free; {self.used.count(False) * self.PAGE} in pieces")
        at = best
        self.used[at:at + n] = [True] * n
        before = {}
        for page in self.marks[at:at + n]:
            for sem, value in page:
                before[id(sem)] = max(before.get(id(sem), (0, 0, sem))[0], value), 0, sem
        before = [(sem, value) for value, _, sem in before.values()]
        for page in range(at, at + n):
            self.marks[page] = []
        return Piece(self, at, n, self.arena[:, at * self.PAGE:at * self.PAGE + columns], before)


class Piece:
    def __init__(self, space, at, pages, ap, before):
        self.space, self.at, self.pages, self.ap, self.before = space, at, pages, ap, before

    def give(self, *marks):
        flat = []
        for m in marks:
            flat += m if isinstance(m, list) else [m]
        flat = [m for m in flat if m is not None]
        self.space.gifts += 1
        for page in range(self.at, self.at + self.pages):
            self.space.used[page] = False
            self.space.given[page] = self.space.gifts
            self.space.marks[page] = list(flat)


def split(ap, *sizes):
    names = "abcd"[:len(sizes)]
    return ap.rearrange(f"p ({' '.join(names)}) -> p {' '.join(names)}", **dict(zip(names, sizes)))


def spread(ap, shape):
    while len(ap.shape) < len(shape):
        ap = ap.unsqueeze(len(ap.shape))
    return ap.to_broadcast(list(shape))


def repeated(ap, count):
    return ap.unsqueeze(1).to_broadcast([ap.shape[0], count] + list(ap.shape[1:]))


class Program:
    def __init__(self, nc, dram, small_at, out, blocks=4):
        self.nc, self.dram, self.small_at, self.out, self.blocks = nc, dram, small_at, out, blocks


    def build(self):
        nc = self.nc
        from contextlib import ExitStack
        with ExitStack() as ctx:
            sem = lambda name: ctx.enter_context(nc.semaphore(name))
            columns = 206 * 256
            arena = ctx.enter_context(nc.sbuf_tensor("arena", [P, columns], F32))
            self.psum = ctx.enter_context(nc.psum_tensor("banks", [P, 8, 512], F32))
            self.space = Space(arena, columns)
            self.pe, self.act, self.dve, self.pool, self.sp = (Queue(sem(n)) for n in ("pe", "act", "dve", "pool", "sp"))
            self.sem = sem
            self.start()
            self.block1()
            if self.blocks >= 2:
                self.block2()
            if self.blocks >= 3:
                self.block3()
            if self.blocks >= 4:
                self.block4()
            self.finish()
            block = ctx.enter_context(nc.Block())
            block.tensor(lambda e: self.pe.emit(e))
            block.scalar(lambda e: self.act.emit(e))
            block.vector(lambda e: self.dve.emit(e))
            block.gpsimd(lambda e: self.pool.emit(e))
            block.sync(lambda e: self.sp.emit(e))

    def load(self, name, top=False, source=None, queue=None):
        if name in self.early:
            return self.early.pop(name)
        source = self.dram[name] if source is None else source
        piece = self.space.take(source.shape[-1], top)
        t = Transfers(self.sem(f"load_{name}"))
        t.start(queue or self.sp, piece.ap, source, piece.before)
        return piece, t.mark

    def load_early(self, *names):
        for name in names:
            self.early[name] = self.load(name, True)

    def start(self):
        self.early = {}
        x_nat, xT = self.space.take(SEQS * TILES * CH), self.space.take(SEQS * CHUNKS * (TOKENS + 1))
        self.x_nat = split(x_nat.ap, SEQS, TILES, CH)
        self.xT = split(xT.ap, SEQS, CHUNKS, TOKENS + 1)
        self.x_ready, self.xT_ready = [None] * SEQS, [None] * SEQS
        self.xT_read = [[] for _ in range(SEQS)]
        self.pieces = {}
        for group in "keep", "small":
            self.pieces[group], self.small_ready = self.load(group)
            if group == "keep":
                keep_ready = self.small_ready
        self.small_ready = [keep_ready, self.small_ready]
        self.wqkv, self.wqkv_ready = self.load("a_wqkv", True)
        xT_in = split(self.dram["xT"], SEQS, CHUNKS, TOKENS)
        for b in range(SEQS):
            t = Transfers(self.sem(f"x{b}"))
            t.start(self.sp, self.xT[:, b, :, 1:], xT_in[:, b])
            self.xT_ready[b] = t.mark
            if b == 0:
                self.wproj, self.wproj_ready = self.load("a_wproj", True)
                self.wqk, self.wqk_ready = self.load("a_wqk", True)
            t = Transfers(self.sem(f"xn{b}"))
            t.start(self.sp, self.x_nat[:, b], self.dram["x"][b].rearrange("(t p) c -> p t c", p=P))
            self.x_ready[b] = t.mark
        self.edge_zero = self.pool(lambda e: e.memset(self.xT[:, :, :, 0:1], 0.0))
        self.half = self.space.take(64)
        self.half_ready = self.pool(lambda e: e.memset(self.half.ap, -0.5))
        ident = self.S("identity")
        self.ident16 = self.space.take(64)
        self.ident16 = self.ident16.ap.bitcast(BF16)
        self.ident16_ready = self.dve(lambda e: e.tensor_copy(self.ident16, ident), self.small_ready)

    def S(self, name):
        group, at, n = self.small_at[name]
        return self.pieces[group].ap[:, at:at + n]

    def finish(self):
        t = Transfers(self.sem("store"))
        for b in range(SEQS):
            t.start(self.sp, self.out[b].rearrange("(t p) c -> p t c", p=P), self.x_nat[:, b], self.x_ready[b])
        self.sp.wait([t.mark])


    def rsqrt(self, out, in_, scratch, count, *marks):
        eps = self.pool(lambda e: e.tensor_scalar(scratch, in_, EPS, None, ALU.add), *marks, self.half_ready)
        half = self.half.ap[:, 0:count]
        return self.pool(lambda e: e.tensor_tensor(out, scratch, half, ALU.pow), eps)

    def norm_and_turn(self, b, banks, sums, turn=True):
        x, small = self.x_nat[:, b], self.space.take(TILES * 10)
        stats = split(small.ap[:, 0:TILES * 6], TILES, 6)
        mv = split(small.ap[:, TILES * 6:TILES * 8], TILES, 2)
        rstd, scratch = small.ap[:, TILES * 8:TILES * 9], small.ap[:, TILES * 9:TILES * 10]
        for t in range(TILES):
            s = self.dve(lambda e, t=t: e.bn_stats(stats[:, t], x[:, t]), sums[t], small.before)
            m = self.dve(lambda e, t=t: e.bn_aggr(mv[:, t], stats[:, t]), s)
        yield
        r = self.rsqrt(rstd, mv[:, :, 1], scratch, TILES, m)
        yield
        done = []
        for t in range(TILES):
            done.append(self.dve(lambda e, t=t: e.tensor_scalar(
                x[:, t], x[:, t], mv[:, t, 0:1], rstd[:, t:t + 1], ALU.subtract, ALU.mult), r))
        small.give(done[-1])
        self.x_ready[b] = done[-1]
        if not turn:
            return
        yield
        for c in range(CHUNKS):
            i, bank, free = banks.take()
            for t in range(TILES):
                put = self.pe(lambda e, t=t: e.transpose(bank[:, t * P:(t + 1) * P], x[:, t, c * P:(c + 1) * P], self.S("identity")),
                              done[t], free)
            out = self.xT[:, b, c, 1:]
            q = self.act if c else self.dve
            if c:
                copied = self.act(lambda e: e.activation(out, bank, ACT.Copy), put, self.xT_read[b], self.edge_zero)
            else:
                first = self.dve(lambda e: e.tensor_copy(out, bank), put, self.xT_read[b], self.edge_zero)
            banks.give(i, copied if c else first)
            yield
        self.xT_ready[b] = [first, copied]
        self.xT_read[b] = []

    @staticmethod
    def interleave(makers, lanes, offset=0):
        active, rounds = [], 0
        makers = list(makers)
        while active or makers:
            if makers and len(active) < lanes and (not active or rounds >= offset):
                active.append(makers.pop(0)())
                rounds = 0
            rounds += 1
            for g in list(active):
                if next(g, "end") == "end":
                    active.remove(g)

    TILE_LANES, TILE_OFFSET = 2, 4

    @staticmethod
    def weave(streams):
        active, since = [[] for _ in streams], [offset for _, _, offset, _ in streams]
        waiting, rounds = [True] * len(streams), 0
        while any(waiting) or any(active):
            rounds += 1
            for n, (source, lanes, offset, pace) in enumerate(streams):
                since[n] += 1
                if waiting[n] and len(active[n]) < lanes and (since[n] >= offset or not active[n]):
                    g = next(source, None)
                    if g is None:
                        waiting[n] = False
                    else:
                        active[n].append(g)
                        since[n] = 0
                for k, g in enumerate(list(active[n])):
                    if (rounds + k) % pace == 0 and next(g, "end") == "end":
                        active[n].remove(g)


    def gating(self, banks):
        S, sp = self.S, self.space
        H, HD = 16, 16
        work = sp.take(16 + 9 * P + 64)
        w = work.ap
        mean = split(w[:, 0:16], CHUNKS, SEQS)
        area = [w[:, 16 + i * P:16 + (i + 1) * P] for i in range(9)]
        wqk = split(self.wqk.ap, CHUNKS, H, 2 * HD)
        for b in range(SEQS):
            m = self.dve(lambda e, b=b: e.tensor_reduce(mean[:, :, b], self.xT[:, b, :, 1:], AX.X, ALU.add),
                         self.xT_ready[b], work.before)
            if b % 2:
                yield
        m = self.dve(lambda e: e.tensor_scalar(w[:, 0:16], w[:, 0:16], 1.0 / TOKENS, None, ALU.mult), m)
        i, bank, free = banks.take()
        for h in range(H):
            for c in range(CHUNKS):
                mm = self.pe(lambda e, h=h, c=c: e.matmul(bank[0:32, h * SEQS:(h + 1) * SEQS], wqk[:, c, h],
                                                          mean[:, c, :], start=c == 0, stop=c == 1), m, free, self.wqk_ready)
        self.wqk.give(mm)
        qk = area[0]
        qk_ready = self.act(lambda e: e.activation(qk[0:32, :], bank[0:32, 0:P], ACT.Copy), mm)
        banks.give(i, qk_ready)

        def product(out, lhsT, rhs, rows, *marks, copy=None):
            i, bank, free = banks.take()
            mm = self.pe(lambda e: e.matmul(bank[0:rows, 0:P], lhsT, rhs, start=True, stop=True), *marks, free)
            done = copy(bank, mm)
            banks.give(i, done)
            return done

        plain = lambda out, rows, bias: lambda bank, mm: self.dve(
            lambda e: e.tensor_scalar(out, bank[0:rows, 0:P], bias, None, ALU.add), mm)
        ax, hid, phi, psi, dev, sq, rs, pg, psi2 = area
        hid_r = product(None, S("a_phi1")[0:32], qk[0:32], P, qk_ready, copy=lambda bank, mm: self.act(
            lambda e: e.activation(hid, bank[:, 0:P], ACT.Silu, bias=S("a_bphi1")), mm))
        yield
        phi_r = product(None, S("a_phi2"), hid, 16, hid_r, copy=plain(phi[0:16], 16, S("a_bphi2")[0:16]))
        yield
        ax_r = product(None, S("a_A")[0:32], qk[0:32], P, copy=lambda bank, mm: self.dve(
            lambda e: e.tensor_copy(hid, bank[:, 0:P]), mm, phi_r))
        yield
        psi_r = product(None, S("a_psi1"), hid, P, ax_r, copy=plain(psi, P, S("a_bpsi1")))
        yield
        dev_r = product(None, S("same_head32"), psi, P, psi_r, copy=lambda bank, mm: self.dve(
            lambda e: e.scalar_tensor_tensor(dev, bank[:, 0:P], -1.0 / 32, psi, ALU.mult, ALU.add), mm))
        yield
        sq_r = self.dve(lambda e: e.tensor_tensor(sq, dev, dev, ALU.mult), dev_r)
        var_r = product(None, S("same_head32"), sq, P, sq_r, copy=lambda bank, mm: self.dve(
            lambda e: e.tensor_scalar(rs, bank[:, 0:P], 1.0 / 32, EPS, ALU.mult, ALU.add), mm))
        yield
        std_r = self.act(lambda e: e.activation(sq, rs, ACT.Sqrt), var_r)
        rstd_r = self.dve(lambda e: e.reciprocal(rs, sq), std_r)
        a = self.dve(lambda e: e.tensor_tensor(dev, dev, rs, ALU.mult), rstd_r)
        a = self.dve(lambda e: e.tensor_scalar(dev, dev, S("a_lng"), S("a_lnb"), ALU.mult, ALU.add), a)
        gelu_r = self.act(lambda e: e.activation(pg, dev, ACT.Gelu), a)
        yield
        psi2_r = product(None, S("a_psi2"), pg, 16, gelu_r, copy=plain(psi2[0:16], 16, S("a_bpsi2")[0:16]))
        yield
        t = self.dve(lambda e: e.tensor_tensor(psi2[0:16], psi2[0:16], phi[0:16], ALU.mult), psi2_r)
        t = self.dve(lambda e: e.tensor_scalar(psi2[0:16], psi2[0:16], S("a_temp")[0:16], S("a_mix")[0:16],
                                               ALU.mult, ALU.mult), t)
        i, bank, free = banks.take()
        terms = split(psi2, 4, 4, SEQS)
        place = split(S("spread16"), 4, P)
        for j in range(4):
            mm = self.pe(lambda e, j=j: e.matmul(split(bank[:, 0:32], 4, SEQS), place[0:16, j], terms[0:16, :, j, :],
                                                 start=j == 0, stop=j == 3), t, free)
        self.factor = sp.take(32)
        factor = split(self.factor.ap, 4, SEQS)
        f = self.dve(lambda e: e.scalar_tensor_tensor(factor, split(bank[:, 0:32], 4, SEQS), 1.0,
                                                      spread(S("a_gamma"), [P, 4, SEQS]), ALU.add, ALU.mult),
                     mm, self.factor.before)
        banks.give(i, f)
        work.give(f)
        self.factor_ready = f

    BACKGROUND = (2, 1, 2, 2)

    Q_PARTS, K_PARTS = (0, 1, 2, 0, 1, 0), (0, 0, 0, 1, 1, 2)
    STACK, SHIFT_ROWS = 96, 8

    def block1(self):
        sp, pe, act, dve, pool = self.space, self.pe, self.act, self.dve, self.pool
        S = self.S
        H, HD, HALF, UNIT = 16, 16, 8, 4
        STACK, ROWS = self.STACK, self.SHIFT_ROWS
        SCALE = HD ** -0.5 / 0.72
        max_banks, exp_banks = Banks(self.psum, (0, 1, 2)), Banks(self.psum, (3, 4))
        out_banks, misc = Banks(self.psum, (5, 6)), Banks(self.psum, (7,))
        wq, wk = (split(self.wqkv.ap, CHUNKS, 3, CH)[:, :, n] for n in (0, 1))
        wv = split(self.wqkv.ap, CHUNKS, 3, CH)[:, :, 2]
        xT = self.xT
        units = 2 * 2 * SEQS

        setup = sp.take(2 + 16 + 64 + 64)
        sp.rested = True
        alpha = setup.ap[:, 0:2]
        alpha_ready = dve(lambda e: e.tensor_scalar(alpha, S("a_alpha"), SCALE, None, ALU.mult), self.small_ready, setup.before)
        beta16 = split(setup.ap[:, 2:2 + 32].bitcast(BF16)[:, 0:48], 3, H)
        rest = split(setup.ap[:, 40:40 + 32], 2, H)
        m = dve(lambda e: e.tensor_copy(beta16[:, 0], S("a_beta")), self.small_ready)
        m = dve(lambda e: e.tensor_tensor(rest[:, 0], S("a_beta"), beta16[:, 0], ALU.subtract), m)
        m = dve(lambda e: e.tensor_copy(beta16[:, 1], rest[:, 0]), m)
        m = dve(lambda e: e.tensor_tensor(rest[:, 1], rest[:, 0], beta16[:, 1], ALU.subtract), m)
        beta_ready = dve(lambda e: e.tensor_copy(beta16[:, 2], rest[:, 1]), m)

        stacks_dram = self.nc.dram_tensor("stacks", (2 * SEQS, 2, STACK, HALF * TOKENS), BF16).ap()
        shift_dram = self.nc.dram_tensor("shifts", (units, ROWS * UNIT, TOKENS), BF16).ap()

        dens_dram = self.nc.dram_tensor("dens", (SEQS, 2, UNIT, 4 * TOKENS), F32).ap()
        dens_dma = [[Transfers(self.sem(f"dens_{way}{n}")) for way in ("there", "back")] for n in range(2)]

        slots = []
        for n in range(4):
            piece = sp.take(2 * UNIT * TOKENS // 2)
            view = split(piece.ap.bitcast(BF16), 2, UNIT, TOKENS)
            flat = split(piece.ap.bitcast(BF16), 2, UNIT * TOKENS)
            zero = dve(lambda e: e.memset(piece.ap[STACK:P, 0:UNIT * TOKENS // 2], 0.0), piece.before)
            made = dve(lambda e: e.tensor_copy(flat[STACK:P, 1], S("ones5")[STACK:P].to_broadcast([P - STACK, UNIT * TOKENS])),
                       self.small_ready, piece.before)
            slots.append(dict(piece=piece, stack=view, flat=flat, made=[zero, made], read=None,
                              dma=Transfers(self.sem(f"stack{n}")), shift=Transfers(self.sem(f"shift{n}")),
                              shift_out=Transfers(self.sem(f"shift_out{n}"))))
        shifts = []
        for n in range(2):
            piece = sp.take(TILES * ROWS * UNIT // 2)
            made = pool(lambda e: e.memset(piece.ap, 0.0), piece.before)
            shifts.append(dict(ap=split(piece.ap.bitcast(BF16), TILES, ROWS, UNIT), piece=piece, made=made, read=None))
        values = []
        for n in range(2):
            piece = sp.take(TILES * H * 32)
            made = pool(lambda e: e.memset(piece.ap, 1.0), piece.before)
            values.append(dict(ap=split(piece.ap, TILES, H, 32), piece=piece, made=made, read=None))
        biased = {}

        parts_dma = [[Transfers(self.sem(f"parts_{side}{n}")) for side in "qk"] for n in range(2)]
        stored = {}

        def prepare(half):
            b, c = divmod(half, 2)
            for side, w in enumerate((wq, wk)):
                out = parts_dma[half % 2][side]
                i, bank, free = misc.take()
                for k in range(CHUNKS):
                    mm = pe(lambda e: e.matmul(bank, w[:, k, c * P:(c + 1) * P], xT[:, b, k, 1:], start=k == 0, stop=k == 1),
                            free, self.xT_ready[b], self.wqkv_ready)
                rest, parts = sp.take(2 * TOKENS), sp.take(3 * TOKENS // 2)
                whole, left = rest.ap[:, 0:TOKENS], rest.ap[:, TOKENS:]
                part = split(parts.ap.bitcast(BF16), 3, TOKENS)
                if side == 0:
                    m = act(lambda e: e.activation(whole, bank, ACT.Copy, scale=alpha[:, c:c + 1]), mm, alpha_ready, rest.before)
                else:
                    m = act(lambda e: e.activation(whole, bank, ACT.Copy), mm, rest.before)
                misc.give(i, m)
                cut = dve if half < 2 else pool
                a = cut(lambda e: e.tensor_copy(part[:, 0], whole), m, parts.before)
                yield
                a = cut(lambda e: e.tensor_tensor(left, whole, part[:, 0], ALU.subtract), a)
                a = cut(lambda e: e.tensor_copy(part[:, 1], left), a)
                yield
                a = cut(lambda e: e.tensor_tensor(part[:, 2], left, part[:, 1], ALU.subtract), a)
                rest.give(a)
                to = stacks_dram[half, side].rearrange("(n d) (h t) -> n (d h) t", d=HD, h=HALF)
                runs = ((0, part[:, 0:3]), (3, part[:, 0:2]), (5, part[:, 0:1])) if side == 0 else (
                    (0, repeated(part[:, 0], 3)), (3, repeated(part[:, 1], 2)), (5, part[:, 2:3]))
                for at, src in runs:
                    out.start(self.sp, to[at:at + src.shape[1]].rearrange("n q t -> q n t"), src, a)
                parts.give(out.mark)
                yield
            stored[half] = [out.mark for out in parts_dma[half % 2]]
            if c == 0:
                biased[b] = pool(lambda e: e.tensor_tensor(self.x_nat[:, b], self.x_nat[:, b], repeated(S("a_bproj"), TILES), ALU.add),
                                 self.x_ready[b], self.small_ready)
                v = values[b % 2]
                for t in range(TILES):
                    i, bank, free = misc.take()
                    for k in range(CHUNKS):
                        mm = pe(lambda e: e.matmul(bank[:, 0:CH], xT[:, b, k, 1 + t * P:1 + (t + 1) * P], wv[:, k],
                                                   start=k == 0, stop=k == 1), free, self.xT_ready[b])
                    m = act(lambda e: e.activation(v["ap"][:, t, :, 0:HD], split(bank[:, 0:CH], H, HD), ACT.Copy), mm, v["made"], v["read"])
                    misc.give(i, m)
                    v["ready"] = m
                    yield

        def fetch(u):
            half, g2 = divmod(u, 2)
            slot = slots[u % 4]
            for side in range(2):
                slot["dma"].start(self.sp, slot["flat"][0:STACK, side],
                                  stacks_dram[half, side, :, g2 * UNIT * TOKENS:(g2 + 1) * UNIT * TOKENS],
                                  stored[half], slot["read"], slot["made"])

        def score_maxima(u, t):
            slot, sh = slots[u % 4], shifts[u % 2]
            st = slot["stack"]
            if t == 0:
                sh["max_piece"] = sp.take(TILES * UNIT * 2)
                sh["max"] = split(sh["max_piece"].ap[:, 0:16], TILES, UNIT)
            for j in range(UNIT):
                i, bank, free = max_banks.take()
                mm = pe(lambda e: e.matmul(bank, st[0:STACK, 0, j, t * P:(t + 1) * P], st[0:STACK, 1, j, :],
                                           start=True, stop=True), free, slot["dma"].mark)
                m = dve(lambda e: e.tensor_reduce(sh["max"][:, t, j:j + 1], bank, AX.X, ALU.max, negate=True), mm, sh["max_piece"].before)
                max_banks.give(i, m)
                sh["max_ready"] = m
                yield

        def shift_rows(u):
            half, g2 = divmod(u, 2)
            slot, sh = slots[u % 4], shifts[u % 2]
            h0 = (half % 2) * HALF + g2 * UNIT
            rest = split(sh["max_piece"].ap[:, 16:32], TILES, UNIT)
            mx, out = sh["max"], sh["ap"]
            for n in range(3):
                beta_in = dve(lambda e: e.tensor_copy(out[:, :, 2 + n], repeated(beta16[:, n, h0:h0 + 4], TILES)), beta_ready, sh["made"], sh["read"])
            m = dve(lambda e: e.tensor_tensor(mx, mx, repeated(S("a_beta")[:, h0:h0 + 4], TILES), ALU.subtract), sh["max_ready"])
            m = dve(lambda e: e.tensor_copy(out[:, :, 0], mx), m)
            m = dve(lambda e: e.tensor_tensor(rest, mx, out[:, :, 0], ALU.subtract), m)
            m = dve(lambda e: e.tensor_copy(out[:, :, 1], rest), m)
            sh["max_piece"].give(m)
            yield
            i, bank, free = misc.take()
            n_rows = ROWS * UNIT
            for t in range(TILES):
                mm = pe(lambda e: e.matmul(bank[0:n_rows, t * P:(t + 1) * P], out[:, t].rearrange("p s j -> p (s j)"), self.ident16,
                                           start=True, stop=True), m, beta_in, free, self.ident16_ready)
            sh["read"] = mm
            flat = sp.take(TOKENS // 2)
            rows = flat.ap.bitcast(BF16)
            m = act(lambda e: e.activation(rows[0:n_rows], bank[0:n_rows], ACT.Copy), mm, flat.before)
            misc.give(i, m)
            slot["shift_out"].start(self.sp, shift_dram[u], rows[0:n_rows], m)
            flat.give(slot["shift_out"].mark)
            slot["shift"].start(self.sp, slot["flat"][STACK:STACK + ROWS, 0], shift_dram[u].rearrange("(s j) t -> s (j t)", j=UNIT),
                                slot["shift_out"].mark, slot["read"])

        def attend(u, t):
            half, g2 = divmod(u, 2)
            slot, v = slots[u % 4], values[(half // 2) % 2]
            st = slot["stack"]
            e_piece = sp.take(UNIT * TOKENS)
            ex = split(e_piece.ap, UNIT, TOKENS)
            marks = []
            for j in range(UNIT):
                i, bank, free = exp_banks.take()
                mm = pe(lambda e: e.matmul(bank, st[:, 1, j, t * P:(t + 1) * P], st[:, 0, j, :],
                                           start=True, stop=True), free, slot["dma"].mark, slot["shift"].mark)
                m = act(lambda e: e.activation(ex[:, j], bank, ACT.Exp), mm, e_piece.before)
                exp_banks.give(i, m)
                marks.append(m)
                if j < UNIT - 1:
                    yield
            if t == TILES - 1:
                slot["read"] = mm

            def values_product():
                if t == 0:
                    outs[u] = out_banks.take()
                _, out, out_free = outs[u]
                h0 = (half % 2) * HALF + g2 * UNIT
                for j in range(UNIT):
                    mm = pe(lambda e: e.matmul(out[32 * j:32 * j + 32, :], v["ap"][:, t, h0 + j, :], ex[:, j],
                                               start=t == 0, stop=t == TILES - 1, skip_group_check=True),
                            marks[j], v["ready"], out_free)
                e_piece.give(mm)
                if t == TILES - 1:
                    v["read"] = mm
                    aside.append(lambda: set_aside(u, mm))
            pending.append(values_product)

        outs, raw, pending, aside, shifting = {}, {}, [], [], []

        def set_aside(u, mm):
            b, g = divmod(u, 4)
            if g == 0:
                raw[b] = (sp.take(4 * TOKENS), [])
            sums, marks = raw[b]
            i, out, _ = outs.pop(u)
            cols = slice(g * TOKENS, (g + 1) * TOKENS)
            m = dve(lambda e: e.tensor_copy(sums.ap[:, cols], out), mm, sums.before)
            out_banks.give(i, m)
            marks.append(m)

        def project(b):
            sums, marks = raw.pop(b)
            wp = split(self.wproj.ap, 4, CH)
            factor = split(self.factor.ap, 4, SEQS)
            few = sp.take(4 * 4 * TOKENS // P)
            gather, back = dens_dma[b % 2]
            rows_of_ones = sums.ap[HD:P:32]
            gather.start(self.pool, dens_dram[b, 0], rows_of_ones, marks)
            gather.start(self.pool, few.ap, dens_dram[b, 0].rearrange("j t -> (j t)").rearrange("(p n) -> p n", p=P), gather.mark, few.before)
            gathered = gather.mark
            for _ in range(3):
                yield
            m = dve(lambda e: e.reciprocal(few.ap, few.ap), gathered)
            yield
            back.start(self.pool, dens_dram[b, 1].rearrange("j t -> (j t)").rearrange("(p n) -> p n", p=P), few.ap, m)
            stored_back = back.mark
            few.give(stored_back)
            dens = sp.take(4 * TOKENS)
            for j in range(4):
                back.start(self.pool, dens.ap[32 * j:32 * j + 32], dens_dram[b, 1, j:j + 1].to_broadcast([32, 4 * TOKENS]),
                           stored_back, dens.before)
            inverse = back.mark
            for _ in range(6):
                yield
            ready = []
            for g in range(4):
                cols = slice(g * TOKENS, (g + 1) * TOKENS)
                ready.append(dve(lambda e: e.scalar_tensor_tensor(sums.ap[:, cols], sums.ap[:, cols], factor[:, g, b:b + 1], dens.ap[:, cols],
                                                                  ALU.mult, ALU.mult), inverse, self.factor_ready))
                if g % 2:
                    yield
            dens.give(ready[-1])
            rows = []
            for t in range(TILES):
                i, bank, free = misc.take()
                for g in range(4):
                    at = g * TOKENS + t * P
                    mm = pe(lambda e: e.matmul(bank[:, 0:CH], sums.ap[:, at:at + P], wp[:, g], start=g == 0, stop=g == 3),
                            ready, free, self.wproj_ready)
                x = self.x_nat[:, b, t]
                s = dve(lambda e: e.tensor_tensor(x, x, bank[:, 0:CH], ALU.add), mm, biased[b])
                misc.give(i, s)
                rows.append(s)
                yield
            sums.give(mm)
            yield from self.norm_and_turn(b, misc, rows)

        background, preparing = [], {}

        def advance():
            while background:
                if next(background[0], "end") != "end":
                    return
                background.pop(0)

        def prepared(half):
            while preparing.get(half) in background:
                advance()

        def prepare_behind(half):
            if half < 2 * SEQS and half not in preparing:
                preparing[half] = prepare(half)
                background.insert(0, preparing[half])

        prepare_behind(0)
        prepared(0)
        prepare_behind(1)
        prepared(1)
        self.factor_ready = None
        background.append(self.gating(misc))
        LAG = 2
        for u in range(4):
            fetch(u)
        for u in range(-LAG, units):
            if u % 2 == 0:
                prepare_behind((u + 4) // 2)
            for t in range(TILES):
                earlier = list(pending)
                pending.clear()
                both = ([score_maxima(u + LAG, t)] if u + LAG < units else []) + ([attend(u, t)] if u >= 0 else [])
                for _ in range(UNIT):
                    for g in both:
                        next(g, None)
                while aside:
                    aside.pop(0)()
                for product in earlier:
                    product()
                while shifting and t == 1:
                    for _ in shifting.pop(0):
                        pass
                if t == 1 and u >= 0 and u + 3 < units and u + 3 >= 4:
                    prepared((u + 3) // 2)
                    fetch(u + 3)
                for _ in range(self.BACKGROUND[t]):
                    advance()
            if u + LAG < units:
                shifting.append(shift_rows(u + LAG))
                next(shifting[0])
            if u >= 4 and u % 4 == 0:
                while self.factor_ready is None:
                    advance()
                background.append(project(u // 4 - 1))
                if u == units - UNIT and self.blocks >= 2:
                    self.load_early("d_Wq", "d_WkT", "d_Wv", "d_Wo")
        pending.pop()()
        aside.pop()()
        background.append(project(SEQS - 1))
        while background:
            advance()
        self.banks = Banks(self.psum, ())
        for group in (max_banks, exp_banks, out_banks, misc):
            self.banks.free += group.free
        marks = self.all_marks()
        for d in slots + shifts + values:
            d["piece"].give(marks)
        for piece in (setup, self.wqkv, self.wproj, self.factor):
            piece.give(marks)
        sp.rested = False

    def pe_mark(self):
        return (self.pe.sem, self.pe.count)

    def act_mark(self):
        return (self.act.sem, self.act.count)

    def dve_mark(self):
        return (self.dve.sem, self.dve.count)

    def pool_mark(self):
        return (self.pool.sem, self.pool.count)


    def all_marks(self):
        return [self.pe_mark(), self.act_mark(), self.dve_mark(), self.pool_mark()]

    def block2(self):
        sp, pe, act, dve, pool, S = self.space, self.pe, self.act, self.dve, self.pool, self.S
        H, HD, SLOTS, EXPERTS, HIDDEN = 16, 16, 16, 16, 1024
        banks = self.banks
        W = {}
        for n in ("d_Wq", "d_WkT", "d_Wv", "d_Wo"):
            W[n] = self.load(n, True)
        w2 = lambda n: split(W[n][0].ap, CHUNKS, CH)
        ident = S("identity")

        RING = 7
        order = [(m, 4 * q + j) for q in range(4) for m in ("e_W1", "e_Wg", "e_W2") for j in range(4)]
        ring = [sp.take(2048, True) for _ in range(RING)]
        ring_dma = [Transfers(self.sem(f"expert{n}")) for n in range(RING)]
        arrived, issued, released = {}, [0], {}
        def load_next(mark):
            n = issued[0]
            if n < len(order):
                m, e = order[n]
                ring_dma[n % RING].start(self.sp, ring[n % RING].ap, self.dram[m][e], ring[n % RING].before, mark)
                arrived[order[n]] = (ring[n % RING].ap, ring_dma[n % RING].mark)
                issued[0] += 1
        for _ in range(RING):
            load_next(None)
        bias = {}
        def load_bias(q):
            for n in ("e_b1", "e_bg"):
                piece = sp.take(HIDDEN, True)
                t = Transfers(self.sem(f"{n}{q}"))
                t.start(self.sp, piece.ap, self.dram[n][q], piece.before)
                bias[n, q] = (piece, t.mark)

        once = sp.take(32 + 2 * 256 * 2 + 8)
        q_T = split(once.ap[:, 0:32], CHUNKS, SLOTS)
        q_blk = split(once.ap[:, 32:32 + 512], CHUNKS, H, SLOTS)
        meet = split(once.ap[:, 544:544 + 512], CHUNKS, H * SLOTS)
        const = once.ap[:, 1056:1058]
        head_of = split(S("head_of"), CHUNKS, H)
        i, bank, free = banks.take()
        for f in range(CHUNKS):
            for k in range(CHUNKS):
                mm = pe(lambda e: e.matmul(bank[:, f * 16:f * 16 + 16], w2("d_Wq")[:, k, f * P:(f + 1) * P],
                                           split(S("slotT"), CHUNKS, SLOTS)[:, k], start=k == 0, stop=k == 1), free, W["d_Wq"][1])
        for f in range(CHUNKS):
            m = dve(lambda e: e.tensor_scalar(q_T[:, f], bank[:, f * 16:f * 16 + 16], S("d_bq")[:, f:f + 1], 0.25, ALU.add, ALU.mult),
                    mm, once.before)
        banks.give(i, m)
        for f in range(CHUNKS):
            blk = dve(lambda e: e.tensor_tensor(q_blk[:, f], repeated(q_T[:, f], H), spread(head_of[:, f], [P, H, SLOTS]), ALU.mult), m)
        i, bank, free = banks.take()
        for c in range(CHUNKS):
            for f in range(CHUNKS):
                mm = pe(lambda e: e.matmul(bank[:, c * 256:(c + 1) * 256], w2("d_WkT")[:, f, c * P:(c + 1) * P],
                                           q_blk[:, f].rearrange("p h s -> p (h s)"), start=f == 0, stop=f == 1), free, blk, W["d_WkT"][1])
        meet_ready = act(lambda e: e.activation(meet.rearrange("p c n -> p (c n)"), bank, ACT.Copy), mm, once.before)
        banks.give(i, meet_ready)
        i, bank, free = banks.take()
        for t in range(2):
            for f in range(CHUNKS):
                mm = pe(lambda e: e.matmul(bank[:, t:t + 1], q_blk[:, f].rearrange("p h s -> p (h s)")[:, t * P:(t + 1) * P],
                                           S("d_bk")[:, f:f + 1], start=f == 0, stop=f == 1), free, blk)
        const_ready = dve(lambda e: e.tensor_copy(const, bank[:, 0:2]), mm, meet_ready)
        banks.give(i, const_ready)

        gathered = sp.take(CHUNKS * H * P)
        g_view = split(gathered.ap, CHUNKS, H, SEQS, SLOTS)
        gathered_ready = []
        o_bias = []
        for b in range(SEQS):
            o_bias.append(None)

        def slots_attend(b):
            work = sp.take(2 * TOKENS + 16)
            s = split(work.ap[:, 0:2 * TOKENS], 2, TOKENS)
            st = work.ap[:, 2 * TOKENS:]
            turned = sp.take(TILES * 2 * P)
            aT = split(turned.ap, TILES, 2, P)
            copies = []
            for t in range(2):
                i, bank, free = banks.take()
                for c in range(CHUNKS):
                    mm = pe(lambda e: e.matmul(bank, meet[:, c, t * P:(t + 1) * P], self.xT[:, b, c, 1:], start=c == 0, stop=c == 1),
                            free, meet_ready, self.xT_ready[b])
                m = dve(lambda e: e.tensor_scalar(s[:, t], bank, const[:, t:t + 1], None, ALU.add), mm, const_ready, work.before)
                banks.give(i, m)
                yield
                m = dve(lambda e: e.tensor_reduce(st[:, t:t + 1], s[:, t], AX.X, ALU.max, negate=True), m)
                m = act(lambda e: e.activation(s[:, t], s[:, t], ACT.Exp, bias=st[:, t:t + 1], accum_out=st[:, 4 + t:5 + t]), m)
                yield
                m = dve(lambda e: e.reciprocal(st[:, 8 + t:9 + t], st[:, 4 + t:5 + t]), m)
                m = dve(lambda e: e.tensor_scalar(s[:, t], s[:, t], st[:, 8 + t:9 + t], None, ALU.mult), m)
                yield
                i, bank, free = banks.take()
                for n in range(TILES):
                    mm = pe(lambda e: e.transpose(bank[:, n * P:(n + 1) * P], s[:, t, n * P:(n + 1) * P], ident), m, free)
                m = act(lambda e: e.activation(aT[:, :, t], split(bank, TILES, P), ACT.Copy), mm, turned.before)
                banks.give(i, m)
                copies.append(m)
                yield
            work.give(m)
            i, bank, free = banks.take()
            for c in range(CHUNKS):
                for n in range(TILES):
                    mm = pe(lambda e: e.matmul(bank[:, c * 256:(c + 1) * 256], self.x_nat[:, b, n, c * P:(c + 1) * P],
                                               aT[:, n].rearrange("p t s -> p (t s)"), start=n == 0, stop=n == TILES - 1),
                            copies, free, self.x_ready[b])
            turned.give(mm)
            for c in range(CHUNKS):
                m = dve(lambda e: e.tensor_copy(g_view[:, c, :, b, :], split(bank[:, c * 256:(c + 1) * 256], H, SLOTS)), mm, gathered.before)
            banks.give(i, m)
            gathered_ready.append(m)
            o_bias[b] = pool(lambda e: e.tensor_tensor(self.x_nat[:, b], self.x_nat[:, b], repeated(S("c_bo"), TILES), ALU.add), mm)

        self.interleave([lambda b=b: slots_attend(b) for b in range(SEQS)], 4, 1)

        slots = sp.take(256 * 4 + 32)
        o, h, tmp = (slots.ap[:, n * 256:(n + 1) * 256] for n in range(3))
        oT = split(slots.ap[:, 768:1024], CHUNKS, P)
        st = slots.ap[:, 1024:]
        g3 = split(gathered.ap, CHUNKS, H, P)
        i, bank, free = banks.take()
        for hd in range(H):
            for c in range(CHUNKS):
                mm = pe(lambda e: e.matmul(bank[:, hd * 16:hd * 16 + 16], g3[:, c, hd], w2("d_Wv")[:, c, hd * 16:hd * 16 + 16],
                                           start=c == 0, stop=c == 1), free, gathered_ready, W["d_Wv"][1])
        gathered.give(mm)
        m = dve(lambda e: e.tensor_tensor(tmp, bank[:, 0:256], S("d_bv"), ALU.add), mm, slots.before)
        banks.give(i, m)

        def turned(src, m):
            i, bank, free = banks.take()
            for c in range(CHUNKS):
                mm = pe(lambda e: e.transpose(bank[:, c * P:(c + 1) * P], src[:, c * P:(c + 1) * P], ident), m, free)
            return i, split(bank[:, 0:256], CHUNKS, P), mm

        i, bank, mm = turned(tmp, m)
        m = dve(lambda e: e.tensor_copy(oT, bank), mm)
        banks.give(i, m)
        i, bank, free = banks.take()
        for c in range(CHUNKS):
            mm = pe(lambda e: e.matmul(bank[:, 0:256], oT[:, c], w2("d_Wo")[:, c], start=c == 0, stop=c == 1), m, free, W["d_Wo"][1])
        m = dve(lambda e: e.tensor_tensor(o, bank[:, 0:256], S("d_bo"), ALU.add), mm)
        banks.give(i, m)
        for n in ("d_Wq", "d_WkT", "d_Wv", "d_Wo"):
            W[n][0].give(m)
        once.give(self.all_marks())
        o_ready = dve(lambda e: e.tensor_tensor(o, o, S("slot"), ALU.add), m)
        m = dve(lambda e: e.bn_stats(st[:, 0:6], o), o_ready)
        m = dve(lambda e: e.bn_aggr(st[:, 6:8], st[:, 0:6]), m)
        m = self.rsqrt(st[:, 8:9], st[:, 7:8], st[:, 9:10], 1, m)
        m = dve(lambda e: e.tensor_scalar(h, o, st[:, 6:7], st[:, 8:9], ALU.subtract, ALU.mult), m)
        m = dve(lambda e: e.tensor_tensor(h, h, S("e_lng"), ALU.mult), m)
        h_ready = dve(lambda e: e.tensor_tensor(h, h, S("e_lnb"), ALU.add), m)
        i, bank, mm = turned(o, o_ready)
        oT_ready = dve(lambda e: e.tensor_copy(oT, bank), mm)
        banks.give(i, oT_ready)
        padded = sp.take(CHUNKS * EXPERTS * 32)
        hT = split(padded.ap, CHUNKS, EXPERTS, 32)
        z = pool(lambda e: e.memset(padded.ap, 0.0), padded.before)
        i, bank, mm = turned(h, h_ready)
        for c in range(CHUNKS):
            hT_ready = dve(lambda e: e.tensor_copy(hT[:, c, :, 0:SEQS].rearrange("p e b -> p b e"), split(bank[:, c], SEQS, EXPERTS)), mm, z)
        banks.give(i, hT_ready)

        for q in range(4):
            load_bias(q)
            act_in = []
            for which, (m_name, b_name) in enumerate((("e_W1", "e_b1"), ("e_Wg", "e_bg"))):
                piece, b_ready = bias[b_name, q]
                done = []
                taken = [banks.take() for _ in range(2)]
                for n in range(2):
                    for k in range(CHUNKS):
                        for j in range(4):
                            w, w_ready = arrived[m_name, 4 * q + j]
                            mm = pe(lambda e: e.matmul(taken[n][1][32 * j:32 * j + 32], hT[:, k, 4 * q + j],
                                                       split(w, CHUNKS, HIDDEN)[:, k, n * 512:(n + 1) * 512],
                                                       start=k == 0, stop=k == 1, skip_group_check=True), taken[n][2], hT_ready, w_ready)
                for j in range(4):
                    load_next(mm)
                for n in range(2):
                    m = dve(lambda e: e.tensor_tensor(piece.ap[:, n * 512:(n + 1) * 512], taken[n][1], piece.ap[:, n * 512:(n + 1) * 512], ALU.add), mm, b_ready)
                    banks.give(taken[n][0], m)
                m = act(lambda e: e.activation(piece.ap, piece.ap, ACT.Silu), m)
                act_in.append((piece, m))
            (u, u_r), (g, g_r) = act_in
            m = dve(lambda e: e.tensor_tensor(u.ap, u.ap, g.ap, ALU.mult), u_r, g_r)
            hid = sp.take(HIDDEN)
            hidT = split(hid.ap, 8, P)
            for n in range(2):
                i, bank, free = banks.take()
                for f in range(4):
                    mm = pe(lambda e: e.transpose(bank[:, f * P:(f + 1) * P], u.ap[:, (4 * n + f) * P:(4 * n + f + 1) * P], ident), m, free)
                hm = act(lambda e: e.activation(hidT[:, 4 * n:4 * n + 4], split(bank, 4, P), ACT.Copy), mm, hid.before)
                banks.give(i, hm)
            u.give(hm)
            g.give(hm)
            i, bank, free = banks.take()
            for f in range(8):
                for j in range(4):
                    w, w_ready = arrived["e_W2", 4 * q + j]
                    mm = pe(lambda e: e.matmul(bank[32 * j:32 * j + 32, 0:256], hidT[:, f, 32 * j:32 * j + 32], split(w, 8, 256)[:, f],
                                               start=f == 0, stop=f == 7, skip_group_check=True), hm, free, w_ready)
            for j in range(4):
                load_next(mm)
            m = dve(lambda e: e.tensor_copy(tmp, bank[:, 0:256]), mm)
            banks.give(i, m)
            hid.give(mm)
            i, bank, mm = turned(tmp, m)
            for c in range(CHUNKS):
                out = split(oT[:, c], SEQS, SLOTS)[:, :, 4 * q:4 * q + 4]
                m = dve(lambda e: e.tensor_tensor(out, out, split(bank[:, c], 4, 32)[:, :, 0:SEQS].rearrange("p j b -> p b j"), ALU.add), mm, oT_ready)
            banks.give(i, m)
            oT_ready = m
        for n in range(RING):
            ring[n].give(mm, ring_dma[n].mark)
        padded.give(self.all_marks())
        for c in range(CHUNKS):
            out = split(oT[:, c], SEQS, SLOTS)
            m = dve(lambda e: e.tensor_tensor(out, out, repeated(split(S("e_b2T"), CHUNKS, SLOTS)[:, c], SEQS), ALU.add), oT_ready)
        oT_ready = m

        for n in ("c_WqT", "c_Wk", "c_Wv", "c_Wo"):
            W[n] = self.load(n, True)
        kv = sp.take(2 * 256 + 256)
        kvT = split(kv.ap[:, 0:512], 2, CHUNKS, P)
        bq_wide = split(kv.ap[:, 512:768], CHUNKS, P)
        for f in range(CHUNKS):
            bq_ready = pool(lambda e: e.tensor_copy(bq_wide[:, f], S("c_bq")[:, f:f + 1].to_broadcast([P, P])), kv.before)
        for n, (name, bias_name, scale) in enumerate((("c_Wk", "c_bk", 0.25), ("c_Wv", "c_bv", 1.0))):
            i, bank, free = banks.take()
            for f in range(CHUNKS):
                for c in range(CHUNKS):
                    mm = pe(lambda e: e.matmul(bank[:, f * P:(f + 1) * P], w2(name)[:, c, f * P:(f + 1) * P], oT[:, c], start=c == 0, stop=c == 1),
                            oT_ready, free, W[name][1])
            for f in range(CHUNKS):
                kv_ready = dve(lambda e: e.tensor_scalar(kvT[:, n, f], bank[:, f * P:(f + 1) * P], S(bias_name)[:, f:f + 1], scale, ALU.add, ALU.mult), mm, kv.before)
            banks.give(i, kv_ready)
        slots.give(self.all_marks())
        if self.blocks >= 3:
            self.load_early("r_WqT", "r_WkvT", "r_WoT", "decay_q", "decay_k")

        def tokens_attend(b):
            blocks_piece = sp.take(2 * 512)
            blk = split(blocks_piece.ap, 2, CHUNKS, H, SLOTS)
            both = sp.take(512 + 512 + 256)
            meet_b, vo = split(both.ap[:, 0:512], CHUNKS, 256), split(both.ap[:, 512:1024], 2, CH)
            shift = both.ap[:, 1024:1280]
            for n in range(2):
                for f in range(CHUNKS):
                    kb = split(kvT[:, n, f], SEQS, SLOTS)[:, b]
                    m = dve(lambda e: e.tensor_tensor(blk[:, n, f], repeated(kb, H), spread(head_of[:, f], [P, H, SLOTS]), ALU.mult),
                            kv_ready, blocks_piece.before)
            flat = blk.rearrange("p n f h s -> p n f (h s)")
            yield
            i, bank, free = banks.take()
            for c in range(CHUNKS):
                for f in range(CHUNKS):
                    mm = pe(lambda e: e.matmul(bank[:, c * 256:(c + 1) * 256], w2("c_WqT")[:, f, c * P:(c + 1) * P], flat[:, 0, f],
                                               start=f == 0, stop=f == 1), m, free, W["c_WqT"][1])
            r1 = act(lambda e: e.activation(both.ap[:, 0:512], bank, ACT.Copy), mm, both.before)
            banks.give(i, r1)
            i, bank, free = banks.take()
            for f in range(CHUNKS):
                mm = pe(lambda e: e.matmul(bank[:, 0:256], bq_wide[:, f], flat[:, 0, f], start=f == 0, stop=f == 1), m, free, bq_ready)
            r2 = act(lambda e: e.activation(shift, bank[:, 0:256], ACT.Copy), mm, both.before)
            banks.give(i, r2)
            i, bank, free = banks.take()
            for t in range(2):
                for f in range(CHUNKS):
                    mm = pe(lambda e: e.matmul(bank[:, t * 256:(t + 1) * 256], flat[:, 1, f, t * P:(t + 1) * P], w2("c_Wo")[:, f],
                                               start=f == 0, stop=f == 1), m, free, W["c_Wo"][1])
            r3 = act(lambda e: e.activation(both.ap[:, 512:1024], bank, ACT.Copy), mm, both.before)
            banks.give(i, r3)
            blocks_piece.give(mm)
            yield
            sums = []
            for pair in range(2):
                work = sp.take(512 + 96)
                s, s3 = work.ap[:, 0:512], split(work.ap[:, 0:512], 2 * H, SLOTS)
                mx, den, rden = (work.ap[:, 512 + 32 * n:544 + 32 * n] for n in range(3))
                i, bank, free = banks.take()
                for t in range(2):
                    for c in range(CHUNKS):
                        n = 2 * pair + t
                        mm = pe(lambda e: e.matmul(bank[:, t * 256:(t + 1) * 256], self.xT[:, b, c, 1 + n * P:1 + (n + 1) * P], meet_b[:, c],
                                                   start=c == 0, stop=c == 1), r1, free, self.xT_ready[b])
                m = dve(lambda e: e.tensor_tensor(split(s, 2, 256), split(bank, 2, 256), repeated(shift, 2), ALU.add), mm, r2, work.before)
                banks.give(i, m)
                yield
                m = dve(lambda e: e.tensor_reduce(mx, s3, AX.X, ALU.max), m)
                m = dve(lambda e: e.tensor_tensor(s3, s3, spread(mx, [P, 2 * H, SLOTS]), ALU.subtract), m)
                m = act(lambda e: e.activation(s, s, ACT.Exp), m)
                yield
                m = dve(lambda e: e.tensor_reduce(den, s3, AX.X, ALU.add), m)
                m = dve(lambda e: e.reciprocal(rden, den), m)
                m = pool(lambda e: e.tensor_tensor(s3, s3, spread(rden, [P, 2 * H, SLOTS]), ALU.mult), m)
                yield
                i, bank, free = banks.take()
                for n in range(4):
                    mm = pe(lambda e: e.transpose(bank[:, n * P:(n + 1) * P], s[:, n * P:(n + 1) * P], ident), m, free)
                turned_piece = sp.take(512)
                aT = split(turned_piece.ap, 2, 2, P)
                m = act(lambda e: e.activation(turned_piece.ap, bank, ACT.Copy), mm, turned_piece.before)
                banks.give(i, m)
                work.give(m)
                yield
                i, bank, free = banks.take()
                for t in range(2):
                    for n in range(2):
                        mm = pe(lambda e: e.matmul(bank[:, t * 256:(t + 1) * 256], aT[:, t, n], vo[:, n], start=n == 0, stop=n == 1), m, r3, free)
                turned_piece.give(mm)
                x = self.x_nat[:, b, 2 * pair:2 * pair + 2]
                m = dve(lambda e: e.tensor_tensor(x, x, split(bank, 2, 256), ALU.add), mm, o_bias[b])
                banks.give(i, m)
                sums += [m, m]
                yield
            both.give(m)
            yield from self.norm_and_turn(b, banks, sums)

        self.interleave([lambda b=b: tokens_attend(b) for b in range(SEQS)], 5, 2)
        marks = self.all_marks()
        kv.give(marks)
        for n in ("c_WqT", "c_Wk", "c_Wv", "c_Wo"):
            W[n][0].give(marks)


    def block3(self):
        sp, pe, act, dve, pool, S = self.space, self.pe, self.act, self.dve, self.pool, self.S
        banks = self.banks
        H, HD = 8, 32
        W = {n: self.load(n, True) for n in ("r_WqT", "r_WkvT", "r_WoT", "decay_q", "decay_k")}
        if self.blocks >= 4:
            self.load_early("rot0", "w_qkv0", "w_o0", "w_10", "w_20")
        wq, wo = split(W["r_WqT"][0].ap, CHUNKS, CH), split(W["r_WoT"][0].ap, CHUNKS, CH)
        wkv = split(W["r_WkvT"][0].ap, CHUNKS, 2 * CH)
        decay = [split(W[n][0].ap, CHUNKS, TOKENS) for n in ("decay_q", "decay_k")]
        decay_ready = [W["decay_q"][1], W["decay_k"][1]]
        decay_nat = split(S("decay_k_nat"), TILES, H)
        block_ones, causal = S("same_head32"), S("causal")

        def retain(b):
            rotated = sp.take(2 * CHUNKS * TOKENS)
            qk = split(rotated.ap, 2, CHUNKS, TOKENS)
            qk_ready = []
            for side in range(2):
                for g in range(CHUNKS):
                    w = wq if side == 0 else wkv
                    i, bank, free = banks.take()
                    for c in range(CHUNKS):
                        mm = pe(lambda e: e.matmul(bank, w[:, c, g * P:(g + 1) * P], self.xT[:, b, c, 1:], start=c == 0, stop=c == 1),
                                free, self.xT_ready[b], W["r_WqT"][1], W["r_WkvT"][1])
                    m = dve(lambda e: e.tensor_tensor(qk[:, side, g], bank, decay[side][:, g], ALU.mult), mm, decay_ready, rotated.before)
                    banks.give(i, m)
                    qk_ready.append(m)
                    yield
            nat = sp.take(2 * TILES * CH)
            kn, vn = split(nat.ap[:, 0:TILES * CH], TILES, CH), split(nat.ap[:, TILES * CH:], TILES, CH)
            nat_ready = []
            for t in range(TILES):
                i, bank, free = banks.take()
                for c in range(CHUNKS):
                    mm = pe(lambda e: e.matmul(bank, self.xT[:, b, c, 1 + t * P:1 + (t + 1) * P], wkv[:, c], start=c == 0, stop=c == 1), free)
                m = dve(lambda e: e.tensor_tensor(split(kn[:, t], H, HD), split(bank[:, 0:CH], H, HD),
                                                  spread(decay_nat[:, t], [P, H, HD]), ALU.mult), mm, nat.before)
                m2 = act(lambda e: e.activation(vn[:, t], bank[:, CH:], ACT.Copy), mm, m, nat.before)
                banks.give(i, m2)
                nat_ready += [m, m2]
                yield
            normed = sp.take(2 * TOKENS)
            yn = split(normed.ap, 2, TOKENS)
            for g in range(2):
                state = sp.take(3 * P)
                s3 = split(state.ap, 3, P)
                i, bank, free = banks.take()
                for t in range(3):
                    mm = pe(lambda e: e.matmul(bank[:, t * P:(t + 1) * P], kn[:, t, g * P:(g + 1) * P], vn[:, t, g * P:(g + 1) * P],
                                               start=True, stop=True), nat_ready, free)
                m = dve(lambda e: e.tensor_tensor(s3, split(bank[:, 0:3 * P], 3, P), repeated(block_ones, 3), ALU.mult), mm, state.before)
                banks.give(i, m)
                m = pool(lambda e: e.tensor_tensor(s3[:, 1], s3[:, 1], s3[:, 0], ALU.add), m)
                state_ready = pool(lambda e: e.tensor_tensor(s3[:, 2], s3[:, 2], s3[:, 1], ALU.add), m)
                own = sp.take(4 * TOKENS)
                a = split(own.ap, 4, TOKENS)
                own_ready = []
                four = [banks.take() for _ in range(4)]
                for t in range(TILES):
                    for j in range(4):
                        r = slice(32 * j, 32 * j + 32)
                        mm = pe(lambda e: e.matmul(four[j][1][:, t * P:(t + 1) * P], qk[r, 1, g, t * P:(t + 1) * P], qk[r, 0, g, t * P:(t + 1) * P],
                                                   start=True, stop=True), qk_ready, four[j][2])
                for j in range(4):
                    m = dve(lambda e: e.tensor_tensor(split(a[:, j], TILES, P), split(four[j][1], TILES, P), repeated(causal, TILES), ALU.mult), mm, own.before)
                    banks.give(four[j][0], m)
                    own_ready.append(m)
                yield
                i, bank, free = banks.take()
                for t in range(TILES):
                    cols = slice(t * P, (t + 1) * P)
                    if t:
                        pe(lambda e: e.matmul(bank[:, cols], s3[:, t - 1], qk[:, 0, g, cols], start=True, stop=False, skip_group_check=True),
                           state_ready, free)
                    for j in range(4):
                        mm = pe(lambda e: e.matmul(bank[32 * j:32 * j + 32, cols], vn[:, t, g * P + 32 * j:g * P + 32 * j + 32], a[:, j, cols],
                                                   start=t == 0, stop=True, skip_group_check=True), own_ready, free)
                own.give(mm)
                state.give(mm)
                stats = sp.take(24)
                st = stats.ap
                m = dve(lambda e: e.bn_stats(st[:, 0:6], bank), mm, stats.before)
                m = dve(lambda e: e.bn_aggr(st[:, 6:8], st[:, 0:6]), m)
                m = dve(lambda e: e.scalar_tensor_tensor(st[:, 7:8], st[:, 6:7], st[:, 6:7], st[:, 7:8], ALU.mult, ALU.add), m)
                yield
                i2, bank2, free2 = banks.take()
                mm2 = pe(lambda e: e.matmul(bank2[:, 0:2], block_ones, st[:, 6:8], start=True, stop=True), m, free2)
                m = dve(lambda e: e.tensor_scalar(st[:, 8:10], bank2[:, 0:2], 1.0 / HD, None, ALU.mult), mm2)
                banks.give(i2, m)
                m = dve(lambda e: e.tensor_tensor(st[:, 10:11], st[:, 8:9], st[:, 8:9], ALU.mult), m)
                m = dve(lambda e: e.tensor_tensor(st[:, 11:12], st[:, 9:10], st[:, 10:11], ALU.subtract), m)
                m = self.rsqrt(st[:, 12:13], st[:, 11:12], st[:, 13:14], 1, m)
                yield
                m = dve(lambda e: e.tensor_tensor(st[:, 14:15], st[:, 12:13], S("r_gw")[:, g:g + 1], ALU.mult), m)
                m = dve(lambda e: e.tensor_tensor(st[:, 15:16], st[:, 8:9], st[:, 14:15], ALU.mult), m)
                m = dve(lambda e: e.tensor_tensor(st[:, 16:17], S("r_gb")[:, g:g + 1], st[:, 15:16], ALU.subtract), m)
                m = dve(lambda e: e.tensor_scalar(yn[:, g], bank, st[:, 14:15], st[:, 16:17], ALU.mult, ALU.add), m, normed.before)
                banks.give(i, m)
                stats.give(m)
                yield
            nat.give(mm)
            rotated.give(mm)
            sums = []
            for pair in range(2):
                i, bank, free = banks.take()
                for t in range(2):
                    n = 2 * pair + t
                    for g in range(2):
                        mm = pe(lambda e: e.matmul(bank[:, t * CH:(t + 1) * CH], yn[:, g, n * P:(n + 1) * P], wo[:, g], start=g == 0, stop=g == 1),
                                m, free, W["r_WoT"][1])
                x = self.x_nat[:, b, 2 * pair:2 * pair + 2]
                s = dve(lambda e: e.tensor_tensor(x, x, split(bank, 2, CH), ALU.add), mm, self.x_ready[b])
                banks.give(i, s)
                sums += [s, s]
                yield
            normed.give(mm)
            yield from self.norm_and_turn(b, banks, sums)

        self.interleave([lambda b=b: retain(b) for b in range(SEQS)], 4, 6)
        for n in W:
            W[n][0].give(self.all_marks())


    def turn(self, b, banks, m):
        copied = []
        for c in range(CHUNKS):
            i, bank, free = banks.take()
            for t in range(TILES):
                put = self.pe(lambda e: e.transpose(bank[:, t * P:(t + 1) * P], self.x_nat[:, b, t, c * P:(c + 1) * P], self.S("identity")), m, free)
            out = self.xT[:, b, c, 1:]
            if c:
                copied.append(self.act(lambda e: e.activation(out, bank, ACT.Copy), put, self.xT_read[b]))
            else:
                copied.append(self.dve(lambda e: e.tensor_copy(out, bank), put, self.xT_read[b]))
            banks.give(i, copied[-1])
            yield
        self.xT_ready[b] = copied
        self.xT_read[b] = []

    def block4(self):
        sp, pe, act, dve, pool, S = self.space, self.pe, self.act, self.dve, self.pool, self.S
        banks = self.banks
        LAYERS, H, HD, HID_TILES = 2, 8, 64, 6
        PAIRS = H // 2
        ident = S("identity")
        xT = self.xT
        self.pieces["small"].give(self.all_marks())
        late, late_ready = self.load("late")
        self.pieces["late"] = late
        kept_x = self.nc.dram_tensor("kept_x", (SEQS, P, TILES * CH), F32).ap()
        kept_dma = [Transfers(self.sem(f"kept{b}")) for b in range(SEQS)]
        for b in range(SEQS):
            kept_dma[b].start(self.sp, kept_x[b], self.x_nat[:, b].rearrange("p t c -> p (t c)"), self.x_ready[b])
            self.x_ready[b] = [self.x_ready[b], kept_dma[b].mark]

        q_pads = []
        for _ in range(self.TILE_LANES):
            piece = sp.take(PAIRS * 2 * P)
            q_pads.append((split(piece.ap, PAIRS, 2, P), pool(lambda e: e.memset(piece.ap, 0.0), piece.before)))

        W = {}

        def load_attention(l):
            rot, arrived = self.load(f"rot{l}", True)
            cos, sin, s_qk, s_kq = (rot.ap[:, a:b] for a, b in ((0, 512), (512, 1024), (1024, 1152), (1152, 1280)))
            m1 = pool(lambda e: e.tensor_tensor(split(cos, TILES, 2 * HD), split(cos, TILES, 2 * HD), repeated(s_qk, TILES), ALU.mult), arrived)
            m2 = pool(lambda e: e.tensor_tensor(split(sin, TILES, 2 * HD), split(sin, TILES, 2 * HD), repeated(s_kq, TILES), ALU.mult), arrived)
            W["rot"] = (rot, [m1, m2])
            W["w_qkv"], W["w_o"] = self.load(f"w_qkv{l}", True), self.load(f"w_o{l}", True)

        def load_mlp(l):
            W["w_1"], W["w_2"] = self.load(f"w_1{l}", True), self.load(f"w_2{l}", True)

        mlp_done, attended = [0] * SEQS, set()
        state = {}

        def tile(l, b, t):
            while mlp_done[b] < l or (t and len(state[l, b]["kept"]) < t):
                yield
            if t == 0:
                if b == 0:
                    load_attention(l)
                state[l, b] = {"kept": [], "k": [], "v": [], "sums": [], "x": self.x_ready[b], "xT": self.xT_ready[b]}
            my = state[l, b]
            kept = sp.take(2 * H * HD)
            my["kept"].append({"piece": kept, "kT": split(kept.ap[:, 0:512], PAIRS, P), "vn": kept.ap[:, 512:], "readers": 2 if t < TILES - 1 else 1})
            kT, vn = my["kept"][t]["kT"], my["kept"][t]["vn"]
            wqkv, wo = split(W["w_qkv"][0].ap, CHUNKS, 3, H * HD), split(W["w_o"][0].ap, PAIRS, CH)
            wqkv_ready, wo_ready, rot_ready = W["w_qkv"][1], W["w_o"][1], W["rot"][1]
            last_use = [W[n][0] for n in ("w_qkv", "w_o", "rot")] if b == SEQS - 1 and t == TILES - 1 else []
            cos, sin = (split(W["rot"][0].ap[:, a:a + 512], TILES, 2, HD) for a in (0, 512))

            def project(side):
                i, bank, free = banks.take()
                for c in range(CHUNKS):
                    at = 1 - c + t * P
                    mm = pe(lambda e: e.matmul(bank, xT[:, b, c, at:at + P], wqkv[:, c, side], start=c == 0, stop=c == 1),
                            free, my["xT"], wqkv_ready)
                return i, bank, mm

            work = sp.take(2 * 1024 + 32)
            a1, a2 = split(work.ap[:, 0:1024], 2, H, HD), split(work.ap[:, 1024:2048], 2, H, HD)
            ss, rn = work.ap[:, 2048:2064], work.ap[:, 2064:2080]
            projected = [project(0), project(1)]
            got = []
            for side in range(2):
                i, bank, mm = projected[side]
                b3 = split(bank, H, HD)
                m = act(lambda e: e.activation(a2[:, side], b3, ACT.Square), mm, work.before)
                squared = dve(lambda e: e.tensor_reduce(split(ss, 2, H)[:, side], a2[:, side], AX.X, ALU.add), m)
                m = dve(lambda e: e.tensor_tensor(a1[:, side], b3, repeated(cos[:, t, side], H), ALU.mult), mm, rot_ready, work.before)
                for half in range(2):
                    lo, hi = slice(32 * half, 32 * half + 32), slice(32 - 32 * half, 64 - 32 * half)
                    m = dve(lambda e: e.tensor_tensor(a2[:, side, :, lo], b3[:, :, hi], repeated(sin[:, t, side, lo], H), ALU.mult), squared)
                banks.give(i, m)
                if side == 0:
                    got.append(pool(lambda e: e.tensor_tensor(a1[:, 0], a1[:, 0], a2[:, 0], ALU.add), m))
                    yield
            m2 = pool(lambda e: e.tensor_scalar(ss, ss, 1e-24, None, ALU.max), squared)
            m2 = pool(lambda e: e.tensor_tensor(rn, ss, self.half.ap[:, 0:16], ALU.pow), m2)
            i, bank, mm = project(2)
            my["v"].append(act(lambda e: e.activation(vn, bank, ACT.Copy), mm, kept.before))
            banks.give(i, my["v"][t])
            m = dve(lambda e: e.tensor_tensor(a1[:, 1], a1[:, 1], a2[:, 1], ALU.add), m)
            turned = dve(lambda e: e.tensor_tensor(split(work.ap[:, 0:1024], 16, HD), split(work.ap[:, 0:1024], 16, HD), spread(rn, [P, 16, HD]), ALU.mult), got, m, m2)
            yield
            yield
            q_pad, q_free = q_pads.pop(0)
            q_ready = []
            for side in range(2):
                i, bank, free = banks.take()
                for pair in range(PAIRS):
                    mm = pe(lambda e: e.transpose(bank[:, pair * P:(pair + 1) * P], work.ap[:, side * 512 + pair * P:side * 512 + (pair + 1) * P], ident), turned, free)
                b3 = split(bank, PAIRS, P)
                if side == 0:
                    q_ready.append(act(lambda e: e.activation(q_pad[0:64, :, 0], b3[0:64], ACT.Copy), mm, q_free))
                    q_ready.append(act(lambda e: e.activation(q_pad[64:P, :, 1], b3[64:P], ACT.Copy), mm))
                    banks.give(i, q_ready[1])
                else:
                    my["k"].append(dve(lambda e: e.tensor_copy(kT, b3), mm, kept.before))
                    banks.give(i, my["k"][t])
            work.give(mm)
            yield
            windows = range(0 if t else 1, 2)
            n_keys = P * len(windows)
            probs = sp.take(H * 2 * P + 32)
            pr = split(probs.ap[:, 0:H * 2 * P], H, 2 * P)
            mx, den, rden = (probs.ap[:, H * 2 * P + 8 * n:H * 2 * P + 8 * n + 8] for n in range(3))
            for h in range(H):
                i, bank, free = banks.take()
                for n in windows:
                    at = (n - windows[0]) * P
                    mm = pe(lambda e: e.matmul(bank[:, at:at + P], q_pad[:, h // 2, h % 2], my["kept"][t - 1 + n]["kT"][:, h // 2], start=True, stop=True),
                            q_ready, my["k"][t], free)
                m = dve(lambda e: e.tensor_tensor_reduce(out=pr[:, h, 2 * P - n_keys:], in0=bank[:, 0:n_keys], in1=S("window_mask")[:, 2 * P - n_keys:],
                                                         scale=1.0, scalar=-3.4e38, op0=ALU.add, op1=ALU.max, accum_out=mx[:, h:h + 1]),
                        mm, probs.before, late_ready)
                banks.give(i, m)
                if h == 3:
                    yield
            q_pads.append((q_pad, mm))
            m = dve(lambda e: e.tensor_scalar(mx, mx, -1.0, None, ALU.mult), m)
            yield
            normal = []
            for h in range(H):
                cols = pr[:, h, 2 * P - n_keys:]
                m2 = act(lambda e: e.activation(cols, cols, ACT.Exp, bias=mx[:, h:h + 1], accum_out=den[:, h:h + 1]), m)
                if h % 4 == 3:
                    q4 = slice(h - 3, h + 1)
                    m3 = dve(lambda e: e.reciprocal(rden[:, q4], den[:, q4]), m2)
                    for hh in range(h - 3, h + 1):
                        c2 = pr[:, hh, 2 * P - n_keys:]
                        normal.append(dve(lambda e: e.tensor_scalar(c2, c2, rden[:, hh:hh + 1], None, ALU.mult), m3))
            yield
            yield
            io, obank, ofree = banks.take()
            for pairs in (0, 1), (2, 3):
                turned = []
                for pair in pairs:
                    i, bank, free = banks.take()
                    b4 = split(bank, 2, 2, P)
                    for hh in range(2):
                        for n in windows:
                            mm = pe(lambda e: e.transpose(b4[:, hh, n], pr[:, 2 * pair + hh, n * P:(n + 1) * P], ident), normal[2 * pair + hh], free)
                    piece = sp.take(512)
                    pT = split(piece.ap, 2, 2, P)
                    src, dst = (b4, pT) if t else (b4[:, :, 1], pT[:, :, 1])
                    if pair % 2:
                        m = act(lambda e: e.activation(dst, src, ACT.Copy), mm, piece.before)
                    else:
                        m = dve(lambda e: e.tensor_copy(dst, src), mm, piece.before)
                    banks.give(i, m)
                    turned.append((pair, piece, pT, m))
                if pairs[1] == 3:
                    probs.give(mm)
                yield
                for pair, piece, pT, m in turned:
                    for n in windows:
                        for hh in range(2):
                            h = 2 * pair + hh
                            mm = pe(lambda e: e.matmul(obank[64 * hh:64 * hh + 64, pair * P:(pair + 1) * P], my["kept"][t - 1 + n]["vn"][:, h * HD:(h + 1) * HD], pT[:, hh, n],
                                                       start=n == windows[0], stop=n == 1, skip_group_check=True), m, ofree, my["v"])
                    piece.give(mm)
            for n in windows:
                read = my["kept"][t - 1 + n]
                read["readers"] -= 1
                if not read["readers"]:
                    read["piece"].give(mm)
            o_piece = sp.take(512)
            m = act(lambda e: e.activation(o_piece.ap, obank, ACT.Copy), mm, o_piece.before)
            banks.give(io, m)
            yield
            i, bank, free = banks.take()
            for pair in range(PAIRS):
                mm = pe(lambda e: e.matmul(bank[:, 0:CH], o_piece.ap[:, pair * P:(pair + 1) * P], wo[:, pair], start=pair == 0, stop=pair == 3), m, free, wo_ready)
            o_piece.give(mm)
            x = self.x_nat[:, b, t]
            s = dve(lambda e: e.tensor_tensor(x, x, bank[:, 0:CH], ALU.add), mm, my["x"])
            banks.give(i, s)
            my["sums"].append(s)
            if t == TILES - 1:
                self.x_ready[b] = my["sums"]
                attended.add((l, b))
            for piece in last_use:
                piece.give(mm, self.dve_mark())

        def mlp(l, b):
            while (l, b) not in attended:
                yield
            if b == 0:
                load_mlp(l)
            w1, w2 = split(W["w_1"][0].ap, CHUNKS, 2, HID_TILES, P), split(W["w_2"][0].ap, HID_TILES, CH)
            w1_ready, w2_ready = W["w_1"][1], W["w_2"][1]
            last_use = [W[n][0] for n in ("w_1", "w_2")] if b == SEQS - 1 else []
            b1 = split(S(f"b_1{l}"), 2, HID_TILES)
            yield from self.turn(b, banks, self.x_ready[b])
            piece = sp.take(TILES * CH + 64)
            hn = split(piece.ap[:, 0:TILES * CH], TILES, CH)
            st = piece.ap[:, TILES * CH:]
            stats, mv, rstd, scratch = split(st[:, 0:48], TILES, 2, 6), split(st[:, 48:56], TILES, 2), st[:, 56:60], st[:, 60:64]
            i, bank, free = banks.take()
            shifted = split(bank, TILES, P)
            for t in range(TILES):
                mm = pe(lambda e: e.transpose(shifted[:, t], xT[:, b, 1, t * P:(t + 1) * P], ident), self.xT_ready[b], free)
            for t in range(TILES):
                m1 = dve(lambda e: e.bn_stats(stats[:, t, 0], self.x_nat[:, b, t, 0:P]), self.x_ready[b], piece.before)
                m2 = dve(lambda e: e.bn_stats(stats[:, t, 1], shifted[:, t]), mm, piece.before)
                m = dve(lambda e: e.bn_aggr(mv[:, t], stats[:, t].rearrange("p a b -> p (a b)")), m1, m2)
            yield
            m = self.rsqrt(rstd, mv[:, :, 1], scratch, TILES, m)
            yield
            done = []
            for t in range(TILES):
                m1 = dve(lambda e: e.tensor_scalar(hn[:, t, 0:P], self.x_nat[:, b, t, 0:P], mv[:, t, 0:1], rstd[:, t:t + 1], ALU.subtract, ALU.mult), m)
                m2 = dve(lambda e: e.tensor_scalar(hn[:, t, P:], shifted[:, t], mv[:, t, 0:1], rstd[:, t:t + 1], ALU.subtract, ALU.mult), m)
                done.append(m2)
            banks.give(i, m2)
            yield
            yield
            turned = sp.take(CHUNKS * TOKENS)
            hT = split(turned.ap, CHUNKS, TOKENS)
            h_ready = []
            for c in range(CHUNKS):
                i, bank, free = banks.take()
                for t in range(TILES):
                    mm = pe(lambda e: e.transpose(bank[:, t * P:(t + 1) * P], hn[:, t, c * P:(c + 1) * P], ident), done, free)
                g, bb = S(f"l_g{l}")[:, c:c + 1], S(f"l_b{l}")[:, c:c + 1]
                if c:
                    h_ready.append(act(lambda e: e.activation(hT[:, c], bank, ACT.Identity, bias=bb, scale=g), mm, turned.before, late_ready))
                else:
                    h_ready.append(dve(lambda e: e.tensor_scalar(hT[:, c], bank, g, bb, ALU.mult, ALU.add), mm, turned.before))
                banks.give(i, h_ready[-1])
            piece.give(mm)
            yield
            hidden = []
            TOGETHER = 3
            for first in range(0, HID_TILES, TOGETHER):
                gates = []
                for n in range(first, first + TOGETHER):
                    ig, gate, gfree = banks.take()
                    for c in range(CHUNKS):
                        mm = pe(lambda e: e.matmul(gate, w1[:, c, 1, n], hT[:, c], start=c == 0, stop=c == 1), h_ready, gfree, w1_ready)
                    gates.append((n, ig, gate, mm))
                    if n < TILES:
                        biased = pool(lambda e: e.tensor_tensor(self.x_nat[:, b, n], self.x_nat[:, b, n], S(f"b_2{l}"), ALU.add), done, late_ready)
                    if n < first + TOGETHER - 1:
                        yield
                for n, ig, gate, mm in gates:
                    out = sp.take(TOKENS)
                    m = act(lambda e: e.activation(out.ap, gate, ACT.Gelu, bias=b1[:, 1, n:n + 1]), mm, out.before)
                    banks.give(ig, m)
                    hidden.append((out, m))
                for n in range(first, first + TOGETHER):
                    out, m = hidden[n]
                    ia, lin, afree = banks.take()
                    for c in range(CHUNKS):
                        mm = pe(lambda e: e.matmul(lin, w1[:, c, 0, n], hT[:, c], start=c == 0, stop=c == 1), afree)
                    m = dve(lambda e: e.scalar_tensor_tensor(out.ap, lin, b1[:, 0, n:n + 1], out.ap, ALU.add, ALU.mult), mm, m)
                    banks.give(ia, m)
                    hidden[n] = out, m
                    yield
            turned.give(mm)
            sums = []
            for pair in range(2):
                i, bank, free = banks.take()
                for t in range(2):
                    n = 2 * pair + t
                    for k in range(HID_TILES):
                        mm = pe(lambda e: e.matmul(bank[:, t * CH:(t + 1) * CH], hidden[k][0].ap[:, n * P:(n + 1) * P], w2[:, k],
                                                   start=k == 0, stop=k == HID_TILES - 1), hidden[k][1], free, w2_ready)
                x = self.x_nat[:, b, 2 * pair:2 * pair + 2]
                s = dve(lambda e: e.tensor_tensor(x, x, split(bank, 2, CH), ALU.add), mm, biased)
                banks.give(i, s)
                sums += [s, s]
                yield
            for out, _ in hidden:
                out.give(mm)
            for w_piece in last_use:
                w_piece.give(mm)
            self.x_ready[b] = sums
            if l == LAYERS - 1:
                again = sp.take(TILES * CH)
                kept_dma[b].start(self.sp, again.ap, kept_x[b], again.before)
                sums = [dve(lambda e: e.tensor_tensor(self.x_nat[:, b], self.x_nat[:, b], split(again.ap, TILES, CH), ALU.add),
                            sums, kept_dma[b].mark)] * TILES
                again.give(sums[0])
                yield from self.norm_and_turn(b, banks, sums, turn=False)
            else:
                yield from self.turn(b, banks, sums)
            mlp_done[b] = l + 1

        order = [(l, b) for l in range(LAYERS) for b in range(SEQS)]
        tiles = iter([tile(l, b, t) for l, b in order for t in range(TILES)])
        mlps = iter([mlp(l, b) for l, b in order])
        self.weave([(tiles, self.TILE_LANES, self.TILE_OFFSET, 1), (mlps, 2, 0, 2)])
def _chunked(w):
    K, N = w.shape
    return w.reshape(K // 128, 128, N).transpose(1, 0, 2).reshape(128, -1)


def _padded(w, shape):
    import numpy as np
    out = np.zeros(shape, w.dtype)
    out[tuple(slice(0, n) for n in w.shape)] = w
    return out


def _constants():
    import numpy as np
    f4 = np.float32
    p = np.arange(128)
    out = {}
    out["identity"] = np.eye(128, dtype=f4)
    out["same_head32"] = (p[:, None] // 32 == p[None, :] // 32).astype(f4)
    out["causal"] = (p[:, None] <= p[None, :]).astype(f4)
    out["ones5"] = _padded(np.ones((5, 1), f4), (32, 1)).repeat(1, 1)
    out["ones5"] = np.concatenate([np.zeros((96, 1), f4), out["ones5"]])
    out["head_of"] = np.stack([((c * 128 + p)[:, None] // 16 == np.arange(16)[None, :]) for c in (0, 1)], 1).astype(f4).reshape(128, 32)
    out["spread16"] = _padded(np.stack([np.eye(128, dtype=f4)[32 * j:32 * j + 16] for j in range(4)], 1).reshape(16, 512), (128, 512))
    g = (1.0 - np.exp(np.linspace(np.log(1.0 / 32.0), np.log(1.0 / 512.0), 8))).astype(f4).astype(np.float64)
    t = np.arange(512)
    rows = np.stack([g[(c * 128 + p) // 32] for c in (0, 1)], 1)
    out["decay_q"] = (rows[:, :, None] ** (t - 256)[None, None, :]).astype(f4).reshape(128, -1)
    out["decay_k"] = (rows[:, :, None] ** (256 - t)[None, None, :]).astype(f4).reshape(128, -1)
    tn = np.arange(4)[None, :] * 128 + p[:, None]
    out["decay_k_nat"] = (g[None, None, :] ** (256 - tn)[:, :, None]).astype(f4).reshape(128, -1)
    half = np.arange(0, 64, 2, dtype=f4)
    inv = (f4(1.0) / f4(10000.0) ** (half / f4(64))).astype(f4)
    tt = np.arange(512, dtype=f4)
    fr = (tt[:, None] * inv[None, :]).astype(f4)
    fr = np.concatenate([fr, fr], -1)
    base = ((half + f4(0.4 * 64)) / f4(1.4 * 64)).astype(f4)
    power = ((tt - f4(256)) / f4(64.0)).astype(f4)
    sc = (base[None, :] ** power[:, None]).astype(f4)
    sc = np.concatenate([sc, sc], -1)
    cos, sin = np.cos(fr), np.sin(fr)
    sin = sin * np.where(np.arange(64) < 32, -1, 1).astype(f4)
    tab = lambda a: np.stack([a * sc * f4(8.0), a / sc], 1).reshape(4, 128, 2, 64).transpose(1, 0, 2, 3).reshape(128, -1).astype(f4)
    out["rot_cos"], out["rot_sin"] = tab(cos), tab(sin)
    i, j = p[:, None], p[None, :]
    big = f4(-3.0e38)
    out["window_mask"] = np.concatenate([np.where(i > j, big, f4(0)), np.where(i < j, big, f4(0))], 1).astype(f4)
    return out


def _layouts(inp):
    import numpy as np
    I = {k: np.asarray(v) for k, v in inp.items()}
    A = {k[8:]: v for k, v in I.items() if k.startswith("L0_attn_")}
    D = {k[7:]: v for k, v in I.items() if k.startswith("L0_ffn_")}
    R = {k[8:]: v for k, v in I.items() if k.startswith("L1_attn_")}
    L = {k[7:]: v for k, v in I.items() if k.startswith("L1_ffn_")}
    p = np.arange(128)
    bc = lambda v: np.broadcast_to(v.reshape(1, -1), (128, v.size))
    col2 = lambda v: v.reshape(2, 128).T
    rows = lambda a: _padded(a, (128,) + a.shape[1:]).reshape(128, -1)
    big, small = {}, {}

    big["x"] = A["x"]
    big["xT"] = A["x"].reshape(8, 512, 2, 128).transpose(3, 0, 2, 1).reshape(128, -1)
    W = A["Wqkv"]
    by_feature = W[:, 0:512].reshape(256, 2, 2, 8, 16).transpose(0, 1, 2, 4, 3).reshape(256, 512)
    big["a_wqkv"] = _chunked(np.concatenate([by_feature, W[:, 512:]], 1))
    big["a_wqk"] = _chunked(W[:, 0:512].reshape(256, 2, 16, 16).transpose(0, 2, 1, 3).reshape(256, 512))
    big["a_wproj"] = _padded(A["Wproj"].reshape(4, 4, 16, 256), (4, 4, 32, 256)).transpose(1, 2, 0, 3).reshape(128, -1)
    small["a_alpha"] = np.stack([A["alpha"][8 * c + p % 8] for c in (0, 1)], 1)
    small["a_beta"] = bc(A["beta"])
    small["a_gamma"] = np.stack([A["gamma"][4 * g + p // 32] for g in range(4)], 1)
    small["a_bproj"] = bc(A["bproj"])
    bd = lambda w, r: _padded(np.stack([_padded(w[t], (r, w.shape[2])) for t in range(4)]), (4, r, w.shape[2]))
    def block_diag(w, r, c):
        out = np.zeros((4 * r, 4 * c), w.dtype)
        for t in range(4):
            out[r * t:r * t + w.shape[1], c * t:c * t + w.shape[2]] = w[t]
        return out
    small["a_A"] = rows(A["A"].transpose(1, 0, 2).reshape(32, 128))
    small["a_phi1"] = rows(_padded(A["Wphi1"].transpose(1, 0, 2), (32, 4, 32)).reshape(32, 128))
    small["a_bphi1"] = _padded(A["bphi1"], (4, 32)).reshape(128, 1)
    small["a_phi2"] = block_diag(A["Wphi2"], 32, 4)
    small["a_bphi2"] = rows(A["bphi2"].reshape(16, 1))
    small["a_psi1"] = block_diag(A["Wpsi1"], 32, 32)
    small["a_bpsi1"] = A["bpsi1"].reshape(128, 1)
    small["a_lng"] = A["ln_g"].reshape(128, 1)
    small["a_lnb"] = A["ln_b"].reshape(128, 1)
    small["a_psi2"] = block_diag(A["Wpsi2"], 32, 4)
    small["a_bpsi2"] = rows(A["bpsi2"].reshape(16, 1))
    small["a_mix"] = rows(np.repeat(A["mixing"], 4).reshape(16, 1))
    small["a_temp"] = rows(np.broadcast_to(A["temp_scale"], (16, 1)))

    for n in ("d_Wq", "d_Wv", "d_Wo", "c_Wk", "c_Wv", "c_Wo"):
        big[n] = _chunked(D[n])
    big["d_WkT"] = _chunked(D["d_Wk"].T)
    big["c_WqT"] = _chunked(D["c_Wq"].T)
    for n in ("d_bq", "d_bk", "c_bq", "c_bk", "c_bv"):
        small[n] = col2(D[n])
    for n in ("d_bv", "d_bo", "c_bo"):
        small[n] = bc(D[n])
    small["slot"] = np.tile(D["slot_query"][0], (8, 1))
    small["slotT"] = _chunked(D["slot_query"][0].T)
    small["e_lng"] = np.tile(D["e_ln_g"], (8, 1))
    small["e_lnb"] = np.tile(D["e_ln_b"], (8, 1))
    big["e_b1"] = np.repeat(D["e_b1"].reshape(4, 4, 1, 1024), 32, 2).reshape(4, 128, 1024)
    big["e_bg"] = np.repeat(D["e_bg"].reshape(4, 4, 1, 1024), 32, 2).reshape(4, 128, 1024)
    small["e_b2T"] = _chunked(D["e_b2"].T)
    for n in ("e_W1", "e_Wg", "e_W2"):
        big[n] = np.stack([_chunked(w) for w in D[n]])

    big["r_WqT"], big["r_WoT"] = _chunked(R["Wq"].T), _chunked(R["Wo"].T)
    big["r_WkvT"] = _chunked(np.concatenate([R["Wk"].T, R["Wv"].T], 1))
    small["r_gw"] = col2(R["gn_weight"])
    small["r_gb"] = col2(R["gn_bias"])

    scales = {}
    for l in range(2):
        big[f"w_qkv{l}"] = _chunked(L["wqkv"][l])
        big[f"w_o{l}"] = _chunked(L["wo"][l])
        w1 = L["w1"][l].reshape(256, 2, 682)
        big[f"w_1{l}"] = _chunked(_padded(w1, (256, 2, 768)).reshape(256, 1536))
        small[f"b_1{l}"] = _padded(L["b1"][l].reshape(2, 682), (2, 768)).reshape(12, 128).T
        big[f"w_2{l}"] = _chunked(_padded(L["w2"][l], (768, 256)))
        small[f"b_2{l}"] = bc(L["b2"][l])
        small[f"l_g{l}"] = col2(L["ln_g"][l])
        small[f"l_b{l}"] = col2(L["ln_b"][l])
        qk = np.stack([L["q_scale"][l], L["k_scale"][l]])
        scales[l] = [bc(qk), bc(np.concatenate([qk[:, 32:], qk[:, :32]], 1))]
    constants = _constants()
    rotary = [constants.pop(n) for n in ("rot_cos", "rot_sin")]
    for l in range(2):
        big[f"rot{l}"] = np.concatenate(rotary + scales[l], 1)
    for n, a in constants.items():
        (big if n in ("decay_q", "decay_k") else small)[n] = a
    at, groups = {}, {}
    for n, a in small.items():
        a = np.ascontiguousarray(a, np.float32).reshape(128, -1)
        group = "keep" if n == "identity" else "late" if n[:4] in ("b_10", "b_11", "b_20", "b_21", "l_g0", "l_g1", "l_b0", "l_b1", "wind") else "small"
        parts = groups.setdefault(group, [])
        at[n] = (group, sum(q.shape[1] for q in parts), a.shape[1])
        parts.append(a)
    for group, parts in groups.items():
        big[group] = np.concatenate(parts, 1)
    return {n: np.ascontiguousarray(a, np.float32) for n, a in big.items()}, at


def kernel(**inputs):
    import concourse.bacc as bacc
    from concourse.bass_utils import run_bass_kernel_spmd

    arrays, small_at = _layouts(inputs)
    nc = bacc.Bacc("TRN2", target_bir_lowering=False, num_devices=1)
    dram = {n: nc.dram_tensor(f"in_{n}", a.shape, mybir.dt.float32, kind="ExternalInput").ap() for n, a in arrays.items()}
    out = nc.dram_tensor("out_x", (8, 512, 256), mybir.dt.float32, kind="ExternalOutput").ap()
    Program(nc, dram, small_at, out).build()
    r = run_bass_kernel_spmd(nc, [{f"in_{n}": a for n, a in arrays.items()}], core_ids=[0])
    return r.results[0]["out_x"]
```
